# Optimizing a Trainium2 kernel written in Bass

```python
import numpy as np
import jax
import jax.numpy as jnp

def _softmax(x, axis=-1):
    return jax.nn.softmax(x, axis=axis)

def _gelu(x):
    return jax.nn.gelu(x, approximate=True)

def _silu(x):
    return jax.nn.silu(x)

def _sigmoid(x):
    return jax.nn.sigmoid(x)

def _layernorm(x, axis=-1, eps=1e-05):
    m = jnp.mean(x, axis=axis, keepdims=True)
    v = jnp.var(x, axis=axis, keepdims=True)
    return (x - m) / jnp.sqrt(v + eps)

def _scatter_add(tgt, idx, src, axis=0):
    return tgt.at[idx].add(src)

def _segment_sum(src, seg, n):
    return jax.ops.segment_sum(src, seg, n)
kernel_name = 'mk_hybrid_d1_jaxref_r8_dc054c'

def setup_inputs(seed: int=0):
    np.random.seed(seed)
    _w = jnp.asarray

    def _L0_attn_a_setup():
        import jax, jax.numpy as jnp
        import numpy as np
        D_MODEL = 128
        N_HEADS = 16
        D_HEAD = D_MODEL // N_HEADS
        SCALE = 1.0 / np.sqrt(D_HEAD)
        key = jax.random.key(seed)
        ks = jax.random.split(key, 5)
        B, S = (2, 256)
        x = jax.random.normal(ks[0], (B, S, D_MODEL), dtype=jnp.float32)
        bound = 1.0 / np.sqrt(D_MODEL)
        Wq = jax.random.uniform(ks[1], (D_MODEL, D_MODEL), jnp.float32, -bound, bound)
        Wk = jax.random.uniform(ks[2], (D_MODEL, D_MODEL), jnp.float32, -bound, bound)
        Wv = jax.random.uniform(ks[3], (D_MODEL, D_MODEL), jnp.float32, -bound, bound)
        Wo = jax.random.uniform(ks[4], (D_MODEL, D_MODEL), jnp.float32, -bound, bound)
        return {'x': x, 'Wq': Wq, 'Wk': Wk, 'Wv': Wv, 'Wo': Wo}
    _L0_attn_a_in = _L0_attn_a_setup()

    def _L0_attn_b_setup():
        import jax, jax.numpy as jnp
        import numpy as np
        B, L, E, H = (1, 512, 128, 16)
        D = E // H
        EPS = 1e-06
        key = jax.random.key(seed)
        k1, k2, k3 = jax.random.split(key, 3)
        x = jax.random.normal(k1, (B, L, E), dtype=jnp.float32)
        qkv_w = jax.random.normal(k2, (E, 3 * E), dtype=jnp.float32) / np.sqrt(E)
        qkv_b = jnp.zeros((3 * E,), dtype=jnp.float32)
        out_w = jax.random.normal(k3, (E, E), dtype=jnp.float32) / np.sqrt(E)
        out_b = jnp.zeros((E,), dtype=jnp.float32)
        return {'x': x, 'qkv_w': qkv_w, 'qkv_b': qkv_b, 'out_w': out_w, 'out_b': out_b}
    _L0_attn_b_in = _L0_attn_b_setup()

    def _L0_ffn_setup():
        import jax, jax.numpy as jnp
        import numpy as np
        DIM, HEADS, FFN, E = (128, 16, 512, 8)
        B, S = (2, 128)
        EPS = 1e-05

        def _ln(x, g, b):
            mu = jnp.mean(x, axis=-1, keepdims=True)
            var = jnp.mean((x - mu) ** 2, axis=-1, keepdims=True)
            return (x - mu) * jax.lax.rsqrt(var + EPS) * g + b
        key = jax.random.key(seed)
        ks = jax.random.split(key, 20)
        sd = 0.02
        d, f = (DIM, FFN)
        return {'x': jax.random.normal(ks[0], (B, S, d), jnp.float32), 'ln1_g': jnp.ones((d,), jnp.float32), 'ln1_b': jnp.zeros((d,), jnp.float32), 'Wqkv': jax.random.normal(ks[1], (d, 3 * d), jnp.float32) * sd, 'bqkv': jnp.zeros((3 * d,), jnp.float32), 'Wo': jax.random.normal(ks[2], (d, d), jnp.float32) * sd, 'bo': jnp.zeros((d,), jnp.float32), 'ln2_g': jnp.ones((d,), jnp.float32), 'ln2_b': jnp.zeros((d,), jnp.float32), 'gate_w': jax.random.normal(ks[3], (d, E), jnp.float32) * sd, 'W1': jax.random.normal(ks[4], (E, d, f), jnp.float32) * sd, 'b1': jnp.zeros((E, f), jnp.float32), 'W2': jax.random.normal(ks[5], (E, f, d), jnp.float32) * sd, 'b2': jnp.zeros((E, d), jnp.float32), 'rW1': jax.random.normal(ks[6], (d, f), jnp.float32) * sd, 'rb1': jnp.zeros((f,), jnp.float32), 'rW2': jax.random.normal(ks[7], (f, d), jnp.float32) * sd, 'rb2': jnp.zeros((d,), jnp.float32), 'coef_w': jax.random.normal(ks[8], (d, 2), jnp.float32) * sd, 'coef_b': jnp.zeros((2,), jnp.float32)}
    _L0_ffn_in = _L0_ffn_setup()
    _d = {'L0_attn_a_x': _L0_attn_a_in['x'], 'L0_attn_a_Wq': _L0_attn_a_in['Wq'], 'L0_attn_a_Wk': _L0_attn_a_in['Wk'], 'L0_attn_a_Wv': _L0_attn_a_in['Wv'], 'L0_attn_a_Wo': _L0_attn_a_in['Wo'], 'L0_attn_b_qkv_w': _L0_attn_b_in['qkv_w'], 'L0_attn_b_qkv_b': _L0_attn_b_in['qkv_b'], 'L0_attn_b_out_w': _L0_attn_b_in['out_w'], 'L0_attn_b_out_b': _L0_attn_b_in['out_b'], 'L0_ffn_ln1_g': _L0_ffn_in['ln1_g'], 'L0_ffn_ln1_b': _L0_ffn_in['ln1_b'], 'L0_ffn_Wqkv': _L0_ffn_in['Wqkv'], 'L0_ffn_bqkv': _L0_ffn_in['bqkv'], 'L0_ffn_Wo': _L0_ffn_in['Wo'], 'L0_ffn_bo': _L0_ffn_in['bo'], 'L0_ffn_ln2_g': _L0_ffn_in['ln2_g'], 'L0_ffn_ln2_b': _L0_ffn_in['ln2_b'], 'L0_ffn_gate_w': _L0_ffn_in['gate_w'], 'L0_ffn_W1': _L0_ffn_in['W1'], 'L0_ffn_b1': _L0_ffn_in['b1'], 'L0_ffn_W2': _L0_ffn_in['W2'], 'L0_ffn_b2': _L0_ffn_in['b2'], 'L0_ffn_rW1': _L0_ffn_in['rW1'], 'L0_ffn_rb1': _L0_ffn_in['rb1'], 'L0_ffn_rW2': _L0_ffn_in['rW2'], 'L0_ffn_rb2': _L0_ffn_in['rb2'], 'L0_ffn_coef_w': _L0_ffn_in['coef_w'], 'L0_ffn_coef_b': _L0_ffn_in['coef_b']}
    _x0 = _d['L0_attn_a_x']
    _d['L0_attn_a_x'] = jax.random.normal(jax.random.fold_in(jax.random.key(seed), 1), (1, 2048, 128), dtype=_x0.dtype)
    del _x0
    return _d

def reference(L0_attn_a_x, L0_attn_a_Wq, L0_attn_a_Wk, L0_attn_a_Wv, L0_attn_a_Wo, L0_attn_b_qkv_w, L0_attn_b_qkv_b, L0_attn_b_out_w, L0_attn_b_out_b, L0_ffn_ln1_g, L0_ffn_ln1_b, L0_ffn_Wqkv, L0_ffn_bqkv, L0_ffn_Wo, L0_ffn_bo, L0_ffn_ln2_g, L0_ffn_ln2_b, L0_ffn_gate_w, L0_ffn_W1, L0_ffn_b1, L0_ffn_W2, L0_ffn_b2, L0_ffn_rW1, L0_ffn_rb1, L0_ffn_rW2, L0_ffn_rb2, L0_ffn_coef_w, L0_ffn_coef_b):

    def _L0_attn_a_ref(x, Wq, Wk, Wv, Wo):
        import jax, jax.numpy as jnp
        import numpy as np
        D_MODEL = 128
        N_HEADS = 16
        D_HEAD = D_MODEL // N_HEADS
        SCALE = 1.0 / np.sqrt(D_HEAD)
        B, S, _ = x.shape

        def proj(W):
            return (x @ W.T).reshape(B, S, N_HEADS, D_HEAD).transpose(0, 2, 1, 3)
        Q, K, V = (proj(Wq), proj(Wk), proj(Wv))
        attn = jnp.einsum('bhqd,bhkd->bhqk', Q, K) * SCALE
        causal = jnp.tril(jnp.ones((S, S), dtype=bool))
        attn = jnp.where(causal, attn, -jnp.inf)
        attn = jax.nn.softmax(attn, axis=-1)
        out = jnp.einsum('bhqk,bhkd->bhqd', attn, V)
        out = out.transpose(0, 2, 1, 3).reshape(B, S, D_MODEL)
        return out @ Wo.T

    def _L0_attn_b_ref(x, qkv_w, qkv_b, out_w, out_b):
        import jax, jax.numpy as jnp
        import numpy as np
        B, L, E, H = (1, 512, 128, 16)
        D = E // H
        EPS = 1e-06
        b, l, e = x.shape
        qkv = x @ qkv_w + qkv_b
        q, k, v = jnp.split(qkv, 3, axis=-1)
        q = q.reshape(b, l, H, D).transpose(0, 2, 1, 3)
        k = k.reshape(b, l, H, D).transpose(0, 2, 1, 3)
        v = v.reshape(b, l, H, D).transpose(0, 2, 1, 3)
        q_prime = jax.nn.elu(q) + 1.0
        k_prime = jax.nn.elu(k) + 1.0
        kv_prod = jnp.einsum('bhld,bhle->bhlde', k_prime, v)
        kv_cumsum = jnp.cumsum(kv_prod, axis=2)
        context = jnp.einsum('bhld,bhlde->bhle', q_prime, kv_cumsum)
        k_cumsum = jnp.cumsum(k_prime, axis=2)
        norm = jnp.einsum('bhld,bhld->bhl', q_prime, k_cumsum)
        output = context / (norm[..., None] + EPS)
        output = output.transpose(0, 2, 1, 3).reshape(b, l, e)
        return output @ out_w + out_b

    def _L0_ffn_ref(x, ln1_g, ln1_b, Wqkv, bqkv, Wo, bo, ln2_g, ln2_b, gate_w, W1, b1, W2, b2, rW1, rb1, rW2, rb2, coef_w, coef_b):
        import jax, jax.numpy as jnp
        import numpy as np
        DIM, HEADS, FFN, E = (128, 16, 512, 8)
        B, S = (2, 128)
        EPS = 1e-05

        def _ln(x, g, b):
            mu = jnp.mean(x, axis=-1, keepdims=True)
            var = jnp.mean((x - mu) ** 2, axis=-1, keepdims=True)
            return (x - mu) * jax.lax.rsqrt(var + EPS) * g + b
        b, s, d = x.shape
        h, dh = (HEADS, d // HEADS)
        xn = _ln(x, ln1_g, ln1_b)
        qkv = xn @ Wqkv + bqkv
        q, k, v = jnp.split(qkv, 3, axis=-1)
        q = q.reshape(b, s, h, dh)
        k = k.reshape(b, s, h, dh)
        v = v.reshape(b, s, h, dh)
        scores = jnp.einsum('bqhd,bkhd->bhqk', q, k) / jnp.sqrt(jnp.float32(dh))
        attn = jax.nn.softmax(scores, axis=-1)
        ctx = jnp.einsum('bhqk,bkhd->bqhd', attn, v).reshape(b, s, d)
        x = x + ctx @ Wo + bo
        xn2 = _ln(x, ln2_g, ln2_b)
        xt = xn2.reshape(b * s, d)
        probs = jax.nn.softmax(xt @ gate_w, axis=-1)
        gate_val = jnp.max(probs, axis=-1, keepdims=True)
        expert_idx = jnp.argmax(probs, axis=-1)
        oh = jax.nn.one_hot(expert_idx, E, dtype=xt.dtype)
        xe = jnp.einsum('te,td->etd', oh, xt)
        he = jax.nn.gelu(jnp.einsum('etd,edf->etf', xe, W1) + b1[:, None, :], approximate=False)
        ye = jnp.einsum('etf,efd->etd', he, W2) + b2[:, None, :]
        moe_out = jnp.einsum('te,etd->td', oh, ye) * gate_val
        rm = jax.nn.gelu(xt @ rW1 + rb1, approximate=False) @ rW2 + rb2
        coef = jax.nn.softmax(xt @ coef_w + coef_b, axis=-1)
        ff = moe_out * coef[:, 0:1] + rm * coef[:, 1:2]
        return x + ff.reshape(b, s, d)
    x = L0_attn_a_x
    x = x + _L0_attn_a_ref(_layernorm(x, axis=-1), L0_attn_a_Wq, L0_attn_a_Wk, L0_attn_a_Wv, L0_attn_a_Wo)
    x = x + _L0_ffn_ref(_layernorm(x, axis=-1), L0_ffn_ln1_g, L0_ffn_ln1_b, L0_ffn_Wqkv, L0_ffn_bqkv, L0_ffn_Wo, L0_ffn_bo, L0_ffn_ln2_g, L0_ffn_ln2_b, L0_ffn_gate_w, L0_ffn_W1, L0_ffn_b1, L0_ffn_W2, L0_ffn_b2, L0_ffn_rW1, L0_ffn_rb1, L0_ffn_rW2, L0_ffn_rb2, L0_ffn_coef_w, L0_ffn_coef_b)
    x = x + _L0_attn_b_ref(_layernorm(x, axis=-1), L0_attn_b_qkv_w, L0_attn_b_qkv_b, L0_attn_b_out_w, L0_attn_b_out_b)
    x = x + _L0_ffn_ref(_layernorm(x, axis=-1), L0_ffn_ln1_g, L0_ffn_ln1_b, L0_ffn_Wqkv, L0_ffn_bqkv, L0_ffn_Wo, L0_ffn_bo, L0_ffn_ln2_g, L0_ffn_ln2_b, L0_ffn_gate_w, L0_ffn_W1, L0_ffn_b1, L0_ffn_W2, L0_ffn_b2, L0_ffn_rW1, L0_ffn_rb1, L0_ffn_rW2, L0_ffn_rb2, L0_ffn_coef_w, L0_ffn_coef_b)
    return x

_drawn_inputs = setup_inputs


def setup_inputs(seed=0):
    import zlib

    import numpy as np

    out = dict(_drawn_inputs(seed))
    spreads = {'L0_attn_b_qkv_b': (0.0, 0.1),
     'L0_attn_b_out_b': (0.0, 0.1),
     'L0_ffn_ln1_g': (1.0, 0.6),
     'L0_ffn_ln1_b': (0.0, 0.8),
     'L0_ffn_bqkv': (0.0, 0.427),
     'L0_ffn_bo': (0.0, 0.1),
     'L0_ffn_ln2_g': (1.0, 0.6),
     'L0_ffn_ln2_b': (0.0, 0.8),
     'L0_ffn_b1': (0.0, 0.8),
     'L0_ffn_b2': (0.0, 0.8),
     'L0_ffn_rb1': (0.0, 0.666),
     'L0_ffn_rb2': (0.0, 0.1),
     'L0_ffn_coef_b': (0.0, 0.8)}
    factors = {'L0_attn_a_Wq': 4.518,
     'L0_attn_a_Wk': 4.367,
     'L0_ffn_Wqkv': 8.0,
     'L0_ffn_Wo': 2.787,
     'L0_ffn_gate_w': 7.344,
     'L0_ffn_W1': 8.0,
     'L0_ffn_W2': 8.0,
     'L0_ffn_coef_w': 7.912}
    for name, (base, spread) in spreads.items():
        noise = np.random.default_rng([zlib.crc32(name.encode()), seed]).standard_normal(out[name].shape)
        drawn = base * np.exp(spread * noise) if base else spread * noise
        out[name] = jnp.asarray(drawn.astype(out[name].dtype))
    for name, factor in factors.items():
        out[name] = (out[name] * factor).astype(out[name].dtype)
    return out
```

```python
from contextlib import ExitStack

import concourse.bass as bass
from concourse import mybir
from concourse.alu_op_type import AluOpType as ALU

F32, BF16 = mybir.dt.float32, mybir.dt.bfloat16
ACT = mybir.ActivationFunctionType
AX = mybir.AxisListType

P = 128
T, D, H, DH = 2048, 128, 16, 8
TILES = T // P
CHUNK = 512
CT = CHUNK // P
CHUNKS = T // CHUNK
QUAD = 4
QUADS = H // QUAD
PAIRS = H // 2
SLOT = 64
MCOL = 48
FFN, EXPERTS = 512, 8
NE = EXPERTS + 1
FC = FFN // P
SCALE = DH ** -0.5
MASKED = -1e30
LEAD = 18
NQ = 4
Q_PARTS = (0, 0, 1, 1, 0, 2)
K_PARTS = (0, 1, 0, 1, 2, 0)
E1 = DH + 1


def attention_schedule(causal):
    keys = [CT * (b + 1) if causal else TILES for b in range(NQ)]
    start = [sum(keys[:b]) for b in range(NQ + 1)]
    steps = start[NQ]
    units = []
    for b in range(NQ):
        for c in range(b + 1 if causal else CHUNKS):
            for tt in range(CT):
                for h in range(QUAD):
                    diagonal = causal and c == b
                    units.append((b, tt, h, c, (tt + 1) * P if diagonal else CHUNK, diagonal))
    assert len(units) == 4 * steps
    first = [next(i for i, u in enumerate(units) if u[0] == b) for b in range(NQ)]
    last = [max(i for i, u in enumerate(units) if u[0] == b) for b in range(NQ)]
    sched = []
    for s in range(-LEAD - 2, steps):
        e = {"units": [], "jobs": [], "chain": []}
        for i in range(4):
            u = 4 * (s + LEAD) + i
            if u >= 0:
                ahead, k = divmod(u, 4 * steps)
                e["units"].append((ahead, u, *units[k]))
                if k == last[units[k][0]]:
                    e["chain"].append((ahead, units[k][0]))
        for ahead in (0, 1):
            for b in range(NQ):
                if s == ahead * steps + first[b] // 4 - LEAD - 2:
                    e["jobs"].append(("qa", ahead, b))
                if s == ahead * steps + start[b] - 1:
                    e["jobs"].append(("qb", ahead, b))
        for b in range(NQ - 1):
            if s == start[b + 1] + 2:
                e["jobs"].append(("ctx", 0, b))
        sched.append(e)
    return keys, start, steps, sched[:LEAD + 2], sched[LEAD + 2:]


def build(nc, x, a_wq, a_wk, a_wv, a_wo, l_wqkv, l_bqkv, l_wo, l_bo, ln1_g, ln1_b, f_wqkv, f_bqkv,
          f_wo, f_bo, ln2_g, ln2_b, gate_w, w1, b1, w2, b2, rw1, rb1, rw2, rb2, coef_w, coef_b, out):
    top = ExitStack()

    def sb(name, cols, dt=F32, parts=P):
        return top.enter_context(nc.sbuf_tensor(name, [parts, cols], dt))

    def sem(name):
        return top.enter_context(nc.semaphore(name))

    made = {}

    def phase_sems(phase, names):
        if phase in made:
            with nc.Block() as block:
                @block.sync
                def _(sp):
                    for h in made[phase].values():
                        sp.sem_clear(h)
        else:
            made[phase] = {n: sem(f"{phase}_{n}") for n in names}
        return made[phase]

    X = sb("X", T)
    U = sb("U", T)
    XH = sb("XH", T)
    QT = sb("QT", TILES * H * SLOT, BF16)
    KT = sb("KT", PAIRS * T, BF16)
    V = sb("V", T)
    AR = sb("AR", 16384)
    W2S = sb("W2S", NE * FC * D)
    IDF = sb("IDF", P)
    IDB = sb("IDB", P, BF16)
    MQK = sb("MQK", P, BF16)
    MKQ = sb("MKQ", P, BF16)
    UPTO = sb("UPTO", P)
    ONES = sb("ONES", P)
    MHALF = sb("MHALF", TILES)
    AW = sb("AW", 4 * D)
    LW = sb("LW", 4 * D)
    FW = sb("FW", 4 * D)
    LB = sb("LB", 4 * D)
    FB = sb("FB", 4 * D)
    GB = sb("GB", 4)
    GC = sb("GC", EXPERTS + 2)
    GCB = sb("GCB", EXPERTS + 2)
    RANK = sb("RANK", EXPERTS)
    B1T = sb("B1T", NE * FC)
    B2S = sb("B2S", D, F32, NE)
    ST6 = sb("ST6", CT * 6)
    MV = sb("MV", CT * 2)
    VE = sb("VE", CT)
    RSTD = sb("RSTD", CT)
    BK = [top.enter_context(nc.psum_tensor(f"BK{i}", [P, 512], F32)) for i in range(2)]
    PS = top.enter_context(nc.psum_tensor("PS", [P, 6 * 512], F32))

    def bank(i, n=1):
        return BK[i][:, :] if i < 2 else PS[:, 512 * (i - 2):512 * (i - 2 + n)]

    def arena(at, cols, dt=F32):
        words = cols if dt == F32 else cols // 2
        v = AR[:, at:at + words]
        return v if dt == F32 else v.bitcast(dt)

    s_in, s_cst, s_wt, s_wtc = sem("inputs_loaded"), sem("constants_made"), sem("a_weights_turned"), sem("a_weights_kept")
    RAW = arena(0, 4 * D)
    B1R = arena(512, P)
    with nc.Block() as block:
        @block.sync
        def _(sp):
            n = 0
            loads = [(X[:, :].rearrange("p (t d) -> p t d", d=D), x.rearrange("b (t p) d -> p (b t) d", p=P))]
            loads += [(RAW[:, D * i:D * i + D], w) for i, w in enumerate((a_wq, a_wk, a_wv, a_wo))]
            loads += [(LW[:, 0:3 * D], l_wqkv), (LW[:, 3 * D:4 * D], l_wo), (FW[:, 0:3 * D], f_wqkv), (FW[:, 3 * D:4 * D], f_wo)]
            loads += [(LB[:, 0:3 * D], l_bqkv.partition_broadcast(P)), (LB[:, 3 * D:4 * D], l_bo.partition_broadcast(P))]
            loads += [(FB[:, 0:3 * D], f_bqkv.partition_broadcast(P)), (FB[:, 3 * D:4 * D], f_bo.partition_broadcast(P))]
            loads += [(GB[:, i:i + 1], v.rearrange("(p o) -> p o", o=1)) for i, v in enumerate((ln1_g, ln1_b, ln2_g, ln2_b))]
            loads += [(GC[:, 0:EXPERTS], gate_w), (GC[:, EXPERTS:EXPERTS + 2], coef_w),
                      (GCB[:, EXPERTS:EXPERTS + 2], coef_b.partition_broadcast(P))]
            loads += [(B1R[0:EXPERTS * FC, :], b1.rearrange("e (c f) -> (e c) f", f=P)),
                      (B1R[EXPERTS * FC:NE * FC, :], rb1.rearrange("(c f) -> c f", f=P))]
            loads += [(B2S[0:EXPERTS, :], b2), (B2S[EXPERTS:NE, :], rb2.rearrange("(o d) -> o d", o=1))]
            w2v = W2S[:, :].rearrange("p (e c d) -> p e c d", c=FC, d=D)
            loads += [(w2v[:, e, :, :], w2[e, :, :].rearrange("(c p) d -> p c d", p=P)) for e in range(EXPERTS)]
            loads += [(w2v[:, EXPERTS, :, :], rw2.rearrange("(c p) d -> p c d", p=P))]
            for dst, src in loads:
                sp.dma_start(dst, src).then_inc(s_in, 16)
                n += 16
            sp.wait_ge(s_in, n)

        n_loads = 1 + 4 + 4 + 4 + 4 + 3 + 2 + 2 + NE

        @block.gpsimd
        def _(pool):
            pool.memset(IDF[:, :], 0.0).then_inc(s_cst, 1)
            pool.memset(ONES[:, :], 1.0).then_inc(s_cst, 1)
            pool.memset(MQK[:, :], 0.0).then_inc(s_cst, 1)
            pool.memset(MKQ[:, :], 0.0).then_inc(s_cst, 1)
            pool.memset(MHALF[:, :], -0.5).then_inc(s_cst, 1)
            pool.memset(GCB[:, 0:EXPERTS], 0.0).then_inc(s_cst, 1)
            for e in range(EXPERTS):
                pool.memset(RANK[:, e:e + 1], float(EXPERTS - e)).then_inc(s_cst, 1)
            pool.wait_ge(s_cst, 6 + EXPERTS)
            pool.affine_select(out=IDF[:, :], in_=IDF[:, :], compare_op=ALU.not_equal, fill=1.0, base=0,
                               pattern=[[-1, P]], channel_multiplier=1).then_inc(s_cst, 1)
            pool.affine_select(out=MQK[:, :], in_=MQK[:, :], compare_op=ALU.is_ge, fill=MASKED, base=0,
                               pattern=[[-1, P]], channel_multiplier=1).then_inc(s_cst, 1)
            pool.affine_select(out=MKQ[:, :], in_=MKQ[:, :], compare_op=ALU.is_ge, fill=MASKED, base=0,
                               pattern=[[1, P]], channel_multiplier=-1).then_inc(s_cst, 1)
            pool.affine_select(out=UPTO[:, :], in_=ONES[:, :], compare_op=ALU.is_ge, fill=0.0, base=0,
                               pattern=[[1, P]], channel_multiplier=-1).then_inc(s_cst, 1)
            pool.wait_ge(s_cst, 10 + EXPERTS)
            pool.tensor_copy(IDB[:, :], IDF[:, :]).then_inc(s_cst, 1)

        @block.tensor
        def _(pe):
            pe.wait_ge(s_cst, 10 + EXPERTS)
            pe.wait_ge(s_in, 16 * n_loads)
            for i in range(4):
                pe.transpose(bank(0)[:, D * i:D * i + D], RAW[:, D * i:D * i + D], IDF[:, :])
            n = NE * FC
            pe.transpose(bank(1)[:, 0:n], B1R[0:n, :], IDF[0:n, 0:n]).then_inc(s_wt, 1)

        @block.scalar
        def _(act):
            act.wait_ge(s_wt, 1)
            act.copy(AW[:, :], bank(0)).then_inc(s_wtc, 1)
            act.copy(B1T[:, :], bank(1)[:, 0:NE * FC]).then_inc(s_wtc, 1)

        @block.vector
        def _(dve):
            dve.memset(QT[:, :].bitcast(F32), 0.0).then_inc(s_wtc, 1)

    def norm_dve(dve, s, c, j, n, src, dst):
        k = n * c + j
        if k:
            dve.wait_ge(s["xh"], CT * k)
        for i in range(CT):
            dve.bn_stats(ST6[:, 6 * i:6 * i + 6], src[:, bass.ds((CT * c + i) * P, P)]).then_inc(s["st"], 1)
        dve.wait_ge(s["st"], CT * k + CT)
        for i in range(CT):
            dve.bn_aggr(MV[:, 2 * i:2 * i + 2], ST6[:, 6 * i:6 * i + 6]).then_inc(s["mv"], 1)
        dve.wait_ge(s["mv"], CT * k + CT)
        dve.wait_ge(s["rstd"], k + 1)
        for i in range(CT):
            dve.tensor_scalar(dst[:, bass.ds((CT * c + i) * P, P)], src[:, bass.ds((CT * c + i) * P, P)],
                              MV[:, 2 * i:2 * i + 1], RSTD[:, i:i + 1], ALU.subtract, ALU.mult).then_inc(s["xh"], 1)

    def norm_pool(pool, s, k):
        pool.wait_ge(s["mv"], CT * k + CT)
        if k:
            pool.wait_ge(s["xh"], CT * k)
        pool.tensor_scalar(VE[:, :], MV[:, :].rearrange("p (t two) -> p t two", two=2)[:, :, 1], 1e-5, None,
                           ALU.add).then_inc(s["ve"], 1)
        pool.wait_ge(s["ve"], k + 1)
        pool.tensor_tensor(RSTD[:, :], VE[:, :], MHALF[:, 0:CT], ALU.pow).then_inc(s["rstd"], 1)

    def prepare(kind):
        s = phase_sems("prepare", ("st", "mv", "ve", "rstd", "xh", "turned", "xt", "qkv", "qk", "v",
                                            "a0", "r1", "a1", "a2", "tok", "ktp", "kte", "e", "ones", "bias"))
        W = {"a": AW, "f": FW, "l": LW}[kind]
        B = {"a": None, "f": FB, "l": LB}[kind]
        norms = 2 if kind == "f" else 1
        KTOK = [arena(4096 * p // 2 * 1, 4096, BF16) for p in range(2)]
        QK = [arena(4096 + 1024 * p, 1024) for p in range(2)]
        R1 = [arena(6144 + 1024 * p, 1024) for p in range(2)]
        A = [[arena(8192 + 512 * (3 * p + i), 1024, BF16) for i in range(3)] for p in range(2)]
        XT = [arena(11264 + 512 * p, 512) for p in range(2)]
        TB = [bank(0), bank(1)]
        G = [bank(2, 3), bank(5, 3)]
        QF = KT[:, :].bitcast(F32)
        V1 = QT[:, :].bitcast(F32)

        with nc.Block() as block:
            @block.gpsimd
            def _(pool):
                for k in range(norms * CHUNKS):
                    norm_pool(pool, s, k)
                if kind == "f":
                    pool.wait_ge(s["xh"], CT * norms * CHUNKS)
                    pool.tensor_tensor(U[:, :].rearrange("p (t d) -> p t d", d=D), U[:, :].rearrange("p (t d) -> p t d", d=D),
                                       B[:, 3 * D:4 * D].unsqueeze(1).to_broadcast([P, TILES, D]), ALU.add).then_inc(s["bias"], 1)
                if kind == "l":
                    pool.wait_ge(s["xh"], CT * norms * CHUNKS)
                    pool.tensor_tensor(X[:, :].rearrange("p (t d) -> p t d", d=D), X[:, :].rearrange("p (t d) -> p t d", d=D),
                                       B[:, 3 * D:4 * D].unsqueeze(1).to_broadcast([P, TILES, D]), ALU.add).then_inc(s["bias"], 1)
                    return
                for c in range(CHUNKS):
                    p = c % 2
                    pool.wait_ge(s["a0"], c + 1)
                    pool.wait_ge(s["qk"], c + 1)
                    pool.tensor_tensor(R1[p], QK[p], A[p][0], ALU.subtract).then_inc(s["r1"], 1)
                    pool.wait_ge(s["a1"], c + 1)
                    pool.tensor_tensor(A[p][2], R1[p], A[p][1], ALU.subtract).then_inc(s["a2"], 1)

            @block.vector
            def _(dve):
                for c in range(CHUNKS):
                    if kind == "f":
                        norm_dve(dve, s, c, 0, 2, X, U)
                        norm_dve(dve, s, c, 1, 2, U, XH)
                    else:
                        norm_dve(dve, s, c, 0, 1, X, XH)
                if kind == "l":
                    dve.memset(V1[:, 0:TILES * H * E1], 1.0).then_inc(s["ones"], 1)
                    dve.wait_ge(s["ones"], 1)
                else:
                    for p in range(2):
                        kp = KTOK[p].rearrange("p (n s) -> p n s", s=SLOT)
                        dve.memset(kp[:, :, MCOL:MCOL + 3], 1.0).then_inc(s["ones"], 1)
                        dve.memset(kp[:, :, MCOL + 3:SLOT], 0.0).then_inc(s["ones"], 1)
                for c in range(CHUNKS):
                    p = c % 2
                    src = G[p][:, 0:1024].rearrange("p (i q d) -> p i q d", i=CT, d=D)
                    dst = QK[p].rearrange("p (q i d) -> p i q d", i=CT, d=D)
                    vsrc = G[p][:, 1024:1536]
                    dve.wait_ge(s["qkv"], c + 1)
                    if kind != "l" and c >= 2:
                        dve.wait_ge(s["a0"], c - 1)
                        dve.wait_ge(s["r1"], c - 1)
                    if kind == "l":
                        vdst = V1[:, c * CT * H * E1:(c + 1) * CT * H * E1].rearrange("p (n e) -> p n e", e=E1)[:, :, 0:DH]
                    else:
                        vdst = V[:, c * CHUNK:(c + 1) * CHUNK]
                    if B is None:
                        dve.tensor_copy(dst, src).then_inc(s["qk"], 1)
                        dve.tensor_copy(vdst, vsrc).then_inc(s["v"], 1)
                    else:
                        for i in range(CT):
                            ins = dve.tensor_tensor(dst[:, i], src[:, i], B[:, 0:2 * D].rearrange("p (q d) -> p q d", d=D), ALU.add)
                        ins.then_inc(s["qk"], 1)
                        if kind == "l":
                            for i in range(CT):
                                ins = dve.tensor_tensor(vdst[:, H * i:H * i + H, :],
                                                        vsrc[:, D * i:D * i + D].rearrange("p (h d) -> p h d", d=DH),
                                                        B[:, 2 * D:3 * D].rearrange("p (h d) -> p h d", d=DH), ALU.add)
                        else:
                            ins = dve.tensor_tensor(vdst.rearrange("p (i d) -> p i d", d=D), vsrc.rearrange("p (i d) -> p i d", d=D),
                                                    B[:, 2 * D:3 * D].unsqueeze(1).to_broadcast([P, CT, D]), ALU.add)
                        ins.then_inc(s["v"], 1)
                    if kind == "l":
                        dve.wait_ge(s["qk"], c + 1)
                        dve.tensor_scalar(R1[p], QK[p], 0.0, None, ALU.min).then_inc(s["r1"], 1)
                        dve.wait_ge(s["e"], c + 1)
                        fdst = QF[:, 2 * c * CHUNK:2 * (c + 1) * CHUNK]
                        dve.scalar_tensor_tensor(out=fdst, in0=QK[p], scalar=0.0, in1=A1F[p], op0=ALU.max,
                                                 op1=ALU.add).then_inc(s["tok"], 1)
                        continue
                    qd = QT[:, c * CT * H * SLOT:(c + 1) * CT * H * SLOT].rearrange("p (n s) -> p n s", s=SLOT)
                    kd = KTOK[p].rearrange("p (n s) -> p n s", s=SLOT)
                    dve.wait_ge(s["a2"], c + 1)
                    if c >= 2:
                        dve.wait_ge(s["ktp"], CT * (c - 1))
                    for slot in range(6):
                        for half, (dd, parts) in enumerate(((qd, Q_PARTS), (kd, K_PARTS))):
                            a = A[p][parts[slot]][:, CHUNK * half:CHUNK * half + CHUNK].rearrange("p (n d) -> p n d", d=DH)
                            ins = dve.tensor_copy(dd[:, :, DH * slot:DH * slot + DH], a)
                    ins.then_inc(s["tok"], 1)

            @block.tensor
            def _(pe):
                def turn(c):
                    p = c % 2
                    pe.wait_ge(s["xh"], norms * CT * (c + 1))
                    if c >= 2:
                        pe.wait_ge(s["xt"], c - 1)
                    for i in range(CT):
                        ins = pe.transpose(TB[p][:, P * i:P * i + P], XH[:, (CT * c + i) * P:(CT * c + i + 1) * P], IDF[:, :])
                    ins.then_inc(s["turned"], 1)

                def project(c):
                    p = c % 2
                    pe.wait_ge(s["xt"], c + 1)
                    if c >= 2:
                        if kind == "l":
                            pe.wait_ge(s["v"], c - 1)
                        else:
                            pe.wait_ge(s["kte"], CT * (c - 1))
                    for i in range(CT):
                        lhs = XT[p][:, P * i:P * i + P]
                        pe.matmul(G[p][:, 256 * i:256 * i + 256], lhs, W[:, 0:2 * D], start=True, stop=True)
                        ins = pe.matmul(G[p][:, 1024 + P * i:1024 + P * i + P], lhs, W[:, 2 * D:3 * D], start=True, stop=True)
                    ins.then_inc(s["qkv"], 1)

                def turn_k(c):
                    p = c % 2
                    pe.wait_ge(s["tok"], c + 1)
                    if c < 2:
                        pe.wait_ge(s["ones"], 4 if kind == "a" else 4)
                    for i in range(CT):
                        if i == 3:
                            pe.wait_ge(s["kte"], CT * c + 1)
                        dst = G[p][:, 512 * (i % 3):512 * (i % 3) + 512].bitcast(BF16)
                        for j in range(PAIRS):
                            ins = pe.transpose(dst[:, P * j:P * j + P],
                                               KTOK[p][:, (i * PAIRS + j) * P:(i * PAIRS + j + 1) * P], IDB[:, :])
                        ins.then_inc(s["ktp"], 1)

                turn(0)
                turn(1)
                project(0)
                project(1)
                for c in range(CHUNKS):
                    if c + 2 < CHUNKS:
                        turn(c + 2)
                    if kind != "l":
                        turn_k(c)
                    if c + 2 < CHUNKS:
                        project(c + 2)

            @block.scalar
            def _(act):
                def take_xt(c):
                    p = c % 2
                    act.wait_ge(s["turned"], c + 1)
                    if c >= 2:
                        act.wait_ge(s["qkv"], c - 1)
                    if kind == "f":
                        ins = act.activation(XT[p], TB[p], ACT.Identity, bias=GB[:, 1:2], scale=GB[:, 0:1])
                    else:
                        ins = act.copy(XT[p], TB[p])
                    ins.then_inc(s["xt"], 1)

                take_xt(0)
                take_xt(1)
                for c in range(CHUNKS):
                    p = c % 2
                    if kind == "l":
                        act.wait_ge(s["r1"], c + 1)
                        act.activation(A1F[p], R1[p], ACT.Exp).then_inc(s["e"], 1)
                        if c + 2 < CHUNKS:
                            take_xt(c + 2)
                        continue
                    act.wait_ge(s["qk"], c + 1)
                    if c >= 2:
                        act.wait_ge(s["tok"], c - 1)
                    act.copy(A[p][0], QK[p]).then_inc(s["a0"], 1)
                    if c + 2 < CHUNKS:
                        take_xt(c + 2)
                    act.wait_ge(s["r1"], c + 1)
                    act.copy(A[p][1], R1[p]).then_inc(s["a1"], 1)
                    for i in range(CT):
                        act.wait_ge(s["ktp"], CT * c + i + 1)
                        tile = CT * c + i
                        src = G[p][:, 512 * (i % 3):512 * (i % 3) + 512].bitcast(BF16).rearrange("p (j t) -> p j t", t=P)
                        act.copy(KT[:, :].rearrange("p (j t) -> p j t", t=T)[:, :, P * tile:P * tile + P], src).then_inc(s["kte"], 1)

    A1F = [arena(8192 + 1024 * p, 1024) for p in range(2)]

    def attention(causal):
        s = phase_sems("attention", ("staged", "qa", "qae", "qb", "qbe", "score", "max", "part", "minus",
                                            "qk", "exp", "pv", "acc", "ctx", "ctxe", "rcp", "done", "kc", "kn", "vc", "vset"))
        keys, start, steps, lead_in, body = attention_schedule(causal)
        block_of = [b for b in range(NQ) for _ in range(keys[b])]
        PR = [arena(2048 * i, 2048) for i in range(2)]
        QM = [arena(4096 + 512 * b, 1024, BF16) for b in range(NQ)]
        QA = [arena(6144 + 512 * b, 1024, BF16) for b in range(NQ)]
        QB = [arena(8192 + 512 * i, 1024, BF16) for i in range(2)]
        CTX = arena(9216, 512)
        CN = arena(9728, 512)
        KC = arena(10240, 2 * T, BF16)
        KN = arena(12288, 2 * T, BF16)
        VC = arena(14336, TILES * QUAD * 32)
        MX = ST6X[:, :]
        S2 = [bank(2, 2), bank(4, 2)]
        ACC, MISC = bank(6), bank(7)
        MB = [bank(0), bank(1)]
        kv = lambda k: k.rearrange("p (j t) -> p j t", t=T)
        vc = VC.rearrange("p (t h e) -> p t h e", h=QUAD, e=32)
        lead_units = sum(len(e["units"]) for e in lead_in)
        before = {k: sum(j[0] == k for e in lead_in for j in e["jobs"]) for k in ("qa", "qb", "ctx")}
        EV = {"qa": "qae", "qb": "qbe", "ctx": "ctxe"}

        def wait(e, name, n):
            if not isinstance(n, int) or n > 0:
                e.wait_ge(s[name], n)

        def pe_unit(pe, g, ahead, u, b, tt, h, c, width, diagonal, in_next):
            n = 4 * steps * g + u
            wait(pe, "max", n - 1) if not isinstance(n, int) or n >= 2 else None
            if tt == 0 and h == 0 and c == 0:
                pe.wait_ge(s["qae"], NQ * (g + ahead) + b + 1)
                if in_next:
                    pe.wait_ge(s["kn"], 16 * (g + 1))
            r = SLOT * (h % 2)
            k = kv(KN if in_next else KC)[r:r + MCOL, h // 2, CHUNK * c:CHUNK * c + width]
            q = QA[b].rearrange("p (j t) -> p j t", t=CHUNK)[r:r + MCOL, h // 2, P * tt:P * tt + P]
            dst = MB[u % 2]
            ins = pe.matmul(dst[:, 0:width], q, k, start=True, stop=not diagonal)
            if diagonal:
                ins = pe.matmul(dst[:, width - P:width], IDB[:, :], MQK[:, :], start=False, stop=True)
            ins.then_inc(s["score"], 1)

        def pe_scores(pe, g, st, pair):
            n = steps * g + st
            b = block_of[st]
            kt = st - start[b]
            lo = max(0, kt - CT * b) * P if causal else 0
            if st == 0:
                wait(pe, "exp", 2 * n)
            else:
                pe.wait_ge(s["exp"], 2 * n - 1 + pair)
            if kt == 0 and pair == 0:
                pe.wait_ge(s["qbe"], NQ * g + b + 1)
            for i in range(2):
                r = SLOT * i
                q = QB[b % 2].rearrange("p (j t) -> p j t", t=CHUNK)[r:r + MCOL + 3, pair, lo:CHUNK]
                k = kv(KC)[r:r + MCOL + 3, pair, P * kt:P * kt + P]
                dst = S2[pair][:, CHUNK * i:CHUNK * i + CHUNK]
                diagonal = causal and kt >= CT * b
                ins = pe.matmul(dst[:, lo:CHUNK], k, q, start=True, stop=not diagonal)
                if diagonal:
                    ins = pe.matmul(dst[:, lo:lo + P], IDB[:, :], MKQ[:, :], start=False, stop=True)
            ins.then_inc(s["qk"], 1)

        def pe_values(pe, g, st):
            n = steps * g + st
            b = block_of[st]
            kt = st - start[b]
            lo = max(0, kt - CT * b) * P if causal else 0
            pe.wait_ge(s["exp"], 2 * n + 2)
            if kt == 0:
                wait(pe, "acc", NQ * g + b)
            if st == 0:
                pe.wait_ge(s["vc"], g + 1)
            pr = PR[st % 2].rearrange("p (h t) -> p h t", t=CHUNK)
            for h in range(QUAD):
                ins = pe.matmul(ACC[32 * h:32 * h + 32, lo:CHUNK], vc[:, kt, h, :], pr[:, h, lo:CHUNK],
                                start=kt == 0, stop=kt == keys[b] - 1)
            ins.then_inc(s["pv"], 1)

        def pe_job(pe, g, kind, ahead, b, seen):
            for k in ("qa", "qb", "ctx"):
                wait(pe, EV[k], seen[k](g))
            nb = NQ * (g + ahead) + b
            if kind == "ctx":
                pe.wait_ge(s["acc"], nb + 1)
                for i in range(CT):
                    ins = pe.transpose(MISC[:, P * i:P * i + P], CTX[:, P * i:P * i + P], IDF[:, :])
            else:
                pe.wait_ge(s["staged" if kind == "qa" else "minus"], nb + 1)
                q = QM[b].rearrange("p (t j r) -> p t j r", j=2, r=P)
                dst = MISC.bitcast(BF16).rearrange("p (j t) -> p j t", t=CHUNK)
                for j in range(2):
                    for i in range(CT):
                        ins = pe.transpose(dst[:, j, P * i:P * i + P], q[:, i, j, :], IDB[:, :])
            ins.then_inc(s[kind], 1)

        def seen_before(entries, base, per):
            out, n = [], dict(base)
            for e in entries:
                row = []
                for job in e["jobs"]:
                    row.append({k: (lambda g, a=n[k], m=per[k]: a + m * g) for k in n})
                    n[job[0]] += 1
                out.append(row)
            return out, n

        zero = {"qa": 0, "qb": 0, "ctx": 0}
        seen_lead, _ = seen_before(lead_in, zero, zero)
        per = {"qa": NQ, "qb": NQ, "ctx": NQ}
        seen_body, seen_end = seen_before(body, before, per)

        def in_quad(e, last):
            keep = lambda x: not (last and x[0])
            return [u for u in e["units"] if keep(u)], [j for j in e["jobs"] if not (last and j[1])]

        def pe_body(pe, g, last):
            pe.wait_ge(s["kc"], g + 1)
            for st, e in enumerate(body):
                units, jobs = in_quad(e, last)
                for k, job in enumerate(e["jobs"]):
                    if job in jobs:
                        seen = seen_body[st][k]
                        if last:
                            gone = {q: sum(j[0] == q and j[1] for ee in body[:st] for j in ee["jobs"])
                                    + sum(j[0] == q and j[1] for j in e["jobs"][:k]) for q in zero}
                            seen = {q: (lambda g, f=seen[q], m=gone[q]: f(g) - m) for q in zero}
                        pe_job(pe, g, *job, seen)
                units = [lambda u=u: pe_unit(pe, g, *u, in_next=u[0] == 1) for u in units]
                take = lambda: units.pop(0)() if units else None
                take()
                pe_scores(pe, g, st, 0)
                take()
                pe_scores(pe, g, st, 1)
                take()
                if st:
                    pe_values(pe, g, st - 1)
                take()
            pe_values(pe, g, steps - 1)
            seen = dict(seen_end)
            if last:
                for q in zero:
                    seen[q] -= sum(j[0] == q and j[1] for ee in body for j in ee["jobs"])
            pe_job(pe, g, "ctx", 0, NQ - 1, {q: (lambda g, a=seen[q], m=per[q]: a + m * g) for q in zero})

        def dve_unit(dve, g, ahead, u, b, tt, h, c, width, diagonal):
            dve.wait_ge(s["score"], 4 * steps * g + u + 1)
            if tt == 0 and h == 0 and c == 0:
                wait(dve, "minus", NQ * (g + ahead) + b - NQ + 1) if ahead else None
            at = (b * CT * QUAD + tt * QUAD + h) * CHUNKS + c
            dve.tensor_reduce(MX[:, at:at + 1], MB[u % 2][:, 0:width], AX.X, ALU.max).then_inc(s["max"], 1)

        def dve_chain(dve, g, ahead, b, u_end):
            nb = NQ * (g + ahead) + b
            mx = MX[:, b * CT * QUAD * CHUNKS:(b + 1) * CT * QUAD * CHUNKS].rearrange("p (n c) -> p n c", c=CHUNKS)
            q = QM[b].rearrange("p (n s) -> p n s", s=SLOT)
            n_part = 4 * nb
            dve.wait_ge(s["max"], u_end)
            dve.wait_ge(s["qa"], nb + 1)
            dve.tensor_reduce(NM[:, 0:16], mx[:, :, 0:(b + 1 if causal else CHUNKS)], AX.X, ALU.max,
                              negate=True).then_inc(s["part"], 1)
            dve.wait_ge(s["part"], n_part + 1)
            dve.tensor_copy(q[:, :, MCOL], NM[:, 0:16]).then_inc(s["part"], 1)
            dve.wait_ge(s["part"], n_part + 2)
            dve.tensor_tensor(NM[:, 16:32], NM[:, 0:16], q[:, :, MCOL], ALU.subtract).then_inc(s["part"], 1)
            dve.wait_ge(s["part"], n_part + 3)
            dve.tensor_copy(q[:, :, MCOL + 1], NM[:, 16:32]).then_inc(s["part"], 1)
            dve.wait_ge(s["part"], n_part + 4)
            dve.tensor_tensor(q[:, :, MCOL + 2], NM[:, 16:32], q[:, :, MCOL + 1], ALU.subtract).then_inc(s["minus"], 1)

        def dve_sums(dve, g, b):
            nb = NQ * g + b
            dve.wait_ge(s["ctxe"], nb + 1)
            wait(dve, "done", nb)
            cn = CN.rearrange("p (n e) -> p n e", e=32)
            dve.reciprocal(RC[:, :], cn[:, :, DH]).then_inc(s["rcp"], 1)

        def dve_copy_k(dve, g):
            dve.wait_ge(s["kn"], 16 * (g + 1))
            dve.wait_ge(s["qk"], 2 * steps * (g + 1))
            dve.tensor_copy(KC, KN).then_inc(s["kc"], 1)

        def dve_copy_v(dve, g):
            wait(dve, "pv", steps * (g + 1) if not isinstance(g, int) or g >= 0 else 0)
            v = V[:, :].rearrange("p (t d) -> p t d", d=D)
            q = (g + 1) * QUAD * DH
            v = v[:, :, bass.ds(q, QUAD * DH)] if not isinstance(q, int) else v[:, :, q:q + QUAD * DH]
            dve.tensor_copy(vc[:, :, :, 0:DH], v.rearrange("p t (h d) -> p t h d", d=DH)).then_inc(s["vc"], 1)

        def dve_body(dve, g, last):
            for st, e in enumerate(body):
                units, _ = in_quad(e, last)
                for u in units:
                    dve_unit(dve, g, *u)
                    if (u[0], u[2]) in e["chain"] and u is [w for w in units if (w[0], w[2]) == (u[0], u[2])][-1]:
                        dve_chain(dve, g, u[0], u[2], 4 * steps * g + u[1] + 1)
                for b in range(NQ - 1):
                    if st == start[b + 1] + 3:
                        dve_sums(dve, g, b)
            if not last:
                dve_copy_k(dve, g)
                dve_copy_v(dve, g)
            dve_sums(dve, g, NQ - 1)

        def act_exp(act, g, st, pair):
            n = steps * g + st
            b = block_of[st]
            lo = max(0, st - start[b] - CT * b) * P if causal else 0
            act.wait_ge(s["qk"], 2 * n + pair + 1)
            if pair == 0:
                wait(act, "pv", steps * g + max(st - 1, 0))
            src = S2[pair].rearrange("p (h t) -> p h t", t=CHUNK)[:, :, lo:CHUNK]
            dst = PR[st % 2].rearrange("p (h t) -> p h t", t=CHUNK)[:, 2 * pair:2 * pair + 2, lo:CHUNK]
            act.activation(dst, src, ACT.Exp, scale=SCALE).then_inc(s["exp"], 1)

        def act_sums(act, g, b):
            nb = NQ * g + b
            act.wait_ge(s["pv"], steps * g + start[b + 1])
            wait(act, "ctx", nb)
            act.copy(CTX, ACC).then_inc(s["acc"], 1)

        def act_job(act, g, kind, ahead, b):
            nb = NQ * (g + ahead) + b
            act.wait_ge(s[kind], nb + 1)
            if kind == "ctx":
                wait(act, "done", nb)
                act.copy(CN, MISC).then_inc(s["ctxe"], 1)
            else:
                act.copy(QA[b] if kind == "qa" else QB[b % 2], MISC.bitcast(BF16)).then_inc(s[EV[kind]], 1)

        def act_body(act, g, last):
            for st, e in enumerate(body):
                for job in in_quad(e, last)[1]:
                    act_job(act, g, *job)
                act_exp(act, g, st, 0)
                act_exp(act, g, st, 1)
                if st in start[1:NQ]:
                    act_sums(act, g, start.index(st) - 1)
            act_sums(act, g, NQ - 1)
            act_job(act, g, "ctx", 0, NQ - 1)

        def pool_stage(pool, g, b):
            nb = NQ * g + b
            wait(pool, "qb", nb - NQ + 1) if not isinstance(nb, int) or nb >= NQ else None
            q = QT[:, :].rearrange("p (t r) -> p t r", r=H * SLOT)
            at = g * QUAD * SLOT
            sl = slice(at, at + QUAD * SLOT) if isinstance(at, int) else bass.ds(at, QUAD * SLOT)
            pool.tensor_copy(QM[b].rearrange("p (t r) -> p t r", r=QUAD * SLOT), q[:, CT * b:CT * b + CT, sl]).then_inc(s["staged"], 1)

        def pool_context(pool, g, b):
            pool.wait_ge(s["rcp"], NQ * g + b + 1)
            cn = CN.rearrange("p (t h e) -> p t h e", h=QUAD, e=32)[:, :, :, 0:DH]
            at = g * QUAD * DH
            sl = slice(at, at + QUAD * DH) if isinstance(at, int) else bass.ds(at, QUAD * DH)
            dst = XH[:, :].rearrange("p (t d) -> p t d", d=D)[:, CT * b:CT * b + CT, sl].rearrange("p t (h d) -> p t h d", d=DH)
            rc = RC[:, :].rearrange("p (t h) -> p t h", h=QUAD).unsqueeze(3).to_broadcast([P, CT, QUAD, DH])
            pool.tensor_tensor(dst, cn, rc, ALU.mult).then_inc(s["done"], 1)

        with nc.Block() as block:
            @block.sync
            def _(sp):
                sp.dma_start(kv(KN), kv(KT[:, :])[:, 2:4, :]).then_inc(s["kn"], 16)
                with sp.Fori(0, QUADS - 2) as g:
                    sp.wait_ge(s["kc"], g + 2)
                    sp.wait_ge(s["score"], 4 * steps * (g + 1) + lead_units)
                    sp.dma_start(kv(KN), kv(KT[:, :])[:, bass.ds(2 * g + 4, 2), :]).then_inc(s["kn"], 16)

            @block.gpsimd
            def _(pool):
                for b in range(NQ):
                    pool_stage(pool, 0, b)
                with pool.Fori(0, QUADS - 1) as g:
                    for b in range(NQ):
                        pool_stage(pool, g + 1, b)
                        pool_context(pool, g, b)
                for b in range(NQ):
                    pool_context(pool, QUADS - 1, b)

            @block.vector
            def _(dve):
                dve.tensor_copy(kv(KC), kv(KT[:, :])[:, 0:2, :]).then_inc(s["kc"], 1)
                dve.memset(VC, 0.0).then_inc(s["vset"], 1)
                dve.wait_ge(s["vset"], 1)
                dve.memset(vc[:, :, :, DH:DH + 1], 1.0).then_inc(s["vset"], 1)
                dve_copy_v(dve, -1)
                for e in lead_in:
                    for u in e["units"]:
                        dve_unit(dve, 0, *u)
                        if (u[0], u[2]) in e["chain"] and u is [w for w in e["units"] if (w[0], w[2]) == (u[0], u[2])][-1]:
                            dve_chain(dve, 0, u[0], u[2], u[1] + 1)
                with dve.Fori(0, QUADS - 1) as g:
                    dve_body(dve, g, False)
                dve_body(dve, QUADS - 1, True)

            @block.scalar
            def _(act):
                for e in lead_in:
                    for job in e["jobs"]:
                        act_job(act, 0, *job)
                with act.Fori(0, QUADS - 1) as g:
                    act_body(act, g, False)
                act_body(act, QUADS - 1, True)

            @block.tensor
            def _(pe):
                pe.wait_ge(s["kc"], 1)
                for st, e in enumerate(lead_in):
                    for k, job in enumerate(e["jobs"]):
                        pe_job(pe, 0, *job, seen_lead[st][k])
                    for u in e["units"]:
                        pe_unit(pe, 0, *u, in_next=False)
                pe.wait_ge(s["vset"], 2)
                with pe.Fori(0, QUADS - 1) as g:
                    pe_body(pe, g, False)
                pe_body(pe, QUADS - 1, True)

    def project_out(W, dst_of, res):
        s = phase_sems("project", ("t", "te", "o", "oe"))
        CTT = [arena(512 * p, 512) for p in range(2)]
        with nc.Block() as block:
            @block.tensor
            def _(pe):
                def turn(c):
                    if c >= 2:
                        pe.wait_ge(s["te"], c - 1)
                    for i in range(CT):
                        ins = pe.transpose(bank(c % 2)[:, P * i:P * i + P], XH[:, (CT * c + i) * P:(CT * c + i + 1) * P], IDF[:, :])
                    ins.then_inc(s["t"], 1)

                turn(0)
                for c in range(CHUNKS):
                    if c + 1 < CHUNKS:
                        turn(c + 1)
                    pe.wait_ge(s["te"], c + 1)
                    if c >= 2:
                        pe.wait_ge(s["oe"], c - 1)
                    for i in range(CT):
                        ins = pe.matmul(bank(2 + c % 2)[:, P * i:P * i + P], CTT[c % 2][:, P * i:P * i + P], W, start=True, stop=True)
                    ins.then_inc(s["o"], 1)

            @block.scalar
            def _(act):
                for c in range(CHUNKS):
                    act.wait_ge(s["t"], c + 1)
                    if c >= 2:
                        act.wait_ge(s["o"], c - 1)
                    act.copy(CTT[c % 2], bank(c % 2)).then_inc(s["te"], 1)

            @block.vector
            def _(dve):
                for c in range(CHUNKS):
                    dve.wait_ge(s["o"], c + 1)
                    a = slice(CHUNK * c, CHUNK * c + CHUNK)
                    dve.tensor_tensor(dst_of[:, a], bank(2 + c % 2), res[:, a], ALU.add).then_inc(s["oe"], 1)

    def experts():
        s = phase_sems("experts", ("w", "st", "mv", "ve", "rstd", "xh", "t", "xt", "lg", "r", "ex", "sw",
                                            "stt", "sts", "b2", "h", "gelu", "y", "acc", "xx"))
        W1S = QT[:, :].bitcast(F32)
        W1R = arena(0, FFN)
        XTT = KT[:, :].bitcast(F32)[:, 0:T]
        HT = [KT[:, :].bitcast(F32)[:, T + 2048 * i:T + 2048 * (i + 1)] for i in range(2)]
        L = arena(512, TILES * 10)
        EX = arena(768, TILES * 10)
        G1 = arena(1024, TILES * 8)
        R = arena(1280, 16 * TILES)
        SW = arena(2048, TILES * NE)
        SWT = arena(2304, T)

        def w1(e, f):
            if e == EXPERTS:
                return W1R[:, P * f:P * f + P]
            return W1S[:, FFN * e + P * f:FFN * e + P * f + P]

        def v3(a, n):
            return a.rearrange("p (t n) -> p t n", n=n)

        def col(a):
            return a.unsqueeze(2)

        with nc.Block() as block:
            @block.sync
            def _(sp):
                sp.dma_start(W1S.rearrange("p (e f) -> p e f", f=FFN)[:, 0:EXPERTS, :], w1_in.rearrange("e p f -> p e f")).then_inc(s["w"], 16)
                sp.dma_start(W1R, rw1).then_inc(s["w"], 16)

            @block.gpsimd
            def _(pool):
                for c in range(CHUNKS):
                    norm_pool(pool, s, c)
                pool.tensor_tensor(X[:, :], X[:, :], U[:, :], ALU.add).then_inc(s["xx"], 1)

            @block.vector
            def _(dve):
                for c in range(CHUNKS):
                    norm_dve(dve, s, c, 0, 1, U, XH)
                n = [0]

                def then(ins):
                    n[0] += 1
                    ins.then_inc(s["r"], 1)
                    dve.wait_ge(s["r"], n[0])

                r = lambda i: R[:, 16 * i:16 * i + 16]
                dve.wait_ge(s["lg"], TILES)
                then(dve.tensor_tensor(v3(L, 10), v3(bank(4)[:, 0:160], 10), GCB[:, :].unsqueeze(1).to_broadcast([P, TILES, 10]), ALU.add))
                dve.tensor_reduce(r(0), v3(L, 10)[:, :, 0:8], AX.X, ALU.max)
                then(dve.tensor_reduce(r(1), v3(L, 10)[:, :, 8:10], AX.X, ALU.max))
                dve.tensor_tensor(v3(EX, 10)[:, :, 0:8], v3(L, 10)[:, :, 0:8], col(r(0)).to_broadcast([P, TILES, 8]), ALU.subtract)
                then(dve.tensor_tensor(v3(EX, 10)[:, :, 8:10], v3(L, 10)[:, :, 8:10], col(r(1)).to_broadcast([P, TILES, 2]), ALU.subtract))
                then(dve.tensor_tensor(v3(G1, 8), v3(L, 10)[:, :, 0:8], col(r(0)).to_broadcast([P, TILES, 8]), ALU.is_equal))
                then(dve.tensor_tensor(v3(G1, 8), v3(G1, 8), RANK[:, :].unsqueeze(1).to_broadcast([P, TILES, 8]), ALU.mult))
                then(dve.tensor_reduce(r(2), v3(G1, 8), AX.X, ALU.max))
                then(dve.tensor_tensor(v3(G1, 8), v3(G1, 8), col(r(2)).to_broadcast([P, TILES, 8]), ALU.is_equal))
                dve.wait_ge(s["ex"], 1)
                dve.tensor_reduce(r(3), v3(EX, 10)[:, :, 0:8], AX.X, ALU.add)
                then(dve.tensor_reduce(r(4), v3(EX, 10)[:, :, 8:10], AX.X, ALU.add))
                dve.reciprocal(r(5), r(3))
                then(dve.reciprocal(r(6), r(4)))
                then(dve.tensor_tensor(r(7), r(5), r(6), ALU.mult))
                then(dve.tensor_tensor(r(8), r(7), v3(EX, 10)[:, :, 8], ALU.mult))
                dve.tensor_tensor(v3(SW, NE)[:, :, 0:8], v3(G1, 8), col(r(8)).to_broadcast([P, TILES, 8]), ALU.mult)
                dve.tensor_tensor(v3(SW, NE)[:, :, 8], r(6), v3(EX, 10)[:, :, 9], ALU.mult).then_inc(s["sw"], 1)
                dve.wait_ge(s["sw"], 1)
                dve.wait_ge(s["xx"], 1)
                for c in range(CHUNKS):
                    dve.wait_ge(s["b2"], c + 1)
                    a = slice(CHUNK * c, CHUNK * c + CHUNK)
                    dve.tensor_tensor(X[:, a], X[:, a], bank(6 + c % 2), ALU.add).then_inc(s["acc"], 1)
                with dve.Fori(0, CHUNKS) as c:
                    for e in range(NE):
                        k = NE * c + e
                        dve.wait_ge(s["y"], k + 1)
                        dve.wait_ge(s["acc"], CHUNKS + k)
                        for i in range(CT):
                            a = bass.ds((CT * c + i) * P, P)
                            ins = dve.scalar_tensor_tensor(out=X[:, a], in0=bank(6 + e % 2)[:, P * i:P * i + P],
                                                           scalar=SW[:, bass.ds((CT * c + i) * NE + e, 1)], in1=X[:, a],
                                                           op0=ALU.mult, op1=ALU.add)
                        ins.then_inc(s["acc"], 1)

            @block.scalar
            def _(act):
                for c in range(CHUNKS):
                    act.wait_ge(s["t"], c + 1)
                    act.activation(XTT[:, CHUNK * c:CHUNK * c + CHUNK], bank(c % 2), ACT.Identity, bias=GB[:, 3:4],
                                   scale=GB[:, 2:3]).then_inc(s["xt"], 1)
                act.wait_ge(s["r"], 3)
                act.activation(EX, EX, ACT.Exp).then_inc(s["ex"], 1)
                for c in range(CHUNKS):
                    act.wait_ge(s["stt"], c + 1)
                    act.copy(SWT[0:NE, CHUNK * c:CHUNK * c + CHUNK], bank(2 + c % 2)[0:NE, :]).then_inc(s["sts"], 1)
                with act.Fori(0, CHUNKS) as c:
                    for e in range(NE):
                        k = NE * c + e
                        act.wait_ge(s["y"], NE * c + max(e - 1, 0))
                        for f in range(FC):
                            act.wait_ge(s["h"], FC * k + f + 1)
                            act.activation(HT[e % 2][:, CHUNK * f:CHUNK * f + CHUNK], bank(2 + f), ACT.Gelu,
                                           bias=B1T[:, FC * e + f:FC * e + f + 1]).then_inc(s["gelu"], 1)

            @block.tensor
            def _(pe):
                for c in range(CHUNKS):
                    pe.wait_ge(s["xh"], CT * (c + 1))
                    if c >= 2:
                        pe.wait_ge(s["xt"], c - 1)
                    for i in range(CT):
                        ins = pe.transpose(bank(c % 2)[:, P * i:P * i + P], XH[:, (CT * c + i) * P:(CT * c + i + 1) * P], IDF[:, :])
                    ins.then_inc(s["t"], 1)
                for t in range(TILES):
                    if t % CT == 0:
                        pe.wait_ge(s["xt"], t // CT + 1)
                    pe.matmul(bank(4)[:, 10 * t:10 * t + 10], XTT[:, P * t:P * t + P], GC[:, :], start=True, stop=True).then_inc(s["lg"], 1)
                pe.wait_ge(s["sw"], 1)
                for c in range(CHUNKS):
                    if c >= 2:
                        pe.wait_ge(s["sts"], c - 1)
                    for i in range(CT):
                        t = CT * c + i
                        ins = pe.transpose(bank(2 + c % 2)[0:NE, P * i:P * i + P], SW[:, NE * t:NE * t + NE], IDF[:, :])
                    ins.then_inc(s["stt"], 1)
                for c in range(CHUNKS):
                    pe.wait_ge(s["sts"], c + 1)
                    if c >= 2:
                        pe.wait_ge(s["acc"], c - 1)
                    for i in range(CT):
                        t = CT * c + i
                        ins = pe.matmul(bank(6 + c % 2)[:, P * i:P * i + P], SWT[0:NE, P * t:P * t + P], B2S[:, :], start=True, stop=True)
                    ins.then_inc(s["b2"], 1)
                pe.wait_ge(s["w"], 32)
                pe.wait_ge(s["acc"], CHUNKS)

                def second(c, e):
                    k = NE * c + e
                    pe.wait_ge(s["gelu"], FC * k + FC)
                    pe.wait_ge(s["acc"], CHUNKS + NE * c + max(e - 1, 0))
                    for i in range(CT):
                        for f in range(FC):
                            ins = pe.matmul(bank(6 + e % 2)[:, P * i:P * i + P], HT[e % 2][:, CHUNK * f + P * i:CHUNK * f + P * i + P],
                                            W2S[:, (FC * e + f) * D:(FC * e + f + 1) * D], start=f == 0, stop=f == FC - 1)
                    ins.then_inc(s["y"], 1)

                with pe.Fori(0, CHUNKS) as c:
                    for e in range(NE):
                        k = NE * c + e
                        for f in range(FC):
                            if e == 0:
                                pe.wait_ge(s["gelu"], FC * k)
                            else:
                                pe.wait_ge(s["gelu"], FC * (k - 1) + f + 1)
                            pe.matmul(bank(2 + f), w1(e, f), XTT[:, bass.ds(CHUNK * c, CHUNK)], start=True, stop=True).then_inc(s["h"], 1)
                        if e:
                            second(c, e - 1)
                    second(c, NE - 1)

    w1_in = w1

    def linear_attention():
        s = phase_sems("linear", ("kv", "ks", "c", "prod", "red", "eps", "rcp", "o"))
        N = H * E1 * DH
        QF = KT[:, :].bitcast(F32).rearrange("p (c q i d) -> p c q i d", q=2, i=CT, d=D)
        V1 = QT[:, :].bitcast(F32)[:, 0:TILES * H * E1]
        KV = [arena(1280 * i, N) for i in range(2)]
        KS = [arena(2560 + 1280 * i, N) for i in range(2)]
        PROD = arena(5120, N)
        RED = arena(6400, H * E1)
        DEN = arena(6656, H)
        RDEN = arena(6688, H)
        C = [PS[:, 1536 * i:1536 * i + N] for i in range(2)]

        def hed(a):
            return a.rearrange("p (h e d) -> p h e d", e=E1, d=DH)

        with nc.Block() as block:
            @block.gpsimd
            def _(pool):
                pool.memset(KS[0], 0.0).then_inc(s["ks"], 1)
                for t in range(TILES):
                    i = t % 2
                    k = QF[:, t // CT, 1, t % CT, :].rearrange("p (h d) -> p h d", d=DH).unsqueeze(2).to_broadcast([P, H, E1, DH])
                    v = V1[:, H * E1 * t:H * E1 * (t + 1)].rearrange("p (h e) -> p h e", e=E1).unsqueeze(3).to_broadcast([P, H, E1, DH])
                    if t >= 2:
                        pool.wait_ge(s["c"], t - 1)
                    pool.tensor_tensor(hed(KV[i]), k, v, ALU.mult).then_inc(s["kv"], 1)
                    if t + 1 < TILES:
                        pool.wait_ge(s["kv"], t + 1)
                        if t >= 1:
                            pool.wait_ge(s["c"], t)
                        pool.wait_ge(s["ks"], t + 1)
                        pool.tensor_tensor(KS[1 - i], KS[i], KV[i], ALU.add).then_inc(s["ks"], 1)

            @block.tensor
            def _(pe):
                for t in range(TILES):
                    i = t % 2
                    pe.wait_ge(s["kv"], t + 1)
                    pe.wait_ge(s["ks"], t + 1)
                    if t >= 2:
                        pe.wait_ge(s["prod"], t - 1)
                    for a in range(0, N, 512):
                        b = min(a + 512, N)
                        pe.matmul(C[i][:, a:b], UPTO[:, :], KV[i][:, a:b], start=True, stop=False)
                        ins = pe.matmul(C[i][:, a:b], ONES[:, :], KS[i][:, a:b], start=False, stop=True)
                    ins.then_inc(s["c"], 1)

            @block.vector
            def _(dve):
                for t in range(TILES):
                    i = t % 2
                    q = QF[:, t // CT, 0, t % CT, :].rearrange("p (h d) -> p h d", d=DH).unsqueeze(2).to_broadcast([P, H, E1, DH])
                    dve.wait_ge(s["c"], t + 1)
                    dve.tensor_tensor(hed(PROD), hed(C[i]), q, ALU.mult).then_inc(s["prod"], 1)
                    dve.wait_ge(s["prod"], t + 1)
                    dve.tensor_reduce(RED, PROD.rearrange("p (n d) -> p n d", d=DH), AX.X, ALU.add).then_inc(s["red"], 1)
                    dve.wait_ge(s["red"], t + 1)
                    red = RED.rearrange("p (h e) -> p h e", e=E1)
                    dve.tensor_scalar(DEN, red[:, :, DH], 1e-6, None, ALU.add).then_inc(s["eps"], 1)
                    dve.wait_ge(s["eps"], t + 1)
                    dve.reciprocal(RDEN, DEN).then_inc(s["rcp"], 1)
                    dve.wait_ge(s["rcp"], t + 1)
                    dve.tensor_tensor(XH[:, P * t:P * t + P].rearrange("p (h d) -> p h d", d=DH), red[:, :, 0:DH],
                                      RDEN.unsqueeze(2).to_broadcast([P, H, DH]), ALU.mult).then_inc(s["o"], 1)

    ST6X = sb("MX", NQ * CT * QUAD * CHUNKS)
    NM = sb("NM", 32)
    RC = sb("RC", CT * QUAD)

    def ffn():
        prepare("f")
        attention(False)
        project_out(FW[:, 3 * D:4 * D], U, U)
        experts()

    def restore_padding(tag):
        done = sem(tag)
        with nc.Block() as block:
            @block.vector
            def _(dve):
                dve.memset(QT[:, :].bitcast(F32), 0.0).then_inc(done, 1)

    prepare("a")
    attention(True)
    project_out(AW[:, 3 * D:4 * D], X, X)
    ffn()
    prepare("l")
    linear_attention()
    project_out(LW[:, 3 * D:4 * D], X, X)
    restore_padding("zero_q")
    ffn()

    s_out = sem("output_stored")
    with nc.Block() as block:
        @block.sync
        def _(sp):
            sp.dma_start(out.rearrange("b (t p) d -> p (b t) d", p=P), X[:, :].rearrange("p (t d) -> p t d", d=D)).then_inc(s_out, 16)
            sp.wait_ge(s_out, 16)
    top.close()


_INS = ["L0_attn_a_x", "L0_attn_a_Wq", "L0_attn_a_Wk", "L0_attn_a_Wv", "L0_attn_a_Wo", "L0_attn_b_qkv_w",
        "L0_attn_b_qkv_b", "L0_attn_b_out_w", "L0_attn_b_out_b", "L0_ffn_ln1_g", "L0_ffn_ln1_b", "L0_ffn_Wqkv",
        "L0_ffn_bqkv", "L0_ffn_Wo", "L0_ffn_bo", "L0_ffn_ln2_g", "L0_ffn_ln2_b", "L0_ffn_gate_w", "L0_ffn_W1",
        "L0_ffn_b1", "L0_ffn_W2", "L0_ffn_b2", "L0_ffn_rW1", "L0_ffn_rb1", "L0_ffn_rW2", "L0_ffn_rb2",
        "L0_ffn_coef_w", "L0_ffn_coef_b"]


def kernel(**inputs):
    import numpy as _np
    import concourse.bacc as _bacc
    from concourse import mybir as _mybir
    from concourse.bass_utils import run_bass_kernel_spmd as _run

    nc = _bacc.Bacc("TRN2", target_bir_lowering=False, num_devices=1)
    arrays, args = {}, []
    for name in _INS:
        a = _np.ascontiguousarray(inputs[name])
        arrays[f"in_{name}_dram"] = a
        args.append(nc.dram_tensor(f"in_{name}_dram", a.shape, _mybir.dt.from_np(a.dtype), kind="ExternalInput").ap())
    args.append(nc.dram_tensor("out_dram", (1, T, D), F32, kind="ExternalOutput").ap())
    build(nc, *args)
    r = _run(nc, [arrays], core_ids=[0])
    return r.results[0]["out_dram"]
```

```python
from contextlib import ExitStack

import concourse.bass as bass
from concourse import mybir
from concourse.alu_op_type import AluOpType as ALU

F32, BF16 = mybir.dt.float32, mybir.dt.bfloat16
ACT = mybir.ActivationFunctionType
AX = mybir.AxisListType

P = 128
T, D, H, DH = 2048, 128, 16, 8
TILES = T // P
CHUNK = 512
CT = CHUNK // P
CHUNKS = T // CHUNK
QUAD = 4
QUADS = H // QUAD
PAIRS = H // 2
SLOT = 64
MCOL = 48
FFN, EXPERTS = 512, 8
NE = EXPERTS + 1
FC = FFN // P
SCALE = DH ** -0.5
MASKED = -1e30
UNIT = 1024
LEAD = 21
NQ = 4
Q_PARTS = (0, 0, 1, 1, 0, 2)
K_PARTS = (0, 1, 0, 1, 2, 0)
E1 = DH + 1


def attention_schedule(causal):
    keys = [CT * (b + 1) if causal else TILES for b in range(NQ)]
    start = [sum(keys[:b]) for b in range(NQ + 1)]
    steps = start[NQ]
    units = []
    for b in range(NQ):
        for tt in range(CT):
            seen = (CT * b + tt + 1) * P if causal else T
            for part in range(-(-seen // UNIT)):
                for h in range(QUAD):
                    width = min(UNIT, seen - UNIT * part)
                    units.append((b, tt, h, part, width, causal and UNIT * part + width == seen))
    assert len(units) % 2 == 0
    work = [u[4] for u in units]
    place = [sum(work[:k]) * steps // sum(work) for k in range(len(units))]
    first = [next(i for i, u in enumerate(units) if u[0] == b) for b in range(NQ)]
    last = [max(i for i, u in enumerate(units) if u[0] == b) for b in range(NQ)]
    sched = []
    early = 5
    turn_q = [-24, -22, -16, -4] if causal else [start[b] - LEAD - early for b in range(NQ)]
    for s in range(-LEAD - early, steps):
        e = {"units": [], "jobs": [], "chain": []}
        for ahead in (0, 1):
            for k, u in enumerate(units):
                if ahead * steps + place[k] - LEAD == s:
                    e["units"].append((ahead, len(units) * ahead + k, *u))
                    if k == last[u[0]]:
                        e["chain"].append(e["units"][-1])
            for b in range(NQ):
                assert turn_q[b] < place[first[b]] - LEAD
                if s == ahead * steps + turn_q[b]:
                    e["jobs"].append(("qa", ahead, b))
                if s == ahead * steps + start[b] - (2 if causal else 4):
                    e["jobs"].append(("qb", ahead, b))
        for b in range(NQ - 1):
            if s == start[b + 1] + 2:
                e["jobs"].append(("ctx", 0, b))
        sched.append(e)
    return keys, start, steps, len(units), sched[:LEAD + early], sched[LEAD + early:]


def build(nc, x, a_wq, a_wk, a_wv, a_wo, l_wqkv, l_bqkv, l_wo, l_bo, ln1_g, ln1_b, f_wqkv, f_bqkv,
          f_wo, f_bo, ln2_g, ln2_b, gate_w, w1, b1, w2, b2, rw1, rb1, rw2, rb2, coef_w, coef_b, out):
    top = ExitStack()

    def sb(name, cols, dt=F32, parts=P):
        return top.enter_context(nc.sbuf_tensor(name, [parts, cols], dt))

    def sem(name):
        return top.enter_context(nc.semaphore(name))

    made = {}

    def phase_sems(phase, names):
        if phase in made:
            with nc.Block() as block:
                @block.sync
                def _(sp):
                    for h in made[phase].values():
                        sp.sem_clear(h)
        else:
            made[phase] = {n: sem(f"{phase}_{n}") for n in names}
        return made[phase]

    X = sb("X", T)
    U = sb("U", T)
    XH = sb("XH", T)
    QT = sb("QT", TILES * H * SLOT, BF16)
    KT = sb("KT", PAIRS * T, BF16)
    V = sb("V", T)
    AR = sb("AR", 19456)
    W2S = sb("W2S", NE * FC * D)
    IDF = sb("IDF", P)
    IDB = sb("IDB", P, BF16)
    MQK = sb("MQK", P, BF16)
    MKQ = sb("MKQ", P, BF16)
    UPTO = sb("UPTO", P)
    ONES = sb("ONES", P)
    MHALF = sb("MHALF", TILES)
    AW = sb("AW", 4 * D)
    LW = sb("LW", 4 * D)
    FW = sb("FW", 4 * D)
    LB = sb("LB", 4 * D)
    FB = sb("FB", 4 * D)
    GB = sb("GB", 4)
    GC = sb("GC", EXPERTS + 2)
    GCB = sb("GCB", EXPERTS + 2)
    RANK = sb("RANK", EXPERTS)
    B1T = sb("B1T", NE * FC)
    B2S = sb("B2S", D, F32, NE)
    ST6 = sb("ST6", CT * 6)
    MV = sb("MV", CT * 2)
    VE = sb("VE", CT)
    RSTD = sb("RSTD", CT)
    MX = sb("MX", NQ * CT * QUAD * 2)
    NM = sb("NM", 2 * CT * QUAD)
    RC = sb("RC", CT * QUAD)
    PS = top.enter_context(nc.psum_tensor("PS", [P, 8 * 512], F32))

    def bank(i, n=1):
        return PS[:, 512 * i:512 * (i + n)]

    def arena(at, cols, dt=F32):
        words = cols if dt == F32 else cols // 2
        v = AR[:, at:at + words]
        return v if dt == F32 else v.bitcast(dt)

    s_in, s_cst, s_wt, s_wtc = sem("inputs_loaded"), sem("constants_made"), sem("a_weights_turned"), sem("a_weights_kept")
    RAW = arena(0, 4 * D)
    B1R = arena(512, P)
    with nc.Block() as block:
        @block.sync
        def _(sp):
            n = 0
            loads = [(X[:, :].rearrange("p (t d) -> p t d", d=D), x.rearrange("b (t p) d -> p (b t) d", p=P))]
            loads += [(RAW[:, D * i:D * i + D], w) for i, w in enumerate((a_wq, a_wk, a_wv, a_wo))]
            loads += [(LW[:, 0:3 * D], l_wqkv), (LW[:, 3 * D:4 * D], l_wo), (FW[:, 0:3 * D], f_wqkv), (FW[:, 3 * D:4 * D], f_wo)]
            loads += [(LB[:, 0:3 * D], l_bqkv.partition_broadcast(P)), (LB[:, 3 * D:4 * D], l_bo.partition_broadcast(P))]
            loads += [(FB[:, 0:3 * D], f_bqkv.partition_broadcast(P)), (FB[:, 3 * D:4 * D], f_bo.partition_broadcast(P))]
            loads += [(GB[:, i:i + 1], v.rearrange("(p o) -> p o", o=1)) for i, v in enumerate((ln1_g, ln1_b, ln2_g, ln2_b))]
            loads += [(GC[:, 0:EXPERTS], gate_w), (GC[:, EXPERTS:EXPERTS + 2], coef_w),
                      (GCB[:, EXPERTS:EXPERTS + 2], coef_b.partition_broadcast(P))]
            loads += [(B1R[0:EXPERTS * FC, :], b1.rearrange("e (c f) -> (e c) f", f=P)),
                      (B1R[EXPERTS * FC:NE * FC, :], rb1.rearrange("(c f) -> c f", f=P))]
            loads += [(B2S[0:EXPERTS, :], b2), (B2S[EXPERTS:NE, :], rb2.rearrange("(o d) -> o d", o=1))]
            w2v = W2S[:, :].rearrange("p (e c d) -> p e c d", c=FC, d=D)
            loads += [(w2v[:, e, :, :], w2[e, :, :].rearrange("(c p) d -> p c d", p=P)) for e in range(EXPERTS)]
            loads += [(w2v[:, EXPERTS, :, :], rw2.rearrange("(c p) d -> p c d", p=P))]
            for dst, src in loads:
                sp.dma_start(dst, src).then_inc(s_in, 16)
                n += 16
            sp.wait_ge(s_in, n)

        n_loads = 1 + 4 + 4 + 4 + 4 + 3 + 2 + 2 + NE

        @block.gpsimd
        def _(pool):
            pool.memset(IDF[:, :], 0.0).then_inc(s_cst, 1)
            pool.memset(ONES[:, :], 1.0).then_inc(s_cst, 1)
            pool.memset(MQK[:, :], 0.0).then_inc(s_cst, 1)
            pool.memset(MKQ[:, :], 0.0).then_inc(s_cst, 1)
            pool.memset(MHALF[:, :], -0.5).then_inc(s_cst, 1)
            pool.memset(GCB[:, 0:EXPERTS], 0.0).then_inc(s_cst, 1)
            for e in range(EXPERTS):
                pool.memset(RANK[:, e:e + 1], float(EXPERTS - e)).then_inc(s_cst, 1)
            pool.wait_ge(s_cst, 6 + EXPERTS)
            pool.affine_select(out=IDF[:, :], in_=IDF[:, :], compare_op=ALU.not_equal, fill=1.0, base=0,
                               pattern=[[-1, P]], channel_multiplier=1).then_inc(s_cst, 1)
            pool.affine_select(out=MQK[:, :], in_=MQK[:, :], compare_op=ALU.is_ge, fill=MASKED, base=0,
                               pattern=[[-1, P]], channel_multiplier=1).then_inc(s_cst, 1)
            pool.affine_select(out=MKQ[:, :], in_=MKQ[:, :], compare_op=ALU.is_ge, fill=MASKED, base=0,
                               pattern=[[1, P]], channel_multiplier=-1).then_inc(s_cst, 1)
            pool.affine_select(out=UPTO[:, :], in_=ONES[:, :], compare_op=ALU.is_ge, fill=0.0, base=0,
                               pattern=[[1, P]], channel_multiplier=-1).then_inc(s_cst, 1)
            pool.wait_ge(s_cst, 10 + EXPERTS)
            pool.tensor_copy(IDB[:, :], IDF[:, :]).then_inc(s_cst, 1)

        @block.tensor
        def _(pe):
            pe.wait_ge(s_cst, 10 + EXPERTS)
            pe.wait_ge(s_in, 16 * n_loads)
            for i in range(4):
                pe.transpose(bank(0)[:, D * i:D * i + D], RAW[:, D * i:D * i + D], IDF[:, :])
            n = NE * FC
            pe.transpose(bank(1)[:, 0:n], B1R[0:n, :], IDF[0:n, 0:n]).then_inc(s_wt, 1)

        @block.scalar
        def _(act):
            act.wait_ge(s_wt, 1)
            act.copy(AW[:, :], bank(0)).then_inc(s_wtc, 1)
            act.copy(B1T[:, :], bank(1)[:, 0:NE * FC]).then_inc(s_wtc, 1)

        @block.vector
        def _(dve):
            dve.memset(QT[:, :].bitcast(F32), 0.0).then_inc(s_wtc, 1)

    def norm_dve(dve, s, c, j, n, src, dst):
        k = n * c + j
        if k:
            dve.wait_ge(s["xh"], CT * k)
        for i in range(CT):
            dve.bn_stats(ST6[:, 6 * i:6 * i + 6], src[:, bass.ds((CT * c + i) * P, P)]).then_inc(s["st"], 1)
        dve.wait_ge(s["st"], CT * k + CT)
        for i in range(CT):
            dve.bn_aggr(MV[:, 2 * i:2 * i + 2], ST6[:, 6 * i:6 * i + 6]).then_inc(s["mv"], 1)
        dve.wait_ge(s["mv"], CT * k + CT)
        dve.wait_ge(s["rstd"], k + 1)
        for i in range(CT):
            dve.tensor_scalar(dst[:, bass.ds((CT * c + i) * P, P)], src[:, bass.ds((CT * c + i) * P, P)],
                              MV[:, 2 * i:2 * i + 1], RSTD[:, i:i + 1], ALU.subtract, ALU.mult).then_inc(s["xh"], 1)

    def norm_pool(pool, s, k):
        pool.wait_ge(s["mv"], CT * k + CT)
        if k:
            pool.wait_ge(s["xh"], CT * k)
        pool.tensor_scalar(VE[:, :], MV[:, :].rearrange("p (t two) -> p t two", two=2)[:, :, 1], 1e-5, None,
                           ALU.add).then_inc(s["ve"], 1)
        pool.wait_ge(s["ve"], k + 1)
        pool.tensor_tensor(RSTD[:, :], VE[:, :], MHALF[:, 0:CT], ALU.pow).then_inc(s["rstd"], 1)

    def prepare(kind):
        s = phase_sems("prepare", ("st", "mv", "ve", "rstd", "xh", "turned", "xt", "qkv", "qk", "v",
                                            "a0", "r1", "a1", "a2", "tok", "ktp", "kte", "e", "ones", "bias"))
        W = {"a": AW, "f": FW, "l": LW}[kind]
        B = {"a": None, "f": FB, "l": LB}[kind]
        norms = 2 if kind == "f" else 1
        KTOK = [arena(4096 * p // 2 * 1, 4096, BF16) for p in range(2)]
        QK = [arena(4096 + 1024 * p, 1024) for p in range(2)]
        R1 = [arena(6144 + 1024 * p, 1024) for p in range(2)]
        A = [[arena(8192 + 512 * (3 * p + i), 1024, BF16) for i in range(3)] for p in range(2)]
        XT = [arena(11264 + 512 * p, 512) for p in range(2)]
        TB = [bank(0), bank(1)]
        G = [bank(2, 3), bank(5, 3)]
        QF = KT[:, :].bitcast(F32)
        V1 = QT[:, :].bitcast(F32)

        with nc.Block() as block:
            @block.gpsimd
            def _(pool):
                for k in range(norms * CHUNKS):
                    norm_pool(pool, s, k)
                if kind == "f":
                    pool.wait_ge(s["xh"], CT * norms * CHUNKS)
                    pool.tensor_tensor(U[:, :].rearrange("p (t d) -> p t d", d=D), U[:, :].rearrange("p (t d) -> p t d", d=D),
                                       B[:, 3 * D:4 * D].unsqueeze(1).to_broadcast([P, TILES, D]), ALU.add).then_inc(s["bias"], 1)
                if kind == "l":
                    pool.wait_ge(s["xh"], CT * norms * CHUNKS)
                    pool.tensor_tensor(X[:, :].rearrange("p (t d) -> p t d", d=D), X[:, :].rearrange("p (t d) -> p t d", d=D),
                                       B[:, 3 * D:4 * D].unsqueeze(1).to_broadcast([P, TILES, D]), ALU.add).then_inc(s["bias"], 1)
                    return
                for c in range(CHUNKS):
                    p = c % 2
                    pool.wait_ge(s["a0"], c + 1)
                    pool.wait_ge(s["qk"], c + 1)
                    pool.tensor_tensor(R1[p], QK[p], A[p][0], ALU.subtract).then_inc(s["r1"], 1)
                    pool.wait_ge(s["a1"], c + 1)
                    pool.tensor_tensor(A[p][2], R1[p], A[p][1], ALU.subtract).then_inc(s["a2"], 1)

            @block.vector
            def _(dve):
                for c in range(CHUNKS):
                    if kind == "f":
                        norm_dve(dve, s, c, 0, 2, X, U)
                        norm_dve(dve, s, c, 1, 2, U, XH)
                    else:
                        norm_dve(dve, s, c, 0, 1, X, XH)
                if kind == "l":
                    dve.memset(V1[:, 0:TILES * H * E1], 1.0).then_inc(s["ones"], 1)
                    dve.wait_ge(s["ones"], 1)
                else:
                    for p in range(2):
                        kp = KTOK[p].rearrange("p (n s) -> p n s", s=SLOT)
                        dve.memset(kp[:, :, MCOL:MCOL + 3], 1.0).then_inc(s["ones"], 1)
                        dve.memset(kp[:, :, MCOL + 3:SLOT], 0.0).then_inc(s["ones"], 1)
                for c in range(CHUNKS):
                    p = c % 2
                    src = G[p][:, 0:1024].rearrange("p (i q d) -> p i q d", i=CT, d=D)
                    dst = QK[p].rearrange("p (q i d) -> p i q d", i=CT, d=D)
                    vsrc = G[p][:, 1024:1536]
                    dve.wait_ge(s["qkv"], c + 1)
                    if kind != "l" and c >= 2:
                        dve.wait_ge(s["a0"], c - 1)
                        dve.wait_ge(s["r1"], c - 1)
                    if kind == "l":
                        vdst = V1[:, c * CT * H * E1:(c + 1) * CT * H * E1].rearrange("p (n e) -> p n e", e=E1)[:, :, 0:DH]
                    else:
                        vdst = V[:, c * CHUNK:(c + 1) * CHUNK]
                    if B is None:
                        dve.tensor_copy(dst, src).then_inc(s["qk"], 1)
                        dve.tensor_copy(vdst, vsrc).then_inc(s["v"], 1)
                    else:
                        for i in range(CT):
                            ins = dve.tensor_tensor(dst[:, i], src[:, i], B[:, 0:2 * D].rearrange("p (q d) -> p q d", d=D), ALU.add)
                        ins.then_inc(s["qk"], 1)
                        if kind == "l":
                            for i in range(CT):
                                ins = dve.tensor_tensor(vdst[:, H * i:H * i + H, :],
                                                        vsrc[:, D * i:D * i + D].rearrange("p (h d) -> p h d", d=DH),
                                                        B[:, 2 * D:3 * D].rearrange("p (h d) -> p h d", d=DH), ALU.add)
                        else:
                            ins = dve.tensor_tensor(vdst.rearrange("p (i d) -> p i d", d=D), vsrc.rearrange("p (i d) -> p i d", d=D),
                                                    B[:, 2 * D:3 * D].unsqueeze(1).to_broadcast([P, CT, D]), ALU.add)
                        ins.then_inc(s["v"], 1)
                    if kind == "l":
                        dve.wait_ge(s["qk"], c + 1)
                        dve.tensor_scalar(R1[p], QK[p], 0.0, None, ALU.min).then_inc(s["r1"], 1)
                        dve.wait_ge(s["e"], c + 1)
                        fdst = QF[:, 2 * c * CHUNK:2 * (c + 1) * CHUNK]
                        dve.scalar_tensor_tensor(out=fdst, in0=QK[p], scalar=0.0, in1=A1F[p], op0=ALU.max,
                                                 op1=ALU.add).then_inc(s["tok"], 1)
                        continue
                    qd = QT[:, c * CT * H * SLOT:(c + 1) * CT * H * SLOT].rearrange("p (n s) -> p n s", s=SLOT)
                    kd = KTOK[p].rearrange("p (n s) -> p n s", s=SLOT)
                    dve.wait_ge(s["a2"], c + 1)
                    if c >= 2:
                        dve.wait_ge(s["ktp"], CT * (c - 1))
                    for slot in range(6):
                        for half, (dd, parts) in enumerate(((qd, Q_PARTS), (kd, K_PARTS))):
                            a = A[p][parts[slot]][:, CHUNK * half:CHUNK * half + CHUNK].rearrange("p (n d) -> p n d", d=DH)
                            ins = dve.tensor_copy(dd[:, :, DH * slot:DH * slot + DH], a)
                    ins.then_inc(s["tok"], 1)

            @block.tensor
            def _(pe):
                def turn(c):
                    p = c % 2
                    pe.wait_ge(s["xh"], norms * CT * (c + 1))
                    if c >= 2:
                        pe.wait_ge(s["xt"], c - 1)
                    for i in range(CT):
                        ins = pe.transpose(TB[p][:, P * i:P * i + P], XH[:, (CT * c + i) * P:(CT * c + i + 1) * P], IDF[:, :])
                    ins.then_inc(s["turned"], 1)

                def project(c):
                    p = c % 2
                    pe.wait_ge(s["xt"], c + 1)
                    if c >= 2:
                        if kind == "l":
                            pe.wait_ge(s["v"], c - 1)
                        else:
                            pe.wait_ge(s["kte"], CT * (c - 1))
                    for i in range(CT):
                        lhs = XT[p][:, P * i:P * i + P]
                        pe.matmul(G[p][:, 256 * i:256 * i + 256], lhs, W[:, 0:2 * D], start=True, stop=True)
                        ins = pe.matmul(G[p][:, 1024 + P * i:1024 + P * i + P], lhs, W[:, 2 * D:3 * D], start=True, stop=True)
                    ins.then_inc(s["qkv"], 1)

                def turn_k(c):
                    p = c % 2
                    pe.wait_ge(s["tok"], c + 1)
                    if c < 2:
                        pe.wait_ge(s["ones"], 4 if kind == "a" else 4)
                    for i in range(CT):
                        if i == 3:
                            pe.wait_ge(s["kte"], CT * c + 1)
                        dst = G[p][:, 512 * (i % 3):512 * (i % 3) + 512].bitcast(BF16)
                        for j in range(PAIRS):
                            ins = pe.transpose(dst[:, P * j:P * j + P],
                                               KTOK[p][:, (i * PAIRS + j) * P:(i * PAIRS + j + 1) * P], IDB[:, :])
                        ins.then_inc(s["ktp"], 1)

                turn(0)
                turn(1)
                project(0)
                project(1)
                for c in range(CHUNKS):
                    if c + 2 < CHUNKS:
                        turn(c + 2)
                    if kind != "l":
                        turn_k(c)
                    if c + 2 < CHUNKS:
                        project(c + 2)

            @block.scalar
            def _(act):
                def take_xt(c):
                    p = c % 2
                    act.wait_ge(s["turned"], c + 1)
                    if c >= 2:
                        act.wait_ge(s["qkv"], c - 1)
                    if kind == "f":
                        ins = act.activation(XT[p], TB[p], ACT.Identity, bias=GB[:, 1:2], scale=GB[:, 0:1])
                    else:
                        ins = act.copy(XT[p], TB[p])
                    ins.then_inc(s["xt"], 1)

                take_xt(0)
                take_xt(1)
                for c in range(CHUNKS):
                    p = c % 2
                    if kind == "l":
                        act.wait_ge(s["r1"], c + 1)
                        act.activation(A1F[p], R1[p], ACT.Exp).then_inc(s["e"], 1)
                        if c + 2 < CHUNKS:
                            take_xt(c + 2)
                        continue
                    act.wait_ge(s["qk"], c + 1)
                    if c >= 2:
                        act.wait_ge(s["tok"], c - 1)
                    act.copy(A[p][0], QK[p]).then_inc(s["a0"], 1)
                    if c + 2 < CHUNKS:
                        take_xt(c + 2)
                    act.wait_ge(s["r1"], c + 1)
                    act.copy(A[p][1], R1[p]).then_inc(s["a1"], 1)
                    for i in range(CT):
                        act.wait_ge(s["ktp"], CT * c + i + 1)
                        tile = CT * c + i
                        src = G[p][:, 512 * (i % 3):512 * (i % 3) + 512].bitcast(BF16).rearrange("p (j t) -> p j t", t=P)
                        act.copy(KT[:, :].rearrange("p (j t) -> p j t", t=T)[:, :, P * tile:P * tile + P], src).then_inc(s["kte"], 1)

    A1F = [arena(8192 + 1024 * p, 1024) for p in range(2)]

    def attention(causal):
        s = phase_sems("attention", ("staged", "qa", "qae", "qb", "qbe", "score", "max", "part", "minus",
                                            "qk", "exp", "pv", "acc", "ctx", "ctxe", "rcp", "done", "kc", "kn", "vc", "vset", "qset"))
        keys, start, steps, per_quad, lead_in, body = attention_schedule(causal)
        block_of = [b for b in range(NQ) for _ in range(keys[b])]
        PR = [arena(2048 * i, 2048) for i in range(2)]
        QM = [arena(4096 + 512 * b, 1024, BF16) for b in range(NQ)]
        QA = [arena(6144 + 1024 * b, QUAD * CHUNK, BF16) for b in range(NQ)]
        QB = [arena(10240 + 1024 * i, QUAD * CHUNK, BF16) for i in range(2)]
        CTX = arena(12288, 512)
        CN = arena(12800, 512)
        KC = arena(13312, 2 * T, BF16)
        KN = arena(15360, 2 * T, BF16)
        VC = arena(17408, TILES * QUAD * 32)
        parts = [-(-(CT * (b + 1) * P if causal else T) // UNIT) for b in range(NQ)]
        MB = [bank(0, 2), bank(2, 2)]
        SB = [bank(4), bank(5)]
        ACC, MISC = bank(6), bank(7)
        kv = lambda k: k.rearrange("p (j t) -> p j t", t=T)
        vc = VC.rearrange("p (t h e) -> p t h e", h=QUAD, e=32)
        lead_units = sum(len(e["units"]) for e in lead_in)
        before = {k: sum(j[0] == k for e in lead_in for j in e["jobs"]) for k in ("qa", "qb", "ctx")}
        EV = {"qa": "qae", "qb": "qbe", "ctx": "ctxe"}

        primed = ("pv", "ctx", "exp", "acc", "ctxe", "done")

        def wait(e, name, n):
            n = n + 1 if name in primed else n
            if not isinstance(n, int) or n > 0:
                e.wait_ge(s[name], n)

        def pe_unit(pe, g, ahead, u, b, tt, h, part, width, diagonal, in_next, only=None):
            n = per_quad * g + u
            if not only and (not isinstance(n, int) or n >= 2):
                wait(pe, "max", n - 1)
            if not only and tt == 0 and h == 0 and part == 0:
                wait(pe, "qae", NQ * (g + ahead) + b + 1)
                if in_next:
                    wait(pe, "kn", 16 * (g + 1))
            q = QA[b][:, CHUNK * h + P * tt:CHUNK * h + P * tt + P]
            for a in range(0, width, CHUNK) if only is None else (CHUNK * only,):
                w = min(CHUNK, width - a)
                k = kv(KN if in_next else KC)[:, h // 2, UNIT * part + a:UNIT * part + a + w]
                dst = MB[u % 2][:, a:a + w]
                masked = diagonal and a + w == width
                ins = pe.matmul(dst, q, k, start=True, stop=not masked)
                if masked:
                    ins = pe.matmul(dst[:, w - P:w], IDB[:, :], MQK[:, :], start=False, stop=True)
            if a + w == width:
                ins.then_inc(s["score"], 1)

        def pe_scores(pe, g, st, h):
            n = steps * g + st
            b = block_of[st]
            kt = st - start[b]
            lo = max(0, kt - CT * b) * P if causal else 0
            wait(pe, "exp", 4 * n + (h - 1 if st else max(h - 1, 0)))
            if kt == 0 and h == 0:
                wait(pe, "qbe", NQ * g + b + 1)
            q = QB[b % 2][:, CHUNK * h + lo:CHUNK * h + CHUNK]
            k = kv(KC)[:, h // 2, P * kt:P * kt + P]
            dst = SB[h % 2]
            diagonal = causal and kt >= CT * b
            ins = pe.matmul(dst[:, lo:CHUNK], k, q, start=True, stop=not diagonal)
            if diagonal:
                ins = pe.matmul(dst[:, lo:lo + P], IDB[:, :], MKQ[:, :], start=False, stop=True)
            ins.then_inc(s["qk"], 1)

        def pe_values(pe, g, st):
            n = steps * g + st
            b = block_of[st]
            kt = st - start[b]
            lo = max(0, kt - CT * b) * P if causal else 0
            wait(pe, "exp", 4 * n + 4)
            if kt == 0:
                wait(pe, "acc", NQ * g + b)
            if st == 0:
                wait(pe, "vc", g + 1)
            pr = PR[st % 2].rearrange("p (h t) -> p h t", t=CHUNK)
            for h in range(QUAD):
                ins = pe.matmul(ACC[32 * h:32 * h + 32, lo:CHUNK], vc[:, kt, h, :], pr[:, h, lo:CHUNK],
                                start=kt == 0, stop=kt == keys[b] - 1)
            ins.then_inc(s["pv"], 1)

        def pe_job(pe, g, kind, ahead, b, seen):
            for k in ("qa", "qb", "ctx"):
                wait(pe, EV[k], seen[k](g))
            nb = NQ * (g + ahead) + b
            if kind == "ctx":
                wait(pe, "acc", nb + 1)
                for i in range(CT):
                    ins = pe.transpose(MISC[:, P * i:P * i + P], CTX[:, P * i:P * i + P], IDF[:, :])
            else:
                pe.wait_ge(s["staged" if kind == "qa" else "minus"], nb + 1)
                q = QM[b].rearrange("p (t j r) -> p t j r", j=2, r=P)
                dst = MISC.bitcast(BF16).rearrange("p (j t) -> p j t", t=CHUNK)
                for j in range(2):
                    for i in range(CT):
                        ins = pe.transpose(dst[:, j, P * i:P * i + P], q[:, i, j, :], IDB[:, :])
            ins.then_inc(s[kind], 1)

        def seen_before(entries, base, per):
            out, n = [], dict(base)
            for e in entries:
                row = []
                for job in e["jobs"]:
                    row.append({k: (lambda g, a=n[k], m=per[k]: a + m * g) for k in n})
                    n[job[0]] += 1
                out.append(row)
            return out, n

        zero = {"qa": 0, "qb": 0, "ctx": 0}
        seen_lead, _ = seen_before(lead_in, zero, zero)
        per = {"qa": NQ, "qb": NQ, "ctx": NQ}
        seen_body, seen_end = seen_before(body, before, per)

        def in_quad(e, last):
            keep = lambda x: not (last and x[0])
            return [u for u in e["units"] if keep(u)], [j for j in e["jobs"] if not (last and j[1])]

        def pe_products(pe, g, list_):
            for u, i in list_:
                pe_unit(pe, g, *u, in_next=u[0] == 1, only=i)

        def pe_body(pe, g, last):
            kept = []
            pe.wait_ge(s["kc"], g + 1)
            for st, e in enumerate(body):
                units, jobs = in_quad(e, last)
                for k, job in enumerate(e["jobs"]):
                    if job in jobs:
                        seen = seen_body[st][k]
                        if last:
                            gone = {q: sum(j[0] == q and j[1] for ee in body[:st] for j in ee["jobs"])
                                    + sum(j[0] == q and j[1] for j in e["jobs"][:k]) for q in zero}
                            seen = {q: (lambda g, f=seen[q], m=gone[q]: f(g) - m) for q in zero}
                        pe_job(pe, g, *job, seen)
                fresh = [(u, i) for u in units for i in range(-(-u[6] // CHUNK))]
                n = len(fresh) // 4
                pe_scores(pe, g, st, 0)
                pe_products(pe, g, kept)
                pe_scores(pe, g, st, 1)
                if st:
                    pe_values(pe, g, st - 1)
                pe_scores(pe, g, st, 2)
                pe_products(pe, g, fresh[:n])
                pe_scores(pe, g, st, 3)
                kept = fresh[len(fresh) - n:] if st + 1 < steps else []
                pe_products(pe, g, fresh[n:len(fresh) - len(kept)])
            pe_values(pe, g, steps - 1)
            seen = dict(seen_end)
            if last:
                for q in zero:
                    seen[q] -= sum(j[0] == q and j[1] for ee in body for j in ee["jobs"])
            pe_job(pe, g, "ctx", 0, NQ - 1, {q: (lambda g, a=seen[q], m=per[q]: a + m * g) for q in zero})

        def dve_unit(dve, g, ahead, u, b, tt, h, part, width, diagonal):
            wait(dve, "score", per_quad * g + u + 1)
            at = ((b * CT + tt) * QUAD + h) * 2 + part
            dve.tensor_reduce(MX[:, at:at + 1], MB[u % 2][:, 0:width], AX.X, ALU.max).then_inc(s["max"], 1)

        def dve_chain(dve, g, ahead, b, u_end):
            nb = NQ * (g + ahead) + b
            mx = MX[:, b * CT * QUAD * 2:(b + 1) * CT * QUAD * 2].rearrange("p (n c) -> p n c", c=2)
            q = QM[b].rearrange("p (n s) -> p n s", s=SLOT)
            n_part = 4 * nb
            dve.wait_ge(s["max"], u_end)
            dve.wait_ge(s["qa"], nb + 1)
            dve.tensor_reduce(NM[:, 0:16], mx[:, :, 0:parts[b]], AX.X, ALU.max,
                              negate=True).then_inc(s["part"], 1)
            dve.wait_ge(s["part"], n_part + 1)
            dve.tensor_copy(q[:, :, MCOL], NM[:, 0:16]).then_inc(s["part"], 1)
            dve.wait_ge(s["part"], n_part + 2)
            dve.tensor_tensor(NM[:, 16:32], NM[:, 0:16], q[:, :, MCOL], ALU.subtract).then_inc(s["part"], 1)
            dve.wait_ge(s["part"], n_part + 3)
            dve.tensor_copy(q[:, :, MCOL + 1], NM[:, 16:32]).then_inc(s["part"], 1)
            dve.wait_ge(s["part"], n_part + 4)
            dve.tensor_tensor(q[:, :, MCOL + 2], NM[:, 16:32], q[:, :, MCOL + 1], ALU.subtract).then_inc(s["minus"], 1)

        def dve_sums(dve, g, b):
            nb = NQ * g + b
            wait(dve, "ctxe", nb + 1)
            wait(dve, "done", nb)
            cn = CN.rearrange("p (n e) -> p n e", e=32)
            dve.reciprocal(RC[:, :], cn[:, :, DH]).then_inc(s["rcp"], 1)

        def dve_copy_k(dve, g):
            dve.wait_ge(s["kn"], 16 * (g + 1))
            wait(dve, "qk", 4 * steps * (g + 1))
            dve.tensor_copy(KC, KN).then_inc(s["kc"], 1)

        def dve_copy_v(dve, g):
            if not isinstance(g, int) or g >= 0:
                wait(dve, "pv", steps * (g + 1))
            v = V[:, :].rearrange("p (t d) -> p t d", d=D)
            q = (g + 1) * QUAD * DH
            v = v[:, :, bass.ds(q, QUAD * DH)] if not isinstance(q, int) else v[:, :, q:q + QUAD * DH]
            dve.tensor_copy(vc[:, :, :, 0:DH], v.rearrange("p t (h d) -> p t h d", d=DH)).then_inc(s["vc"], 1)

        def dve_body(dve, g, last):
            for st, e in enumerate(body):
                units, _ = in_quad(e, last)
                for u in units:
                    dve_unit(dve, g, *u)
                    if u in e["chain"]:
                        dve_chain(dve, g, u[0], u[2], per_quad * g + u[1] + 1)
                for b in range(NQ - 1):
                    if st == start[b + 1] + 3:
                        dve_sums(dve, g, b)
            if not last:
                dve_copy_k(dve, g)
                dve_copy_v(dve, g)
            dve_sums(dve, g, NQ - 1)

        def act_exp(act, g, st, h):
            n = steps * g + st
            b = block_of[st]
            lo = max(0, st - start[b] - CT * b) * P if causal else 0
            wait(act, "qk", 4 * n + h + 1)
            if h == 0:
                wait(act, "pv", steps * g + max(st - 1, 0))
            dst = PR[st % 2].rearrange("p (h t) -> p h t", t=CHUNK)[:, h, lo:CHUNK]
            act.activation(dst, SB[h % 2][:, lo:CHUNK], ACT.Exp, scale=SCALE).then_inc(s["exp"], 1)

        def act_sums(act, g, b):
            nb = NQ * g + b
            wait(act, "pv", steps * g + start[b + 1])
            wait(act, "ctx", nb)
            act.copy(CTX, ACC).then_inc(s["acc"], 1)

        def act_job(act, g, kind, ahead, b, pieces=range(4)):
            nb = NQ * (g + ahead) + b
            if 0 in pieces:
                wait(act, kind, nb + 1)
            if kind == "ctx":
                wait(act, "done", nb)
                act.copy(CN, MISC).then_inc(s["ctxe"], 1)
                return
            src = MISC.bitcast(BF16).rearrange("p (j t) -> p j t", t=CHUNK)
            dst = (QA[b] if kind == "qa" else QB[b % 2]).rearrange("p (j i t) -> p j i t", i=2, t=CHUNK)
            for k in pieces:
                j, half = divmod(k, 2)
                r = slice(SLOT * half, SLOT * half + SLOT)
                ins = act.copy(dst[r, j, half, :], src[r, j])
            if 3 in pieces:
                ins.then_inc(s[EV[kind]], 1)

        readout = {}
        for st, e in enumerate(body):
            for job in e["jobs"]:
                for k in range(1 if job[0] == "ctx" else 4):
                    at = (st + k // 2, 2 * (k % 2)) if causal else (st + k, 0)
                    readout.setdefault(at, []).append((job, range(4) if job[0] == "ctx" else [k]))

        def act_body(act, g, last):
            for st in range(steps):
                if st - 1 in start[1:NQ]:
                    act_sums(act, g, start.index(st - 1) - 1)
                for h in range(QUAD):
                    for job, pieces in readout.get((st, h), []):
                        if not (last and job[1]):
                            act_job(act, g, *job, pieces)
                    act_exp(act, g, st, h)
            act_sums(act, g, NQ - 1)
            act_job(act, g, "ctx", 0, NQ - 1)

        def pool_stage(pool, g, b):
            nb = NQ * g + b
            wait(pool, "qb", nb - NQ + 1) if not isinstance(nb, int) or nb >= NQ else None
            q = QT[:, :].rearrange("p (t r) -> p t r", r=H * SLOT)
            at = g * QUAD * SLOT
            sl = slice(at, at + QUAD * SLOT) if isinstance(at, int) else bass.ds(at, QUAD * SLOT)
            pool.tensor_copy(QM[b].rearrange("p (t r) -> p t r", r=QUAD * SLOT), q[:, CT * b:CT * b + CT, sl]).then_inc(s["staged"], 1)

        def pool_context(pool, g, b):
            pool.wait_ge(s["rcp"], NQ * g + b + 1)
            cn = CN.rearrange("p (t h e) -> p t h e", h=QUAD, e=32)[:, :, :, 0:DH]
            at = g * QUAD * DH
            sl = slice(at, at + QUAD * DH) if isinstance(at, int) else bass.ds(at, QUAD * DH)
            dst = XH[:, :].rearrange("p (t d) -> p t d", d=D)[:, CT * b:CT * b + CT, sl].rearrange("p t (h d) -> p t h d", d=DH)
            rc = RC[:, :].rearrange("p (t h) -> p t h", h=QUAD).unsqueeze(3).to_broadcast([P, CT, QUAD, DH])
            pool.tensor_tensor(dst, cn, rc, ALU.mult).then_inc(s["done"], 1)

        with nc.Block() as block:
            @block.sync
            def _(sp):
                sp.dma_start(kv(KN), kv(KT[:, :])[:, 2:4, :]).then_inc(s["kn"], 16)
                with sp.Fori(0, QUADS - 2) as g:
                    sp.wait_ge(s["kc"], g + 2)
                    sp.wait_ge(s["score"], per_quad * (g + 1) + lead_units)
                    sp.dma_start(kv(KN), kv(KT[:, :])[:, bass.ds(2 * g + 4, 2), :]).then_inc(s["kn"], 16)

            @block.gpsimd
            def _(pool):
                pool.sem_inc(s["done"], 1)
                for b in range(NQ):
                    pool_stage(pool, 0, b)
                with pool.Fori(0, QUADS - 1) as g:
                    for b in range(NQ):
                        pool_stage(pool, g + 1, b)
                        pool_context(pool, g, b)
                for b in range(NQ):
                    pool_context(pool, QUADS - 1, b)

            @block.vector
            def _(dve):
                dve.tensor_copy(kv(KC), kv(KT[:, :])[:, 0:2, :]).then_inc(s["kc"], 1)
                for i, q in enumerate((*QA, *QB)):
                    qp = q.bitcast(F32).rearrange("p (j i t) -> p j i t", i=2, t=CHUNK // 2)
                    dve.memset(qp[0:SLOT, :, 1, :], 0.0)
                    dve.memset(qp[SLOT:P, :, 0, :], 0.0).then_inc(s["qset"], 1)
                dve.memset(VC, 0.0).then_inc(s["vset"], 1)
                dve.wait_ge(s["vset"], 1)
                dve.memset(vc[:, :, :, DH:DH + 1], 1.0).then_inc(s["vset"], 1)
                dve_copy_v(dve, -1)
                for e in lead_in:
                    for u in e["units"]:
                        dve_unit(dve, 0, *u)
                        if u in e["chain"]:
                            dve_chain(dve, 0, u[0], u[2], u[1] + 1)
                with dve.Fori(0, QUADS - 1) as g:
                    dve_body(dve, g, False)
                dve_body(dve, QUADS - 1, True)

            @block.scalar
            def _(act):
                for name in ("exp", "acc", "ctxe"):
                    act.sem_inc(s[name], 1)
                for e in lead_in:
                    for job in e["jobs"]:
                        act_job(act, 0, *job)
                with act.Fori(0, QUADS - 1) as g:
                    act_body(act, g, False)
                act_body(act, QUADS - 1, True)

            @block.tensor
            def _(pe):
                for name in ("pv", "ctx"):
                    pe.sem_inc(s[name], 1)
                pe.wait_ge(s["kc"], 1)
                pe.wait_ge(s["qset"], NQ + 2)
                for st, e in enumerate(lead_in):
                    for k, job in enumerate(e["jobs"]):
                        pe_job(pe, 0, *job, seen_lead[st][k])
                    for u in e["units"]:
                        pe_unit(pe, 0, *u, in_next=False)
                pe.wait_ge(s["vset"], 2)
                with pe.Fori(0, QUADS - 1) as g:
                    pe_body(pe, g, False)
                pe_body(pe, QUADS - 1, True)

    def project_out(W, dst_of, res):
        s = phase_sems("project", ("t", "te", "o", "oe"))
        CTT = [arena(512 * p, 512) for p in range(2)]
        with nc.Block() as block:
            @block.tensor
            def _(pe):
                def turn(c):
                    if c >= 2:
                        pe.wait_ge(s["te"], c - 1)
                    for i in range(CT):
                        ins = pe.transpose(bank(c % 2)[:, P * i:P * i + P], XH[:, (CT * c + i) * P:(CT * c + i + 1) * P], IDF[:, :])
                    ins.then_inc(s["t"], 1)

                turn(0)
                for c in range(CHUNKS):
                    if c + 1 < CHUNKS:
                        turn(c + 1)
                    pe.wait_ge(s["te"], c + 1)
                    if c >= 2:
                        pe.wait_ge(s["oe"], c - 1)
                    for i in range(CT):
                        ins = pe.matmul(bank(2 + c % 2)[:, P * i:P * i + P], CTT[c % 2][:, P * i:P * i + P], W, start=True, stop=True)
                    ins.then_inc(s["o"], 1)

            @block.scalar
            def _(act):
                for c in range(CHUNKS):
                    act.wait_ge(s["t"], c + 1)
                    if c >= 2:
                        act.wait_ge(s["o"], c - 1)
                    act.copy(CTT[c % 2], bank(c % 2)).then_inc(s["te"], 1)

            @block.vector
            def _(dve):
                for c in range(CHUNKS):
                    dve.wait_ge(s["o"], c + 1)
                    a = slice(CHUNK * c, CHUNK * c + CHUNK)
                    dve.tensor_tensor(dst_of[:, a], bank(2 + c % 2), res[:, a], ALU.add).then_inc(s["oe"], 1)

    def experts():
        s = phase_sems("experts", ("w", "st", "mv", "ve", "rstd", "xh", "t", "xt", "lg", "r", "ex", "sw",
                                            "stt", "sts", "b2", "h", "gelu", "y", "acc", "xx"))
        W1S = QT[:, :].bitcast(F32)
        W1R = arena(0, FFN)
        XTT = KT[:, :].bitcast(F32)[:, 0:T]
        HT = [KT[:, :].bitcast(F32)[:, T + 2048 * i:T + 2048 * (i + 1)] for i in range(2)]
        L = arena(512, TILES * 10)
        EX = arena(768, TILES * 10)
        G1 = arena(1024, TILES * 8)
        R = arena(1280, 16 * TILES)
        SW = arena(2048, TILES * NE)
        SWT = arena(2304, T)

        def w1(e, f):
            if e == EXPERTS:
                return W1R[:, P * f:P * f + P]
            return W1S[:, FFN * e + P * f:FFN * e + P * f + P]

        def v3(a, n):
            return a.rearrange("p (t n) -> p t n", n=n)

        def col(a):
            return a.unsqueeze(2)

        with nc.Block() as block:
            @block.sync
            def _(sp):
                sp.dma_start(W1S.rearrange("p (e f) -> p e f", f=FFN)[:, 0:EXPERTS, :], w1_in.rearrange("e p f -> p e f")).then_inc(s["w"], 16)
                sp.dma_start(W1R, rw1).then_inc(s["w"], 16)

            @block.gpsimd
            def _(pool):
                for c in range(CHUNKS):
                    norm_pool(pool, s, c)
                pool.tensor_tensor(X[:, :], X[:, :], U[:, :], ALU.add).then_inc(s["xx"], 1)

            @block.vector
            def _(dve):
                for c in range(CHUNKS):
                    norm_dve(dve, s, c, 0, 1, U, XH)
                n = [0]

                def then(ins):
                    n[0] += 1
                    ins.then_inc(s["r"], 1)
                    dve.wait_ge(s["r"], n[0])

                r = lambda i: R[:, 16 * i:16 * i + 16]
                dve.wait_ge(s["lg"], TILES)
                then(dve.tensor_tensor(v3(L, 10), v3(bank(4)[:, 0:160], 10), GCB[:, :].unsqueeze(1).to_broadcast([P, TILES, 10]), ALU.add))
                dve.tensor_reduce(r(0), v3(L, 10)[:, :, 0:8], AX.X, ALU.max)
                then(dve.tensor_reduce(r(1), v3(L, 10)[:, :, 8:10], AX.X, ALU.max))
                dve.tensor_tensor(v3(EX, 10)[:, :, 0:8], v3(L, 10)[:, :, 0:8], col(r(0)).to_broadcast([P, TILES, 8]), ALU.subtract)
                then(dve.tensor_tensor(v3(EX, 10)[:, :, 8:10], v3(L, 10)[:, :, 8:10], col(r(1)).to_broadcast([P, TILES, 2]), ALU.subtract))
                then(dve.tensor_tensor(v3(G1, 8), v3(L, 10)[:, :, 0:8], col(r(0)).to_broadcast([P, TILES, 8]), ALU.is_equal))
                then(dve.tensor_tensor(v3(G1, 8), v3(G1, 8), RANK[:, :].unsqueeze(1).to_broadcast([P, TILES, 8]), ALU.mult))
                then(dve.tensor_reduce(r(2), v3(G1, 8), AX.X, ALU.max))
                then(dve.tensor_tensor(v3(G1, 8), v3(G1, 8), col(r(2)).to_broadcast([P, TILES, 8]), ALU.is_equal))
                dve.wait_ge(s["ex"], 1)
                dve.tensor_reduce(r(3), v3(EX, 10)[:, :, 0:8], AX.X, ALU.add)
                then(dve.tensor_reduce(r(4), v3(EX, 10)[:, :, 8:10], AX.X, ALU.add))
                dve.reciprocal(r(5), r(3))
                then(dve.reciprocal(r(6), r(4)))
                then(dve.tensor_tensor(r(7), r(5), r(6), ALU.mult))
                then(dve.tensor_tensor(r(8), r(7), v3(EX, 10)[:, :, 8], ALU.mult))
                dve.tensor_tensor(v3(SW, NE)[:, :, 0:8], v3(G1, 8), col(r(8)).to_broadcast([P, TILES, 8]), ALU.mult)
                dve.tensor_tensor(v3(SW, NE)[:, :, 8], r(6), v3(EX, 10)[:, :, 9], ALU.mult).then_inc(s["sw"], 1)
                dve.wait_ge(s["sw"], 1)
                dve.wait_ge(s["xx"], 1)
                for c in range(CHUNKS):
                    dve.wait_ge(s["b2"], c + 1)
                    a = slice(CHUNK * c, CHUNK * c + CHUNK)
                    dve.tensor_tensor(X[:, a], X[:, a], bank(6 + c % 2), ALU.add).then_inc(s["acc"], 1)
                with dve.Fori(0, CHUNKS) as c:
                    for e in range(NE):
                        k = NE * c + e
                        dve.wait_ge(s["y"], 1 + k + 1)
                        dve.wait_ge(s["acc"], CHUNKS + k)
                        for i in range(CT):
                            a = bass.ds((CT * c + i) * P, P)
                            ins = dve.scalar_tensor_tensor(out=X[:, a], in0=bank(6 + e % 2)[:, P * i:P * i + P],
                                                           scalar=SW[:, bass.ds((CT * c + i) * NE + e, 1)], in1=X[:, a],
                                                           op0=ALU.mult, op1=ALU.add)
                        ins.then_inc(s["acc"], 1)

            @block.scalar
            def _(act):
                act.sem_inc(s["gelu"], 1)
                for c in range(CHUNKS):
                    act.wait_ge(s["t"], c + 1)
                    act.activation(XTT[:, CHUNK * c:CHUNK * c + CHUNK], bank(c % 2), ACT.Identity, bias=GB[:, 3:4],
                                   scale=GB[:, 2:3]).then_inc(s["xt"], 1)
                act.wait_ge(s["r"], 3)
                act.activation(EX, EX, ACT.Exp).then_inc(s["ex"], 1)
                for c in range(CHUNKS):
                    act.wait_ge(s["stt"], c + 1)
                    act.copy(SWT[0:NE, CHUNK * c:CHUNK * c + CHUNK], bank(2 + c % 2)[0:NE, :]).then_inc(s["sts"], 1)
                with act.Fori(0, CHUNKS) as c:
                    for e in range(NE):
                        k = NE * c + e
                        act.wait_ge(s["y"], 1 + NE * c + max(e - 1, 0))
                        for f in range(FC):
                            act.wait_ge(s["h"], FC * k + f + 1)
                            act.activation(HT[e % 2][:, CHUNK * f:CHUNK * f + CHUNK], bank(2 + f), ACT.Gelu,
                                           bias=B1T[:, FC * e + f:FC * e + f + 1]).then_inc(s["gelu"], 1)

            @block.tensor
            def _(pe):
                pe.sem_inc(s["y"], 1)
                for c in range(CHUNKS):
                    pe.wait_ge(s["xh"], CT * (c + 1))
                    if c >= 2:
                        pe.wait_ge(s["xt"], c - 1)
                    for i in range(CT):
                        ins = pe.transpose(bank(c % 2)[:, P * i:P * i + P], XH[:, (CT * c + i) * P:(CT * c + i + 1) * P], IDF[:, :])
                    ins.then_inc(s["t"], 1)
                for t in range(TILES):
                    if t % CT == 0:
                        pe.wait_ge(s["xt"], t // CT + 1)
                    pe.matmul(bank(4)[:, 10 * t:10 * t + 10], XTT[:, P * t:P * t + P], GC[:, :], start=True, stop=True).then_inc(s["lg"], 1)
                pe.wait_ge(s["sw"], 1)
                for c in range(CHUNKS):
                    if c >= 2:
                        pe.wait_ge(s["sts"], c - 1)
                    for i in range(CT):
                        t = CT * c + i
                        ins = pe.transpose(bank(2 + c % 2)[0:NE, P * i:P * i + P], SW[:, NE * t:NE * t + NE], IDF[:, :])
                    ins.then_inc(s["stt"], 1)
                for c in range(CHUNKS):
                    pe.wait_ge(s["sts"], c + 1)
                    if c >= 2:
                        pe.wait_ge(s["acc"], c - 1)
                    for i in range(CT):
                        t = CT * c + i
                        ins = pe.matmul(bank(6 + c % 2)[:, P * i:P * i + P], SWT[0:NE, P * t:P * t + P], B2S[:, :], start=True, stop=True)
                    ins.then_inc(s["b2"], 1)
                pe.wait_ge(s["w"], 32)
                pe.wait_ge(s["acc"], CHUNKS)

                def second(c, e):
                    k = NE * c + e
                    pe.wait_ge(s["gelu"], 1 + FC * k + FC)
                    pe.wait_ge(s["acc"], CHUNKS + NE * c + max(e - 1, 0))
                    for i in range(CT):
                        for f in range(FC):
                            ins = pe.matmul(bank(6 + e % 2)[:, P * i:P * i + P], HT[e % 2][:, CHUNK * f + P * i:CHUNK * f + P * i + P],
                                            W2S[:, (FC * e + f) * D:(FC * e + f + 1) * D], start=f == 0, stop=f == FC - 1)
                    ins.then_inc(s["y"], 1)

                with pe.Fori(0, CHUNKS) as c:
                    for e in range(NE):
                        k = NE * c + e
                        for f in range(FC):
                            if e == 0:
                                pe.wait_ge(s["gelu"], 1 + FC * k)
                            else:
                                pe.wait_ge(s["gelu"], 1 + FC * (k - 1) + f + 1)
                            pe.matmul(bank(2 + f), w1(e, f), XTT[:, bass.ds(CHUNK * c, CHUNK)], start=True, stop=True).then_inc(s["h"], 1)
                        if e:
                            second(c, e - 1)
                    second(c, NE - 1)

    w1_in = w1

    def linear_attention():
        s = phase_sems("linear", ("kv", "ks", "c", "prod", "red", "eps", "rcp", "o"))
        N = H * E1 * DH
        QF = KT[:, :].bitcast(F32).rearrange("p (c q i d) -> p c q i d", q=2, i=CT, d=D)
        V1 = QT[:, :].bitcast(F32)[:, 0:TILES * H * E1]
        KV = [arena(1280 * i, N) for i in range(2)]
        KS = [arena(2560 + 1280 * i, N) for i in range(2)]
        PROD = arena(5120, N)
        RED = arena(6400, H * E1)
        DEN = arena(6656, H)
        RDEN = arena(6688, H)
        C = [PS[:, 2048 * i:2048 * i + N] for i in range(2)]

        def hed(a):
            return a.rearrange("p (h e d) -> p h e d", e=E1, d=DH)

        with nc.Block() as block:
            @block.gpsimd
            def _(pool):
                pool.memset(KS[0], 0.0).then_inc(s["ks"], 1)
                for t in range(TILES):
                    i = t % 2
                    k = QF[:, t // CT, 1, t % CT, :].rearrange("p (h d) -> p h d", d=DH).unsqueeze(2).to_broadcast([P, H, E1, DH])
                    v = V1[:, H * E1 * t:H * E1 * (t + 1)].rearrange("p (h e) -> p h e", e=E1).unsqueeze(3).to_broadcast([P, H, E1, DH])
                    if t >= 2:
                        pool.wait_ge(s["c"], t - 1)
                    pool.tensor_tensor(hed(KV[i]), k, v, ALU.mult).then_inc(s["kv"], 1)
                    if t + 1 < TILES:
                        pool.wait_ge(s["kv"], t + 1)
                        if t >= 1:
                            pool.wait_ge(s["c"], t)
                        pool.wait_ge(s["ks"], t + 1)
                        pool.tensor_tensor(KS[1 - i], KS[i], KV[i], ALU.add).then_inc(s["ks"], 1)

            @block.tensor
            def _(pe):
                for t in range(TILES):
                    i = t % 2
                    pe.wait_ge(s["kv"], t + 1)
                    pe.wait_ge(s["ks"], t + 1)
                    if t >= 2:
                        pe.wait_ge(s["prod"], t - 1)
                    for a in range(0, N, 512):
                        b = min(a + 512, N)
                        pe.matmul(C[i][:, a:b], UPTO[:, :], KV[i][:, a:b], start=True, stop=False)
                        ins = pe.matmul(C[i][:, a:b], ONES[:, :], KS[i][:, a:b], start=False, stop=True)
                    ins.then_inc(s["c"], 1)

            @block.vector
            def _(dve):
                for t in range(TILES):
                    i = t % 2
                    q = QF[:, t // CT, 0, t % CT, :].rearrange("p (h d) -> p h d", d=DH).unsqueeze(2).to_broadcast([P, H, E1, DH])
                    dve.wait_ge(s["c"], t + 1)
                    dve.tensor_tensor(hed(PROD), hed(C[i]), q, ALU.mult).then_inc(s["prod"], 1)
                    dve.wait_ge(s["prod"], t + 1)
                    dve.tensor_reduce(RED, PROD.rearrange("p (n d) -> p n d", d=DH), AX.X, ALU.add).then_inc(s["red"], 1)
                    dve.wait_ge(s["red"], t + 1)
                    red = RED.rearrange("p (h e) -> p h e", e=E1)
                    dve.tensor_scalar(DEN, red[:, :, DH], 1e-6, None, ALU.add).then_inc(s["eps"], 1)
                    dve.wait_ge(s["eps"], t + 1)
                    dve.reciprocal(RDEN, DEN).then_inc(s["rcp"], 1)
                    dve.wait_ge(s["rcp"], t + 1)
                    dve.tensor_tensor(XH[:, P * t:P * t + P].rearrange("p (h d) -> p h d", d=DH), red[:, :, 0:DH],
                                      RDEN.unsqueeze(2).to_broadcast([P, H, DH]), ALU.mult).then_inc(s["o"], 1)

    def ffn():
        prepare("f")
        attention(False)
        project_out(FW[:, 3 * D:4 * D], U, U)
        experts()

    def restore_padding(tag):
        done = sem(tag)
        with nc.Block() as block:
            @block.vector
            def _(dve):
                dve.memset(QT[:, :].bitcast(F32), 0.0).then_inc(done, 1)

    prepare("a")
    attention(True)
    project_out(AW[:, 3 * D:4 * D], X, X)
    ffn()
    prepare("l")
    linear_attention()
    project_out(LW[:, 3 * D:4 * D], X, X)
    restore_padding("zero_q")
    ffn()

    s_out = sem("output_stored")
    with nc.Block() as block:
        @block.sync
        def _(sp):
            sp.dma_start(out.rearrange("b (t p) d -> p (b t) d", p=P), X[:, :].rearrange("p (t d) -> p t d", d=D)).then_inc(s_out, 16)
            sp.wait_ge(s_out, 16)
    top.close()


_INS = ["L0_attn_a_x", "L0_attn_a_Wq", "L0_attn_a_Wk", "L0_attn_a_Wv", "L0_attn_a_Wo", "L0_attn_b_qkv_w",
        "L0_attn_b_qkv_b", "L0_attn_b_out_w", "L0_attn_b_out_b", "L0_ffn_ln1_g", "L0_ffn_ln1_b", "L0_ffn_Wqkv",
        "L0_ffn_bqkv", "L0_ffn_Wo", "L0_ffn_bo", "L0_ffn_ln2_g", "L0_ffn_ln2_b", "L0_ffn_gate_w", "L0_ffn_W1",
        "L0_ffn_b1", "L0_ffn_W2", "L0_ffn_b2", "L0_ffn_rW1", "L0_ffn_rb1", "L0_ffn_rW2", "L0_ffn_rb2",
        "L0_ffn_coef_w", "L0_ffn_coef_b"]


def kernel(**inputs):
    import numpy as _np
    import concourse.bacc as _bacc
    from concourse import mybir as _mybir
    from concourse.bass_utils import run_bass_kernel_spmd as _run

    nc = _bacc.Bacc("TRN2", target_bir_lowering=False, num_devices=1)
    arrays, args = {}, []
    for name in _INS:
        a = _np.ascontiguousarray(inputs[name])
        arrays[f"in_{name}_dram"] = a
        args.append(nc.dram_tensor(f"in_{name}_dram", a.shape, _mybir.dt.from_np(a.dtype), kind="ExternalInput").ap())
    args.append(nc.dram_tensor("out_dram", (1, T, D), F32, kind="ExternalOutput").ap())
    build(nc, *args)
    r = _run(nc, [arrays], core_ids=[0])
    return r.results[0]["out_dram"]
```

```python
from contextlib import ExitStack

import concourse.bass as bass
from concourse import mybir
from concourse.alu_op_type import AluOpType as ALU

F32, BF16 = mybir.dt.float32, mybir.dt.bfloat16
I32, U32 = mybir.dt.int32, mybir.dt.uint32
ACT = mybir.ActivationFunctionType
AX = mybir.AxisListType

P = 128
T, D, H, DH = 2048, 128, 16, 8
TILES = T // P
NG = 8
CHUNK = 512
CT = CHUNK // P
CHUNKS = T // CHUNK
QUAD = 4
QUADS = H // QUAD
PAIRS = H // 2
SLOT = 64
MCOL = 48
FFN, EXPERTS = 512, 8
NE = EXPERTS + 1
FC = FFN // P
RING = 3
SLOT_TILES = -(-(TILES + EXPERTS - 1) // RING) * RING
SCALE = DH ** -0.5
MASKED = -1e30
UNIT = 1024
LEAD = {True: 19, False: 22}
NQ = 4
Q_PARTS = (0, 0, 1, 1, 0, 2)
K_PARTS = (0, 1, 0, 1, 2, 0)
E1 = DH + 1


def attention_schedule(causal):
    keys = [CT * (b + 1) if causal else TILES for b in range(NQ)]
    start = [sum(keys[:b]) for b in range(NQ + 1)]
    steps = start[NQ]
    lead = LEAD[causal]
    units = []
    for b in range(NQ):
        for tt in range(CT):
            seen = (CT * b + tt + 1) * P if causal else T
            for part in range(-(-seen // UNIT)):
                width = min(UNIT, seen - UNIT * part)
                heads = 2 if width <= CHUNK else 1
                for h in range(0, QUAD, heads):
                    units.append((b, tt, h, part, width, causal and UNIT * part + width == seen, heads))
    assert len(units) % 2 == 0
    place = [k * steps // len(units) for k in range(len(units))]
    first = [next(i for i, u in enumerate(units) if u[0] == b) for b in range(NQ)]
    last = [max(i for i, u in enumerate(units) if u[0] == b) for b in range(NQ)]
    sched = []
    early = 5
    turn_q = [-24, -22, -16, -4] if causal else [start[b] - lead - early for b in range(NQ)]
    for s in range(-lead - early, steps):
        e = {"units": [], "jobs": [], "chain": []}
        for ahead in (0, 1):
            for k, u in enumerate(units):
                if ahead * steps + place[k] - lead == s:
                    e["units"].append((ahead, len(units) * ahead + k, *u))
                    if k == last[u[0]]:
                        e["chain"].append(e["units"][-1])
            for b in range(NQ):
                assert turn_q[b] < place[first[b]] - lead
                if s == ahead * steps + turn_q[b]:
                    e["jobs"].append(("qa", ahead, b))
                if s == ahead * steps + start[b] - (2 if causal else 4):
                    e["jobs"].append(("qb", ahead, b))
        for b in range(NQ - 1):
            if s == start[b + 1] + 2:
                e["jobs"].append(("ctx", 0, b))
        sched.append(e)
    return keys, start, steps, len(units), sched[:lead + early], sched[lead + early:]


def build(nc, x, a_wq, a_wk, a_wv, a_wo, l_wqkv, l_bqkv, l_wo, l_bo, ln1_g, ln1_b, f_wqkv, f_bqkv,
          f_wo, f_bo, ln2_g, ln2_b, gate_w, w1, b1, w2, b2, rw1, rb1, rw2, rb2, coef_w, coef_b, out, xs, ys):
    top = ExitStack()

    def sb(name, cols, dt=F32, parts=P):
        return top.enter_context(nc.sbuf_tensor(name, [parts, cols], dt))

    def sem(name):
        return top.enter_context(nc.semaphore(name))

    made = {}

    def phase_sems(phase, names):
        if phase in made:
            with nc.Block() as block:
                @block.sync
                def _(sp):
                    for h in made[phase].values():
                        sp.sem_clear(h)
        else:
            made[phase] = {n: sem(f"{phase}_{n}") for n in names}
        return made[phase]

    X = sb("X", T)
    U = sb("U", T)
    XH = sb("XH", T)
    QT = sb("QT", TILES * H * SLOT, BF16)
    KT = sb("KT", PAIRS * T, BF16)
    V = sb("V", T)
    AR = sb("AR", 19456)
    W2S = sb("W2S", NE * FC * D)
    IDF = sb("IDF", P)
    IDB = sb("IDB", P, BF16)
    MQK = sb("MQK", P, BF16)
    MKQ = sb("MKQ", P, BF16)
    UPTO = sb("UPTO", P)
    ONES = sb("ONES", P)
    LAST = sb("LAST", P)
    MHALF = sb("MHALF", TILES)
    AW = sb("AW", 4 * D)
    LW = sb("LW", 4 * D)
    FW = sb("FW", 4 * D)
    LB = sb("LB", 4 * D)
    FB = sb("FB", 4 * D)
    GB = sb("GB", 4)
    GC = sb("GC", EXPERTS + 2)
    GCB = sb("GCB", EXPERTS + 2)
    RANK = sb("RANK", EXPERTS)
    B1T = sb("B1T", NE * FC)
    B2S = sb("B2S", D, F32, NE)
    NUM = sb("NUM", SLOT_TILES)
    FULL = sb("FULL", TILES)
    ST6 = sb("ST6", TILES * 6)
    MV = sb("MV", TILES * 2)
    VE = sb("VE", TILES)
    RSTD = sb("RSTD", TILES)
    MX = sb("MX", NQ * CT * QUAD * 2)
    NM = sb("NM", 2 * CT * QUAD)
    RC = sb("RC", CT * QUAD)
    PS = top.enter_context(nc.psum_tensor("PS", [P, 8 * 512], F32))

    def bank(i, n=1):
        return PS[:, 512 * i:512 * (i + n)]

    def arena(at, cols, dt=F32):
        words = cols if dt == F32 else cols // 2
        v = AR[:, at:at + words]
        return v if dt == F32 else v.bitcast(dt)

    s_in, s_cst, s_wt, s_wtc = sem("inputs_loaded"), sem("constants_made"), sem("a_weights_turned"), sem("a_weights_kept")
    RAW = arena(0, 4 * D)
    B1R = arena(512, P)
    ZERO = arena(13312, SLOT_TILES * D)
    s_first, s_zero, s_slots = sem("first_inputs_loaded"), sem("zeros_made"), sem("slots_zeroed")
    n_first, n_rest = 1 + 4 + 2, 4 + 4 + 4 + 3 + 2 + NE
    with nc.Block() as block:
        @block.sync
        def _(sp):
            loads = [(X[:, :].rearrange("p (t d) -> p t d", d=D), x.rearrange("b (t p) d -> p (b t) d", p=P))]
            loads += [(RAW[:, D * i:D * i + D], w) for i, w in enumerate((a_wq, a_wk, a_wv, a_wo))]
            loads += [(B1R[0:EXPERTS * FC, :], b1.rearrange("e (c f) -> (e c) f", f=P)),
                      (B1R[EXPERTS * FC:NE * FC, :], rb1.rearrange("(c f) -> c f", f=P))]
            assert len(loads) == n_first
            loads += [(LW[:, 0:3 * D], l_wqkv), (LW[:, 3 * D:4 * D], l_wo), (FW[:, 0:3 * D], f_wqkv), (FW[:, 3 * D:4 * D], f_wo)]
            loads += [(LB[:, 0:3 * D], l_bqkv.partition_broadcast(P)), (LB[:, 3 * D:4 * D], l_bo.partition_broadcast(P))]
            loads += [(FB[:, 0:3 * D], f_bqkv.partition_broadcast(P)), (FB[:, 3 * D:4 * D], f_bo.partition_broadcast(P))]
            loads += [(GB[:, i:i + 1], v.rearrange("(p o) -> p o", o=1)) for i, v in enumerate((ln1_g, ln1_b, ln2_g, ln2_b))]
            loads += [(GC[:, 0:EXPERTS], gate_w), (GC[:, EXPERTS:EXPERTS + 2], coef_w),
                      (GCB[:, EXPERTS:EXPERTS + 2], coef_b.partition_broadcast(P))]
            loads += [(B2S[0:EXPERTS, :], b2), (B2S[EXPERTS:NE, :], rb2.rearrange("(o d) -> o d", o=1))]
            w2v = W2S[:, :].rearrange("p (e c d) -> p e c d", c=FC, d=D)
            loads += [(w2v[:, e, :, :], w2[e, :, :].rearrange("(c p) d -> p c d", p=P)) for e in range(EXPERTS)]
            loads += [(w2v[:, EXPERTS, :, :], rw2.rearrange("(c p) d -> p c d", p=P))]
            for k, (dst, src) in enumerate(loads):
                sp.dma_start(dst, src).then_inc(s_first if k < n_first else s_in, 16)
            assert len(loads) == n_first + n_rest
            sp.wait_ge(s_zero, 1)
            sp.dma_start(xs.rearrange("(t p) d -> p t d", p=P), ZERO.rearrange("p (t d) -> p t d", d=D)).then_inc(s_slots, 16)
            sp.wait_ge(s_first, 16 * n_first)

        n_set = 6 + EXPERTS + SLOT_TILES + TILES

        @block.gpsimd
        def _(pool):
            pool.memset(IDF[:, :], 0.0).then_inc(s_cst, 1)
            pool.memset(ONES[:, :], 1.0).then_inc(s_cst, 1)
            pool.memset(MQK[:, :], 0.0).then_inc(s_cst, 1)
            pool.memset(MKQ[:, :], 0.0).then_inc(s_cst, 1)
            pool.memset(MHALF[:, :], -0.5).then_inc(s_cst, 1)
            pool.memset(GCB[:, 0:EXPERTS], 0.0).then_inc(s_cst, 1)
            for e in range(EXPERTS):
                pool.memset(RANK[:, e:e + 1], float(EXPERTS - e)).then_inc(s_cst, 1)
            for j in range(SLOT_TILES):
                pool.memset(NUM[:, j:j + 1], float(j)).then_inc(s_cst, 1)
            for j in range(TILES):
                pool.memset(FULL[:, j:j + 1], float(P * j)).then_inc(s_cst, 1)
            pool.wait_ge(s_cst, n_set)
            pool.affine_select(out=IDF[:, :], in_=IDF[:, :], compare_op=ALU.not_equal, fill=1.0, base=0,
                               pattern=[[-1, P]], channel_multiplier=1).then_inc(s_cst, 1)
            pool.affine_select(out=MQK[:, :], in_=MQK[:, :], compare_op=ALU.is_ge, fill=MASKED, base=0,
                               pattern=[[-1, P]], channel_multiplier=1).then_inc(s_cst, 1)
            pool.affine_select(out=MKQ[:, :], in_=MKQ[:, :], compare_op=ALU.is_ge, fill=MASKED, base=0,
                               pattern=[[1, P]], channel_multiplier=-1).then_inc(s_cst, 1)
            pool.affine_select(out=UPTO[:, :], in_=ONES[:, :], compare_op=ALU.is_ge, fill=0.0, base=0,
                               pattern=[[1, P]], channel_multiplier=-1).then_inc(s_cst, 1)
            pool.affine_select(out=LAST[:, :], in_=ONES[:, :], compare_op=ALU.is_ge, fill=0.0, base=1 - P,
                               pattern=[[0, P]], channel_multiplier=1).then_inc(s_cst, 1)
            pool.wait_ge(s_cst, n_set + 5)
            pool.tensor_copy(IDB[:, :], IDF[:, :]).then_inc(s_cst, 1)

        @block.tensor
        def _(pe):
            pe.wait_ge(s_cst, n_set + 5)
            pe.wait_ge(s_first, 16 * n_first)
            for i in range(4):
                pe.transpose(bank(0)[:, D * i:D * i + D], RAW[:, D * i:D * i + D], IDF[:, :])
            n = NE * FC
            pe.transpose(bank(1)[:, 0:n], B1R[0:n, :], IDF[0:n, 0:n]).then_inc(s_wt, 1)

        @block.scalar
        def _(act):
            act.wait_ge(s_wt, 1)
            act.copy(AW[:, :], bank(0)).then_inc(s_wtc, 1)
            act.copy(B1T[:, :], bank(1)[:, 0:NE * FC]).then_inc(s_wtc, 1)

        @block.vector
        def _(dve):
            dve.memset(ZERO, 0.0).then_inc(s_zero, 1)

    def norm_dve(dve, s, j, src, dst):
        groups = TILES // NG
        for g in range(groups):
            k = groups * j + g
            if j:
                dve.wait_ge(s["xh"], NG * (k - groups + 1))
            for i in range(NG * g, NG * (g + 1)):
                dve.bn_stats(ST6[:, 6 * i:6 * i + 6], src[:, i * P:(i + 1) * P]).then_inc(s["st"], 1)
            dve.wait_ge(s["st"], NG * (k + 1))
            for i in range(NG * g, NG * (g + 1)):
                dve.bn_aggr(MV[:, 2 * i:2 * i + 2], ST6[:, 6 * i:6 * i + 6]).then_inc(s["mv"], 1)
        for g in range(groups):
            k = groups * j + g
            dve.wait_ge(s["mv"], NG * (k + 1))
            dve.wait_ge(s["rstd"], k + 1)
            for i in range(NG * g, NG * (g + 1)):
                dve.tensor_scalar(dst[:, i * P:(i + 1) * P], src[:, i * P:(i + 1) * P],
                                  MV[:, 2 * i:2 * i + 1], RSTD[:, i:i + 1], ALU.subtract, ALU.mult).then_inc(s["xh"], 1)

    def norm_pool(pool, s, norms):
        groups = TILES // NG
        for k in range(groups * norms):
            g = k % groups
            v = slice(NG * g, NG * (g + 1))
            pool.wait_ge(s["mv"], NG * (k + 1))
            if k >= groups:
                pool.wait_ge(s["rstd"], k - groups + 1)
            pool.tensor_scalar(VE[:, v], MV[:, :].rearrange("p (t two) -> p t two", two=2)[:, v, 1], 1e-5, None,
                               ALU.add).then_inc(s["ve"], 1)
            pool.wait_ge(s["ve"], k + 1)
            pool.tensor_tensor(RSTD[:, v], VE[:, v], MHALF[:, v], ALU.pow).then_inc(s["rstd"], 1)

    def prepare(kind):
        s = phase_sems("prepare", ("st", "mv", "ve", "rstd", "xh", "turned", "xt", "qkv", "qk", "v",
                                            "a0", "r1", "a1", "a2", "tok", "ktp", "kte", "e", "ones", "bias", "ktd", "zeros"))
        W = {"a": AW, "f": FW, "l": LW}[kind]
        B = {"a": None, "f": FB, "l": LB}[kind]
        norms = 2 if kind == "f" else 1
        KTOK = [arena(2048 * p, 4096, BF16) for p in range(2)]
        QK = [arena(4096 + 1024 * p, 1024) for p in range(2)]
        R1 = [arena(6144 + 1024 * p, 1024) for p in range(2)]
        A = [[arena(8192 + 512 * (3 * p + i), 1024, BF16) for i in range(3)] for p in range(2)]
        XT = [arena(11264 + 512 * c, 512) for c in range(CHUNKS)]
        TB = [bank(0), bank(1)]
        G = [bank(2, 3), bank(5, 3)]
        QF = KT[:, :].bitcast(F32)
        V1 = QT[:, :].bitcast(F32)

        def kt_tile(c, i):
            tile = CT * c + i
            src = G[c % 2][:, 512 * (i % 3):512 * (i % 3) + 512].bitcast(BF16).rearrange("p (j t) -> p j t", t=P)
            return KT[:, :].rearrange("p (j t) -> p j t", t=T)[:, :, P * tile:P * tile + P], src

        with nc.Block() as block:
            if kind == "a":
                @block.sync
                def _(sp):
                    sp.wait_ge(s_in, 16 * n_rest)
                    sp.wait_ge(s_slots, 16)

            @block.gpsimd
            def _(pool):
                norm_pool(pool, s, norms)
                if kind == "l":
                    pool.memset(V1[:, 0:TILES * H * E1], 1.0).then_inc(s["ones"], 1)
                    pool.wait_ge(s["xh"], TILES * norms)
                    pool.tensor_tensor(X[:, :].rearrange("p (t d) -> p t d", d=D), X[:, :].rearrange("p (t d) -> p t d", d=D),
                                       B[:, 3 * D:4 * D].unsqueeze(1).to_broadcast([P, TILES, D]), ALU.add).then_inc(s["bias"], 1)
                    return
                pool.memset(QT[:, :].rearrange("p (n s) -> p n s", s=SLOT)[:, :, MCOL:SLOT], 0.0).then_inc(s["zeros"], 1)
                for c in range(CHUNKS):
                    p = c % 2
                    pool.wait_ge(s["a0"], c + 1)
                    pool.wait_ge(s["qk"], c + 1)
                    if c >= 2:
                        pool.wait_ge(s["a2"], c - 1)
                    pool.tensor_tensor(R1[p], QK[p], A[p][0], ALU.subtract).then_inc(s["r1"], 1)
                if kind == "f":
                    pool.wait_ge(s["xh"], TILES * norms)
                    pool.tensor_tensor(U[:, :].rearrange("p (t d) -> p t d", d=D), U[:, :].rearrange("p (t d) -> p t d", d=D),
                                       B[:, 3 * D:4 * D].unsqueeze(1).to_broadcast([P, TILES, D]), ALU.add).then_inc(s["bias"], 1)

            @block.vector
            def _(dve):
                if kind == "f":
                    norm_dve(dve, s, 0, X, U)
                    norm_dve(dve, s, 1, U, XH)
                else:
                    norm_dve(dve, s, 0, X, XH)
                if kind == "l":
                    dve.wait_ge(s["ones"], 1)
                else:
                    for p in range(2):
                        kp = KTOK[p].rearrange("p (n s) -> p n s", s=SLOT)
                        dve.memset(kp[:, :, MCOL:MCOL + 3], 1.0).then_inc(s["ones"], 1)
                        dve.memset(kp[:, :, MCOL + 3:SLOT], 0.0).then_inc(s["ones"], 1)

                def take(c):
                    p = c % 2
                    src = G[p][:, 0:1024].rearrange("p (i q d) -> p i q d", i=CT, d=D)
                    dst = QK[p].rearrange("p (q i d) -> p i q d", i=CT, d=D)
                    vsrc = G[p][:, 1024:1536]
                    dve.wait_ge(s["qkv"], c + 1)
                    if c >= 2:
                        dve.wait_ge(s["a0"], c - 1)
                        dve.wait_ge(s["e" if kind == "l" else "r1"], c - 1)
                    if kind == "l":
                        vdst = V1[:, c * CT * H * E1:(c + 1) * CT * H * E1].rearrange("p (n e) -> p n e", e=E1)[:, :, 0:DH]
                    else:
                        vdst = V[:, c * CHUNK:(c + 1) * CHUNK]
                    if B is None:
                        dve.tensor_copy(dst, src).then_inc(s["qk"], 1)
                        dve.tensor_copy(vdst, vsrc).then_inc(s["v"], 1)
                    else:
                        for i in range(CT):
                            ins = dve.tensor_tensor(dst[:, i], src[:, i], B[:, 0:2 * D].rearrange("p (q d) -> p q d", d=D), ALU.add)
                        ins.then_inc(s["qk"], 1)
                        if kind == "l":
                            for i in range(CT):
                                ins = dve.tensor_tensor(vdst[:, H * i:H * i + H, :],
                                                        vsrc[:, D * i:D * i + D].rearrange("p (h d) -> p h d", d=DH),
                                                        B[:, 2 * D:3 * D].rearrange("p (h d) -> p h d", d=DH), ALU.add)
                        else:
                            ins = dve.tensor_tensor(vdst.rearrange("p (i d) -> p i d", d=D), vsrc.rearrange("p (i d) -> p i d", d=D),
                                                    B[:, 2 * D:3 * D].unsqueeze(1).to_broadcast([P, CT, D]), ALU.add)
                        ins.then_inc(s["v"], 1)

                def features(c):
                    p = c % 2
                    dve.wait_ge(s["e"], c + 1)
                    dve.wait_ge(s["a0"], c + 1)
                    fdst = QF[:, 2 * c * CHUNK:2 * (c + 1) * CHUNK]
                    dve.scalar_tensor_tensor(out=fdst, in0=A1F[p], scalar=1.0, in1=R1[p], op0=ALU.min,
                                             op1=ALU.add).then_inc(s["tok"], 1)

                def last_part(c):
                    p = c % 2
                    dve.wait_ge(s["a1"], c + 1)
                    dve.wait_ge(s["r1"], c + 1)
                    if c >= 2:
                        dve.wait_ge(s["tok"], c - 1)
                    dve.tensor_tensor(A[p][2], R1[p], A[p][1], ALU.subtract).then_inc(s["a2"], 1)

                def place(c):
                    p = c % 2
                    qd = QT[:, c * CT * H * SLOT:(c + 1) * CT * H * SLOT].rearrange("p (n s) -> p n s", s=SLOT)
                    kd = KTOK[p].rearrange("p (n s) -> p n s", s=SLOT)
                    dve.wait_ge(s["a2"], c + 1)
                    if c >= 2:
                        dve.wait_ge(s["ktp"], CT * (c - 1))
                    for slot in range(6):
                        for half, (dd, parts) in enumerate(((qd, Q_PARTS), (kd, K_PARTS))):
                            a = A[p][parts[slot]][:, CHUNK * half:CHUNK * half + CHUNK].rearrange("p (n d) -> p n d", d=DH)
                            ins = dve.tensor_copy(dd[:, :, DH * slot:DH * slot + DH], a)
                    ins.then_inc(s["tok"], 1)

                def take_kt(c):
                    for i in range(1, CT, 2):
                        dve.wait_ge(s["ktp"], CT * c + i + 1)
                        dve.tensor_copy(*kt_tile(c, i)).then_inc(s["ktd"], 1)

                if kind == "l":
                    take(0)
                    for c in range(CHUNKS):
                        if c + 1 < CHUNKS:
                            take(c + 1)
                        features(c)
                else:
                    for c in range(0, CHUNKS, 2):
                        take(c)
                        take(c + 1)
                        last_part(c)
                        place(c)
                        last_part(c + 1)
                        take_kt(c)
                        place(c + 1)
                        take_kt(c + 1)

            @block.tensor
            def _(pe):
                def turn(c):
                    p = c % 2
                    pe.wait_ge(s["xh"], TILES * (norms - 1) + CT * (c + 1))
                    if c >= 2:
                        pe.wait_ge(s["xt"], c - 1)
                    for i in range(CT):
                        ins = pe.transpose(TB[p][:, P * i:P * i + P], XH[:, (CT * c + i) * P:(CT * c + i + 1) * P], IDF[:, :])
                    ins.then_inc(s["turned"], 1)

                def project(c):
                    p = c % 2
                    pe.wait_ge(s["xt"], c + 1)
                    if c >= 2:
                        if kind == "l":
                            pe.wait_ge(s["v"], c - 1)
                        else:
                            pe.wait_ge(s["kte"], CT // 2 * (c - 1))
                            pe.wait_ge(s["ktd"], CT // 2 * (c - 1))
                    for i in range(CT):
                        lhs = XT[c][:, P * i:P * i + P]
                        pe.matmul(G[p][:, 256 * i:256 * i + 256], lhs, W[:, 0:2 * D], start=True, stop=True)
                        ins = pe.matmul(G[p][:, 1024 + P * i:1024 + P * i + P], lhs, W[:, 2 * D:3 * D], start=True, stop=True)
                    ins.then_inc(s["qkv"], 1)

                def turn_k(c):
                    p = c % 2
                    pe.wait_ge(s["tok"], c + 1)
                    if c < 2:
                        pe.wait_ge(s["ones"], 4)
                    for i in range(CT):
                        if i == 3:
                            pe.wait_ge(s["kte"], CT // 2 * c + 1)
                        dst = G[p][:, 512 * (i % 3):512 * (i % 3) + 512].bitcast(BF16)
                        for j in range(PAIRS):
                            ins = pe.transpose(dst[:, P * j:P * j + P],
                                               KTOK[p][:, (i * PAIRS + j) * P:(i * PAIRS + j + 1) * P], IDB[:, :])
                        ins.then_inc(s["ktp"], 1)

                turn(0)
                turn(1)
                project(0)
                project(1)
                turn(2)
                turn(3)
                for c in range(CHUNKS):
                    if kind != "l":
                        turn_k(c)
                    if c + 2 < CHUNKS:
                        project(c + 2)

            @block.scalar
            def _(act):
                for c in range(CHUNKS):
                    act.wait_ge(s["turned"], c + 1)
                    if kind == "f":
                        ins = act.activation(XT[c], TB[c % 2], ACT.Identity, bias=GB[:, 1:2], scale=GB[:, 0:1])
                    else:
                        ins = act.copy(XT[c], TB[c % 2])
                    ins.then_inc(s["xt"], 1)

                def first_part(c):
                    act.wait_ge(s["qk"], c + 1)
                    if c >= 2:
                        act.wait_ge(s["tok"], c - 1)
                    act.copy(A[c % 2][0], QK[c % 2]).then_inc(s["a0"], 1)

                def second_part(c):
                    act.wait_ge(s["r1"], c + 1)
                    act.copy(A[c % 2][1], R1[c % 2]).then_inc(s["a1"], 1)

                def take_kt(c):
                    for i in range(0, CT, 2):
                        act.wait_ge(s["ktp"], CT * c + i + 1)
                        act.copy(*kt_tile(c, i)).then_inc(s["kte"], 1)

                if kind == "l":
                    for c in range(CHUNKS):
                        act.wait_ge(s["qk"], c + 1)
                        if c >= 2:
                            act.wait_ge(s["tok"], c - 1)
                        act.activation(A1F[c % 2], QK[c % 2], ACT.Exp).then_inc(s["e"], 1)
                        act.activation(R1[c % 2], QK[c % 2], ACT.Relu).then_inc(s["a0"], 1)
                else:
                    for c in range(0, CHUNKS, 2):
                        first_part(c)
                        first_part(c + 1)
                        second_part(c)
                        second_part(c + 1)
                        take_kt(c)
                        take_kt(c + 1)

    A1F = [arena(8192 + 1024 * p, 1024) for p in range(2)]

    def attention(causal):
        s = phase_sems("attention", ("staged", "qa", "qae", "qb", "qbe", "score", "max", "part", "minus",
                                            "qk", "exp", "pv", "acc", "ctx", "ctxe", "rcp", "done", "kc", "kn", "vc", "vset", "qset", "pset"))
        keys, start, steps, per_quad, lead_in, body = attention_schedule(causal)
        block_of = [b for b in range(NQ) for _ in range(keys[b])]
        PR = [arena(2048 * i, 2048) for i in range(2)]
        QM = [arena(4096 + 512 * b, 1024, BF16) for b in range(NQ)]
        QA = [arena(6144 + 1024 * b, QUAD * CHUNK, BF16) for b in range(NQ)]
        QB = [arena(10240 + 1024 * i, QUAD * CHUNK, BF16) for i in range(2)]
        CTX = arena(12288, 512)
        CN = arena(12800, 512)
        KC = arena(13312, 2 * T, BF16)
        KN = arena(15360, 2 * T, BF16)
        VC = arena(17408, TILES * QUAD * 32)
        parts = [-(-(CT * (b + 1) * P if causal else T) // UNIT) for b in range(NQ)]
        MB = [bank(0, 2), bank(2, 2)]
        SB = [bank(4), bank(5)]
        ACC, MISC = bank(6), bank(7)
        kv = lambda k: k.rearrange("p (j t) -> p j t", t=T)
        vc = VC.rearrange("p (t h e) -> p t h e", h=QUAD, e=32)
        lead_units = sum(len(e["units"]) for e in lead_in)
        before = {k: sum(j[0] == k for e in lead_in for j in e["jobs"]) for k in ("qa", "qb", "ctx")}
        EV = {"qa": "qae", "qb": "qbe", "ctx": "ctxe"}

        primed = ("pv", "ctx", "exp", "acc", "ctxe", "done")

        def wait(e, name, n):
            n = n + 1 if name in primed else n
            if not isinstance(n, int) or n > 0:
                e.wait_ge(s[name], n)

        def products(u):
            h, width, heads = u[4], u[6], u[8]
            if heads == 2:
                return [(h + i, 0, width, CHUNK * i) for i in range(2)]
            return [(h, a, min(CHUNK, width - a), a) for a in range(0, width, CHUNK)]

        def pe_unit(pe, g, unit, in_next, only=None):
            ahead, u, b, tt, h, part, width, diagonal, heads = unit
            n = per_quad * g + u
            if not only and (not isinstance(n, int) or n >= 2):
                wait(pe, "max", n - 1)
            if not only and tt == 0 and h == 0 and part == 0:
                wait(pe, "qae", NQ * (g + ahead) + b + 1)
                if in_next:
                    wait(pe, "kn", 16 * (g + 1))
            every = products(unit)
            for head, a, w, at in every if only is None else every[only:only + 1]:
                q = QA[b][:, CHUNK * head + P * tt:CHUNK * head + P * tt + P]
                k = kv(KN if in_next else KC)[:, head // 2, UNIT * part + a:UNIT * part + a + w]
                dst = MB[u % 2][:, at:at + w]
                masked = diagonal and a + w == width
                ins = pe.matmul(dst, q, k, start=True, stop=not masked)
                if masked:
                    ins = pe.matmul(dst[:, w - P:w], IDB[:, :], MQK[:, :], start=False, stop=True)
            if only is None or only == len(every) - 1:
                ins.then_inc(s["score"], 1)

        def pe_scores(pe, g, st, h):
            n = steps * g + st
            b = block_of[st]
            kt = st - start[b]
            lo = max(0, kt - CT * b) * P if causal else 0
            wait(pe, "exp", 4 * n + (h - 1 if st else max(h - 1, 0)))
            if kt == 0 and h == 0:
                wait(pe, "qbe", NQ * g + b + 1)
            q = QB[b % 2][:, CHUNK * h + lo:CHUNK * h + CHUNK]
            k = kv(KC)[:, h // 2, P * kt:P * kt + P]
            dst = SB[h % 2]
            diagonal = causal and kt >= CT * b
            ins = pe.matmul(dst[:, lo:CHUNK], k, q, start=True, stop=not diagonal)
            if diagonal:
                ins = pe.matmul(dst[:, lo:lo + P], IDB[:, :], MKQ[:, :], start=False, stop=True)
            ins.then_inc(s["qk"], 1)

        def pe_values(pe, g, st):
            n = steps * g + st
            b = block_of[st]
            kt = st - start[b]
            lo = max(0, kt - CT * b) * P if causal else 0
            wait(pe, "exp", 4 * n + 4)
            if kt == 0:
                wait(pe, "acc", NQ * g + b)
            if st == 0:
                wait(pe, "vc", g + 1)
            pr = PR[st % 2].rearrange("p (h t) -> p h t", t=CHUNK)
            for h in range(QUAD):
                ins = pe.matmul(ACC[32 * h:32 * h + 32, lo:CHUNK], vc[:, kt, h, :], pr[:, h, lo:CHUNK],
                                start=kt == 0, stop=kt == keys[b] - 1)
            ins.then_inc(s["pv"], 1)

        def pe_job(pe, g, kind, ahead, b, seen):
            for k in ("qa", "qb", "ctx"):
                wait(pe, EV[k], seen[k](g))
            nb = NQ * (g + ahead) + b
            if kind == "ctx":
                wait(pe, "acc", nb + 1)
                for i in range(CT):
                    ins = pe.transpose(MISC[:, P * i:P * i + P], CTX[:, P * i:P * i + P], IDF[:, :])
            else:
                pe.wait_ge(s["staged" if kind == "qa" else "minus"], nb + 1)
                q = QM[b].rearrange("p (t j r) -> p t j r", j=2, r=P)
                dst = MISC.bitcast(BF16).rearrange("p (j t) -> p j t", t=CHUNK)
                for j in range(2):
                    for i in range(CT):
                        ins = pe.transpose(dst[:, j, P * i:P * i + P], q[:, i, j, :], IDB[:, :])
            ins.then_inc(s[kind], 1)

        def seen_before(entries, base, per):
            out, n = [], dict(base)
            for e in entries:
                row = []
                for job in e["jobs"]:
                    row.append({k: (lambda g, a=n[k], m=per[k]: a + m * g) for k in n})
                    n[job[0]] += 1
                out.append(row)
            return out, n

        zero = {"qa": 0, "qb": 0, "ctx": 0}
        seen_lead, _ = seen_before(lead_in, zero, zero)
        per = {"qa": NQ, "qb": NQ, "ctx": NQ}
        seen_body, seen_end = seen_before(body, before, per)

        def in_quad(e, last):
            keep = lambda x: not (last and x[0])
            return [u for u in e["units"] if keep(u)], [j for j in e["jobs"] if not (last and j[1])]

        def pe_products(pe, g, list_):
            for u, i in list_:
                pe_unit(pe, g, u, in_next=u[0] == 1, only=i)

        def pe_body(pe, g, last):
            kept = []
            pe.wait_ge(s["kc"], 2 * g + 1)
            for st, e in enumerate(body):
                units, jobs = in_quad(e, last)
                for k, job in enumerate(e["jobs"]):
                    if job in jobs:
                        seen = seen_body[st][k]
                        if last:
                            gone = {q: sum(j[0] == q and j[1] for ee in body[:st] for j in ee["jobs"])
                                    + sum(j[0] == q and j[1] for j in e["jobs"][:k]) for q in zero}
                            seen = {q: (lambda g, f=seen[q], m=gone[q]: f(g) - m) for q in zero}
                        pe_job(pe, g, *job, seen)
                fresh = [(u, i) for u in units for i in range(len(products(u)))]
                n = len(fresh) // 4
                pe_scores(pe, g, st, 0)
                pe_products(pe, g, kept)
                pe_scores(pe, g, st, 1)
                if st:
                    pe_values(pe, g, st - 1)
                pe_scores(pe, g, st, 2)
                if st == 0:
                    pe.wait_ge(s["kc"], 2 * g + 2)
                pe_products(pe, g, fresh[:n])
                pe_scores(pe, g, st, 3)
                kept = fresh[len(fresh) - n:] if st + 1 < steps else []
                pe_products(pe, g, fresh[n:len(fresh) - len(kept)])
            pe_values(pe, g, steps - 1)
            seen = dict(seen_end)
            if last:
                for q in zero:
                    seen[q] -= sum(j[0] == q and j[1] for ee in body for j in ee["jobs"])
            pe_job(pe, g, "ctx", 0, NQ - 1, {q: (lambda g, a=seen[q], m=per[q]: a + m * g) for q in zero})

        def dve_unit(dve, g, ahead, u, b, tt, h, part, width, diagonal, heads):
            wait(dve, "score", per_quad * g + u + 1)
            at = (b * CT + tt) * QUAD + h
            if heads == 2:
                src = MB[u % 2].rearrange("p (h k) -> p h k", k=CHUNK)[:, :, 0:width]
            else:
                src = MB[u % 2][:, 0:width]
            dve.tensor_reduce(MX[:, :].rearrange("p (n c) -> p n c", c=2)[:, at:at + heads, part], src, AX.X,
                              ALU.max).then_inc(s["max"], 1)

        def dve_chain(dve, g, ahead, b, u_end):
            nb = NQ * (g + ahead) + b
            mx = MX[:, b * CT * QUAD * 2:(b + 1) * CT * QUAD * 2].rearrange("p (n c) -> p n c", c=2)
            q = QM[b].rearrange("p (n s) -> p n s", s=SLOT)
            n_part = 4 * nb
            dve.wait_ge(s["max"], u_end)
            dve.wait_ge(s["qa"], nb + 1)
            dve.tensor_reduce(NM[:, 0:16], mx[:, :, 0:parts[b]], AX.X, ALU.max,
                              negate=True).then_inc(s["part"], 1)
            dve.wait_ge(s["part"], n_part + 1)
            dve.tensor_copy(q[:, :, MCOL], NM[:, 0:16]).then_inc(s["part"], 1)
            dve.wait_ge(s["part"], n_part + 2)
            dve.tensor_tensor(NM[:, 16:32], NM[:, 0:16], q[:, :, MCOL], ALU.subtract).then_inc(s["part"], 1)
            dve.wait_ge(s["part"], n_part + 3)
            dve.tensor_copy(q[:, :, MCOL + 1], NM[:, 16:32]).then_inc(s["part"], 1)
            dve.wait_ge(s["part"], n_part + 4)
            dve.tensor_tensor(q[:, :, MCOL + 2], NM[:, 16:32], q[:, :, MCOL + 1], ALU.subtract).then_inc(s["minus"], 1)

        def dve_sums(dve, g, b):
            nb = NQ * g + b
            wait(dve, "ctxe", nb + 1)
            wait(dve, "done", nb)
            cn = CN.rearrange("p (n e) -> p n e", e=32)
            dve.reciprocal(RC[:, :], cn[:, :, DH]).then_inc(s["rcp"], 1)

        def dve_copy_k(dve, g):
            dve.wait_ge(s["kn"], 16 * (g + 1))
            wait(dve, "qk", 4 * steps * (g + 1))
            for half in range(2):
                keys_ = slice(T // 2 * half, T // 2 * (half + 1))
                dve.tensor_copy(kv(KC)[:, :, keys_], kv(KN)[:, :, keys_]).then_inc(s["kc"], 1)

        def dve_copy_v(dve, g):
            if not isinstance(g, int) or g >= 0:
                wait(dve, "pv", steps * (g + 1))
            v = V[:, :].rearrange("p (t d) -> p t d", d=D)
            q = (g + 1) * QUAD * DH
            v = v[:, :, bass.ds(q, QUAD * DH)] if not isinstance(q, int) else v[:, :, q:q + QUAD * DH]
            dve.tensor_copy(vc[:, :, :, 0:DH], v.rearrange("p t (h d) -> p t h d", d=DH)).then_inc(s["vc"], 1)

        def dve_body(dve, g, last):
            for st, e in enumerate(body):
                units, _ = in_quad(e, last)
                for k, u in enumerate(units):
                    if st == steps - 1 and k == 0:
                        dve_copy_k(dve, g)
                    if st == steps - 1 and k == 1:
                        dve_copy_v(dve, g)
                    dve_unit(dve, g, *u)
                    if u in e["chain"]:
                        dve_chain(dve, g, u[0], u[2], per_quad * g + u[1] + 1)
                for b in range(NQ - 1):
                    if st == start[b + 1] + 3:
                        dve_sums(dve, g, b)
            dve_sums(dve, g, NQ - 1)

        def act_exp(act, g, st, h):
            n = steps * g + st
            b = block_of[st]
            lo = max(0, st - start[b] - CT * b) * P if causal else 0
            wait(act, "qk", 4 * n + h + 1)
            if h == 0:
                wait(act, "pv", steps * g + max(st - 1, 0))
            dst = PR[st % 2].rearrange("p (h t) -> p h t", t=CHUNK)[:, h, lo:CHUNK]
            act.activation(dst, SB[h % 2][:, lo:CHUNK], ACT.Exp, scale=SCALE).then_inc(s["exp"], 1)

        def act_sums(act, g, b):
            nb = NQ * g + b
            wait(act, "pv", steps * g + start[b + 1])
            wait(act, "ctx", nb)
            act.copy(CTX, ACC).then_inc(s["acc"], 1)

        def act_job(act, g, kind, ahead, b, pieces=range(4)):
            nb = NQ * (g + ahead) + b
            if 0 in pieces:
                wait(act, kind, nb + 1)
            if kind == "ctx":
                wait(act, "done", nb)
                act.copy(CN, MISC).then_inc(s["ctxe"], 1)
                return
            src = MISC.bitcast(BF16).rearrange("p (j t) -> p j t", t=CHUNK)
            dst = (QA[b] if kind == "qa" else QB[b % 2]).rearrange("p (j i t) -> p j i t", i=2, t=CHUNK)
            for k in pieces:
                j, half = divmod(k, 2)
                r = slice(SLOT * half, SLOT * half + SLOT)
                ins = act.copy(dst[r, j, half, :], src[r, j])
            if 3 in pieces:
                ins.then_inc(s[EV[kind]], 1)

        readout = {}
        for st, e in enumerate(body):
            for job in e["jobs"]:
                for k in range(1 if job[0] == "ctx" else 4):
                    at = (st + k // 2, 2 * (k % 2)) if causal else (st + k, 0)
                    readout.setdefault(at, []).append((job, range(4) if job[0] == "ctx" else [k]))

        def act_body(act, g, last):
            for st in range(steps):
                if st - 1 in start[1:NQ]:
                    act_sums(act, g, start.index(st - 1) - 1)
                for h in range(QUAD):
                    for job, pieces in readout.get((st, h), []):
                        if not (last and job[1]):
                            act_job(act, g, *job, pieces)
                    act_exp(act, g, st, h)
            act_sums(act, g, NQ - 1)
            act_job(act, g, "ctx", 0, NQ - 1)

        def pool_stage(pool, g, b):
            nb = NQ * g + b
            if not isinstance(nb, int) or nb >= NQ:
                wait(pool, "qb", nb - NQ + 1)
            q = QT[:, :].rearrange("p (t r) -> p t r", r=H * SLOT)
            at = g * QUAD * SLOT
            sl = slice(at, at + QUAD * SLOT) if isinstance(at, int) else bass.ds(at, QUAD * SLOT)
            pool.tensor_copy(QM[b].rearrange("p (t r) -> p t r", r=QUAD * SLOT), q[:, CT * b:CT * b + CT, sl]).then_inc(s["staged"], 1)

        def pool_context(pool, g, b):
            pool.wait_ge(s["rcp"], NQ * g + b + 1)
            cn = CN.rearrange("p (t h e) -> p t h e", h=QUAD, e=32)[:, :, :, 0:DH]
            at = g * QUAD * DH
            sl = slice(at, at + QUAD * DH) if isinstance(at, int) else bass.ds(at, QUAD * DH)
            dst = XH[:, :].rearrange("p (t d) -> p t d", d=D)[:, CT * b:CT * b + CT, sl].rearrange("p t (h d) -> p t h d", d=DH)
            rc = RC[:, :].rearrange("p (t h) -> p t h", h=QUAD).unsqueeze(3).to_broadcast([P, CT, QUAD, DH])
            pool.tensor_tensor(dst, cn, rc, ALU.mult).then_inc(s["done"], 1)

        def zeros_of(q, half):
            qp = q.bitcast(F32).rearrange("p (j i t) -> p j i t", i=2, t=CHUNK // 2)
            return qp[SLOT * half:SLOT * half + SLOT, :, 1 - half, :]

        with nc.Block() as block:
            @block.sync
            def _(sp):
                sp.dma_start(kv(KN), kv(KT[:, :])[:, 2:4, :]).then_inc(s["kn"], 16)
                with sp.Fori(0, QUADS - 2) as g:
                    sp.wait_ge(s["kc"], 2 * g + 4)
                    sp.wait_ge(s["score"], per_quad * (g + 1) + lead_units)
                    sp.dma_start(kv(KN), kv(KT[:, :])[:, bass.ds(2 * g + 4, 2), :]).then_inc(s["kn"], 16)

            @block.gpsimd
            def _(pool):
                pool.sem_inc(s["done"], 1)
                pool.wait_ge(s["staged"], 1)
                for k, q in enumerate((*QA[1:], *QB)):
                    if k + 1 < NQ:
                        pool_stage(pool, 0, k + 1)
                        pool.wait_ge(s["staged"], k + 2)
                    for half in range(2):
                        pool.memset(zeros_of(q, half), 0.0).then_inc(s["pset"], 1)
                        pool.wait_ge(s["pset"], 2 * k + half + 1)
                pool.memset(VC, 0.0).then_inc(s["vset"], 1)
                pool.wait_ge(s["vset"], 1)
                pool.memset(vc[:, :, :, DH:DH + 1], 1.0).then_inc(s["vset"], 1)
                with pool.Fori(0, QUADS - 1) as g:
                    for b in range(NQ):
                        pool_stage(pool, g + 1, b)
                        pool_context(pool, g, b)
                for b in range(NQ):
                    pool_context(pool, QUADS - 1, b)

            @block.vector
            def _(dve):
                pool_stage(dve, 0, 0)
                for half in range(2):
                    dve.memset(zeros_of(QA[0], half), 0.0).then_inc(s["qset"], 1)
                dve.tensor_copy(kv(KC), kv(KT[:, :])[:, 0:2, :]).then_inc(s["kc"], 2)
                for e in lead_in:
                    for u in e["units"]:
                        dve_unit(dve, 0, *u)
                        if u in e["chain"]:
                            dve_chain(dve, 0, u[0], u[2], u[1] + 1)
                dve.wait_ge(s["vset"], 2)
                dve_copy_v(dve, -1)
                with dve.Fori(0, QUADS - 1) as g:
                    dve_body(dve, g, False)
                dve_body(dve, QUADS - 1, True)

            @block.scalar
            def _(act):
                for name in ("exp", "acc", "ctxe"):
                    act.sem_inc(s[name], 1)
                for e in lead_in:
                    for job in e["jobs"]:
                        act_job(act, 0, *job)
                with act.Fori(0, QUADS - 1) as g:
                    act_body(act, g, False)
                act_body(act, QUADS - 1, True)

            @block.tensor
            def _(pe):
                for name in ("pv", "ctx"):
                    pe.sem_inc(s[name], 1)
                pe.wait_ge(s["kc"], 2)
                pe.wait_ge(s["qset"], 2)
                for st, e in enumerate(lead_in):
                    for k, job in enumerate(e["jobs"]):
                        pe_job(pe, 0, *job, seen_lead[st][k])
                    for u in e["units"]:
                        if u[2]:
                            pe.wait_ge(s["pset"], 2 * u[2])
                        pe_unit(pe, 0, u, in_next=False)
                pe.wait_ge(s["vset"], 2)
                pe.wait_ge(s["pset"], 2 * (NQ - 1 + 2))
                with pe.Fori(0, QUADS - 1) as g:
                    pe_body(pe, g, False)
                pe_body(pe, QUADS - 1, True)

    def project_out(W, dst_of, res):
        s = phase_sems("project", ("t", "te", "o", "oe"))
        CTT = [arena(512 * p, 512) for p in range(2)]
        with nc.Block() as block:
            @block.tensor
            def _(pe):
                def turn(c):
                    if c >= 2:
                        pe.wait_ge(s["te"], c - 1)
                    for i in range(CT):
                        ins = pe.transpose(bank(c % 2)[:, P * i:P * i + P], XH[:, (CT * c + i) * P:(CT * c + i + 1) * P], IDF[:, :])
                    ins.then_inc(s["t"], 1)

                turn(0)
                for c in range(CHUNKS):
                    if c + 1 < CHUNKS:
                        turn(c + 1)
                    pe.wait_ge(s["te"], c + 1)
                    if c >= 2:
                        pe.wait_ge(s["oe"], c - 1)
                    for i in range(CT):
                        ins = pe.matmul(bank(2 + c % 2)[:, P * i:P * i + P], CTT[c % 2][:, P * i:P * i + P], W, start=True, stop=True)
                    ins.then_inc(s["o"], 1)

            @block.scalar
            def _(act):
                for c in range(CHUNKS):
                    act.wait_ge(s["t"], c + 1)
                    if c >= 2:
                        act.wait_ge(s["o"], c - 1)
                    act.copy(CTT[c % 2], bank(c % 2)).then_inc(s["te"], 1)

            @block.vector
            def _(dve):
                for c in range(CHUNKS):
                    dve.wait_ge(s["o"], c + 1)
                    a = slice(CHUNK * c, CHUNK * c + CHUNK)
                    dve.tensor_tensor(dst_of[:, a], bank(2 + c % 2), res[:, a], ALU.add).then_inc(s["oe"], 1)

    def experts(tag):
        s = phase_sems("experts", ("w", "st", "mv", "ve", "rstd", "xh", "t", "xt", "lg", "r", "ex", "sw", "stt", "sts",
                                   "b2", "h", "gelu", "y", "acc", "xx", "oh", "rank", "slot", 
                                   "w1c", "b1c", "w2c", "ts", "xts", "hs", "gs", "ys", "yse", "stored", *(f"xs{g}" for g in range(SLOT_TILES // CT))))
        s = {**s, "sent": sem(f"sent_{tag}"), **{f"got{c}": sem(f"got{c}_{tag}") for c in range(CHUNKS)}}
        W1S = QT[:, :].bitcast(F32)[:, 0:EXPERTS * FFN]
        XTT = KT[:, :].bitcast(F32)[:, 0:T]
        HT = [KT[:, :].bitcast(F32)[:, T + 2048 * i:T + 2048 * (i + 1)] for i in range(2)]
        W1R = arena(0, FFN)
        L = arena(512, TILES * 10)
        EX = arena(768, TILES * 10)
        G1 = arena(1024, TILES * 8)
        R = arena(1280, 16 * TILES)
        SW = arena(1536, TILES * NE)
        TMP = arena(1792, TILES * 8)
        PAD = EXPERTS * EXPERTS
        RS = [arena(2048 + 192 * i, PAD + TILES * 8) for i in range(2)]
        NT = arena(2432, TILES * 8)
        END = [arena(2560 + 16 * i, 16) for i in range(2)]
        CMP = arena(2592, SLOT_TILES * 8)
        EJ = arena(2784, SLOT_TILES)
        EI = AR[:, 2816:2816 + SLOT_TILES].bitcast(I32)
        IDX = AR[:, 2848:2848 + TILES].bitcast(U32)
        SWT = arena(2880, T)
        XSS = arena(4928, SLOT_TILES * D)
        YSS = arena(8000, SLOT_TILES * D)
        YG = XSS[:, 0:T]
        XTS = arena(11072, SLOT_TILES * D)
        W1C = [arena(14144 + 512 * i, FFN) for i in range(RING)]
        W2C = [arena(15680 + 512 * i, FFN) for i in range(RING)]
        HTS = [arena(17216 + 512 * i, FFN) for i in range(RING)]
        B1C = [arena(18752 + 4 * i, FC) for i in range(RING)]
        HB = [bank(2), bank(3), bank(0)]
        YB = [bank(4), bank(5), bank(1)]

        def v3(a, n):
            return a.rearrange("p (t n) -> p t n", n=n)

        def col(a):
            return a.unsqueeze(2)

        per = CT
        LOADS = SLOT_TILES // per
        EARLY = CHUNKS // 2

        with nc.Block() as block:
            @block.sync
            def _(sp):
                sp.dma_start(W1S.rearrange("p (e f) -> p e f", f=FFN), w1_in.rearrange("e p f -> p e f")).then_inc(s["w"], 16)
                sp.dma_start(W1R, rw1).then_inc(s["w"], 16)
                sp.wait_ge(s["sent"], 16 * TILES)
                for i in range(LOADS):
                    sp.dma_start(XSS[:, per * D * i:per * D * (i + 1)].rearrange("p (t d) -> p t d", d=D),
                                 xs[P * per * i:P * per * (i + 1), :].rearrange("(t p) d -> p t d", p=P)).then_inc(s[f"xs{i}"], 16)
                with sp.Fori(0, SLOT_TILES) as j:
                    sp.wait_ge(s["yse"], RING + j + 1)
                    sp.dma_start(ys[bass.ds(j * P, P), :], YSS[:, bass.ds(j * D, D)]).then_inc(s["stored"], 16)
                sp.wait_ge(s["stored"], 16 * SLOT_TILES)

            @block.gpsimd
            def _(pool):
                norm_pool(pool, s, 1)
                pool.memset(RS[0], 0.0).then_inc(s["oh"], 1)
                pool.memset(RS[1], 0.0).then_inc(s["oh"], 1)
                pool.memset(END[0], 0.0).then_inc(s["oh"], 1)
                pool.memset(END[1], 0.0).then_inc(s["oh"], 1)
                pool.tensor_tensor(X[:, :], X[:, :], U[:, :], ALU.add).then_inc(s["xx"], 1)
                pool.wait_ge(s["slot"], 2)
                for t in range(TILES):
                    pool.indirect_dma_start(out=xs, out_offset=bass.IndirectOffsetOnAxis(ap=IDX[:, t:t + 1], axis=0),
                                            in_=XH[:, P * t:P * t + P], in_offset=None).then_inc(s["sent"], 16)
                pool.wait_ge(s["stored"], 16 * SLOT_TILES)
                for t in range(TILES):
                    pool.indirect_dma_start(out=YG[:, P * t:P * t + P], out_offset=None, in_=ys,
                                            in_offset=bass.IndirectOffsetOnAxis(ap=IDX[:, t:t + 1], axis=0)).then_inc(s[f"got{t // CT}"], 16)

            @block.vector
            def _(dve):
                norm_dve(dve, s, 0, U, XH)
                n = [0]

                def then(ins):
                    n[0] += 1
                    ins.then_inc(s["r"], 1)
                    dve.wait_ge(s["r"], n[0])

                r = lambda i: R[:, 16 * i:16 * i + 16]
                dve.wait_ge(s["lg"], TILES)
                then(dve.tensor_tensor(v3(L, 10), v3(bank(4)[:, 0:160], 10), GCB[:, :].unsqueeze(1).to_broadcast([P, TILES, 10]), ALU.add))
                dve.tensor_reduce(r(0), v3(L, 10)[:, :, 0:8], AX.X, ALU.max)
                then(dve.tensor_reduce(r(1), v3(L, 10)[:, :, 8:10], AX.X, ALU.max))
                dve.tensor_tensor(v3(EX, 10)[:, :, 0:8], v3(L, 10)[:, :, 0:8], col(r(0)).to_broadcast([P, TILES, 8]), ALU.subtract)
                then(dve.tensor_tensor(v3(EX, 10)[:, :, 8:10], v3(L, 10)[:, :, 8:10], col(r(1)).to_broadcast([P, TILES, 2]), ALU.subtract))
                then(dve.tensor_tensor(v3(G1, 8), v3(L, 10)[:, :, 0:8], col(r(0)).to_broadcast([P, TILES, 8]), ALU.is_equal))
                then(dve.tensor_tensor(v3(G1, 8), v3(G1, 8), RANK[:, :].unsqueeze(1).to_broadcast([P, TILES, 8]), ALU.mult))
                then(dve.tensor_reduce(r(2), v3(G1, 8), AX.X, ALU.max))
                then(dve.tensor_tensor(v3(G1, 8), v3(G1, 8), col(r(2)).to_broadcast([P, TILES, 8]), ALU.is_equal))
                dve.wait_ge(s["oh"], 4)
                now = [v[:, PAD:PAD + TILES * 8] for v in RS]
                then(dve.tensor_copy(now[0], G1))
                a, step = 0, 1
                while step < TILES:
                    back = RS[a][:, PAD - 8 * step:PAD - 8 * step + TILES * 8]
                    then(dve.tensor_tensor(now[1 - a], now[a], back, ALU.add))
                    a, step = 1 - a, 2 * step
                assert a == 0
                dve.sem_inc(s["rank"], 1)
                dve.wait_ge(s["ex"], 1)
                dve.tensor_reduce(r(3), v3(EX, 10)[:, :, 0:8], AX.X, ALU.add)
                then(dve.tensor_reduce(r(4), v3(EX, 10)[:, :, 8:10], AX.X, ALU.add))
                dve.reciprocal(r(5), r(3))
                then(dve.reciprocal(r(6), r(4)))
                then(dve.tensor_tensor(r(7), r(5), r(6), ALU.mult))
                then(dve.tensor_tensor(r(8), r(7), v3(EX, 10)[:, :, 8], ALU.mult))
                dve.tensor_tensor(v3(SW, NE)[:, :, 0:8], v3(G1, 8), col(r(8)).to_broadcast([P, TILES, 8]), ALU.mult)
                dve.tensor_tensor(v3(SW, NE)[:, :, 8], r(6), v3(EX, 10)[:, :, 9], ALU.mult).then_inc(s["sw"], 1)
                dve.wait_ge(s["rank"], 2)
                rank, count = bank(5)[:, 0:TILES * 8], bank(5)[:, TILES * 8:TILES * 8 + 8]
                then(dve.tensor_tensor(v3(NT, TILES), col(count).to_broadcast([P, 8, TILES]),
                                       FULL[:, 0:TILES].unsqueeze(1).to_broadcast([P, 8, TILES]), ALU.is_gt))
                then(dve.tensor_reduce(END[0][:, 8:16], v3(NT, TILES), AX.X, ALU.add))
                for i, step in enumerate((1, 2, 4)):
                    then(dve.tensor_tensor(END[1 - i % 2][:, 8:16], END[i % 2][:, 8:16], END[i % 2][:, 8 - step:16 - step], ALU.add))
                then(dve.scalar_tensor_tensor(out=v3(TMP, 8), in0=END[1][:, 7:15].unsqueeze(1).to_broadcast([P, TILES, 8]),
                                              scalar=float(P), in1=v3(rank, 8), op0=ALU.mult, op1=ALU.add))
                then(dve.tensor_tensor(TMP, TMP, G1, ALU.mult))
                then(dve.tensor_reduce(r(9), v3(TMP, 8), AX.X, ALU.add))
                dve.tensor_scalar(IDX, r(9), -1.0, None, ALU.add).then_inc(s["slot"], 1)
                then(dve.tensor_tensor(v3(CMP, 8), END[1][:, 8:16].unsqueeze(1).to_broadcast([P, SLOT_TILES, 8]),
                                       col(NUM[:, 0:SLOT_TILES]).to_broadcast([P, SLOT_TILES, 8]), ALU.is_le))
                then(dve.tensor_reduce(EJ, v3(CMP, 8), AX.X, ALU.add))
                dve.tensor_scalar(EI, EJ, float(EXPERTS - 1), None, ALU.min).then_inc(s["slot"], 1)

                dve.wait_ge(s["xx"], 1)
                for c in range(CHUNKS):
                    dve.wait_ge(s["b2"], c + 1)
                    a = slice(CHUNK * c, CHUNK * c + CHUNK)
                    dve.tensor_tensor(X[:, a], X[:, a], bank(6 + c % 2), ALU.add).then_inc(s["acc"], 1)

                def residual(c):
                    dve.wait_ge(s["y"], c + 1)
                    dve.wait_ge(s["acc"], CHUNKS)
                    for i in range(CT):
                        t = CT * c + i
                        a = slice(t * P, (t + 1) * P)
                        ins = dve.scalar_tensor_tensor(out=X[:, a], in0=bank(6 + c % 2)[:, P * i:P * i + P],
                                                       scalar=SW[:, t * NE + EXPERTS:t * NE + NE], in1=X[:, a],
                                                       op0=ALU.mult, op1=ALU.add)
                    ins.then_inc(s["acc"], 1)

                for c in range(EARLY):
                    residual(c)
                dve.sem_inc(s["yse"], RING)

                def expert_of(j):
                    return dve.value_load(EI[0:1, bass.ds(j, 1)], min_val=0, max_val=EXPERTS - 1)

                def copy_first(e, i):
                    dve.tensor_copy(W1C[i], W1S[:, bass.ds(e * FFN, FFN)]).then_inc(s["w1c"], 1)

                def copy_rest(e, i):
                    dve.tensor_copy(B1C[i], B1T[:, bass.ds(e * FC, FC)]).then_inc(s["b1c"], 1)
                    dve.tensor_copy(W2C[i], W2S[:, bass.ds(e * (FC * D), FC * D)]).then_inc(s["w2c"], 1)

                def take_output(j, i):
                    dve.wait_ge(s["ys"], RING + j + 1)
                    dve.tensor_copy(YSS[:, bass.ds(j * D, D)], YB[i][:, 0:D]).then_inc(s["yse"], 1)

                dve.wait_ge(s["w"], 32)
                dve.wait_ge(s["slot"], 2)
                for i in range(RING):
                    e = expert_of(i)
                    copy_first(e, i)
                    copy_rest(e, i)
                with dve.Fori(0, SLOT_TILES // RING - 1) as ring:
                    for i in range(RING):
                        j = ring * RING + i
                        e = expert_of(j + RING)
                        dve.wait_ge(s["hs"], RING + j + 1)
                        copy_first(e, i)
                        dve.wait_ge(s["gs"], RING + j + 1)
                        take_output(j, i)
                        copy_rest(e, i)
                for i in range(RING):
                    take_output(SLOT_TILES - RING + i, i)
                for c in range(EARLY, CHUNKS):
                    residual(c)
                dve.wait_ge(s["acc"], 2 * CHUNKS)
                for t in range(TILES):
                    if t % CT == 0:
                        dve.wait_ge(s[f"got{t // CT}"], 16 * CT)
                    a = slice(P * t, P * t + P)
                    ins = dve.scalar_tensor_tensor(out=X[:, a], in0=YG[:, a], scalar=R[:, 8 * 16 + t:8 * 16 + t + 1], in1=X[:, a],
                                                   op0=ALU.mult, op1=ALU.add)
                ins.then_inc(s["acc"], 1)

            @block.scalar
            def _(act):
                for c in range(CHUNKS):
                    act.wait_ge(s["t"], c + 1)
                    act.activation(XTT[:, CHUNK * c:CHUNK * c + CHUNK], bank(c % 2), ACT.Identity, bias=GB[:, 3:4],
                                   scale=GB[:, 2:3]).then_inc(s["xt"], 1)
                act.wait_ge(s["r"], 3)
                act.activation(EX, EX, ACT.Exp).then_inc(s["ex"], 1)

                def sw_turned(c):
                    act.wait_ge(s["stt"], c + 1)
                    act.copy(SWT[0:NE, CHUNK * c:CHUNK * c + CHUNK], bank(c % 2)[0:NE, :]).then_inc(s["sts"], 1)

                def gelu(c):
                    if c >= 2:
                        act.wait_ge(s["y"], c - 1)
                    for f in range(FC):
                        act.wait_ge(s["h"], FC * c + f + 1)
                        act.activation(HT[c % 2][:, CHUNK * f:CHUNK * f + CHUNK], bank(2 + f % 2), ACT.Gelu,
                                       bias=B1T[:, FC * EXPERTS + f:FC * EXPERTS + f + 1]).then_inc(s["gelu"], 1)

                def gelu_slots(j, i):
                    act.wait_ge(s["hs"], RING + j + 1)
                    act.wait_ge(s["ys"], j + 1)
                    act.wait_ge(s["b1c"], j + 1)
                    for f in range(FC):
                        ins = act.activation(HTS[i][:, P * f:P * f + P], HB[i][:, P * f:P * f + P], ACT.Gelu, bias=B1C[i][:, f:f + 1])
                    ins.then_inc(s["gs"], 1)

                for c in range(EARLY):
                    gelu(c)
                for c in range(CHUNKS):
                    sw_turned(c)
                act.sem_inc(s["gs"], RING)
                for g in range(LOADS):
                    act.wait_ge(s["ts"], g + 1)
                    act.activation(XTS[:, per * P * g:per * P * (g + 1)], bank(g % 2), ACT.Identity, bias=GB[:, 3:4],
                                   scale=GB[:, 2:3]).then_inc(s["xts"], 1)
                with act.Fori(0, SLOT_TILES // RING) as ring:
                    for i in range(RING):
                        gelu_slots(ring * RING + i, i)
                for c in range(EARLY, CHUNKS):
                    gelu(c)

            @block.tensor
            def _(pe):
                pe.sem_inc(s["ys"], RING)
                pe.sem_inc(s["hs"], RING)
                for c in range(CHUNKS):
                    pe.wait_ge(s["xh"], CT * (c + 1))
                    if c >= 2:
                        pe.wait_ge(s["xt"], c - 1)
                    for i in range(CT):
                        ins = pe.transpose(bank(c % 2)[:, P * i:P * i + P], XH[:, (CT * c + i) * P:(CT * c + i + 1) * P], IDF[:, :])
                    ins.then_inc(s["t"], 1)
                for t in range(TILES):
                    if t % CT == 0:
                        pe.wait_ge(s["xt"], t // CT + 1)
                    pe.matmul(bank(4)[:, 10 * t:10 * t + 10], XTT[:, P * t:P * t + P], GC[:, :], start=True, stop=True).then_inc(s["lg"], 1)
                pe.wait_ge(s["w"], 32)

                def first(c):
                    for f in range(FC):
                        k = FC * c + f
                        if k >= 2:
                            pe.wait_ge(s["gelu"], k - 1)
                        pe.matmul(bank(2 + f % 2), W1R[:, P * f:P * f + P], XTT[:, CHUNK * c:CHUNK * (c + 1)], start=True, stop=True).then_inc(s["h"], 1)

                def second(c):
                    pe.wait_ge(s["gelu"], FC * c + FC)
                    pe.wait_ge(s["acc"], CHUNKS + max(c - 1, 0))
                    for i in range(CT):
                        for f in range(FC):
                            ins = pe.matmul(bank(6 + c % 2)[:, P * i:P * i + P], HT[c % 2][:, CHUNK * f + P * i:CHUNK * f + P * i + P],
                                            W2S[:, (FC * EXPERTS + f) * D:(FC * EXPERTS + f + 1) * D], start=f == 0, stop=f == FC - 1)
                    ins.then_inc(s["y"], 1)

                def hidden(j, i):
                    pe.wait_ge(s["w1c"], j + 1)
                    pe.wait_ge(s["gs"], j + 1)
                    for f in range(FC):
                        ins = pe.matmul(HB[i][:, P * f:P * f + P], W1C[i][:, P * f:P * f + P], XTS[:, bass.ds(j * P, P)], start=True, stop=True)
                    ins.then_inc(s["hs"], 1)

                def output(j, i):
                    pe.wait_ge(s["w2c"], j + 1)
                    pe.wait_ge(s["gs"], RING + j + 1)
                    pe.wait_ge(s["yse"], j + 1)
                    for f in range(FC):
                        ins = pe.matmul(YB[i][:, 0:D], HTS[i][:, P * f:P * f + P], W2C[i][:, P * f:P * f + P], start=f == 0, stop=f == FC - 1)
                    ins.then_inc(s["ys"], 1)

                first(0)
                pe.wait_ge(s["rank"], 1)
                done = RS[0]
                pe.matmul(bank(5)[:, 0:TILES * 8], UPTO[:, :], G1, start=True, stop=False)
                pe.matmul(bank(5)[:, 0:TILES * 8], ONES[:, :], done[:, PAD - 8:PAD - 8 + TILES * 8], start=False, stop=True)
                pe.matmul(bank(5)[:, TILES * 8:TILES * 8 + 8], ONES[:, :], done[:, PAD + TILES * 8 - 8:PAD + TILES * 8],
                          start=True, stop=True).then_inc(s["rank"], 1)
                for c in range(1, EARLY):
                    first(c)
                pe.wait_ge(s["sw"], 1)
                for c in range(CHUNKS):
                    if c >= 2:
                        pe.wait_ge(s["sts"], c - 1)
                    for i in range(CT):
                        t = CT * c + i
                        ins = pe.transpose(bank(c % 2)[0:NE, P * i:P * i + P], SW[:, NE * t:NE * t + NE], IDF[:, :])
                    ins.then_inc(s["stt"], 1)
                for c in range(CHUNKS):
                    pe.wait_ge(s["sts"], c + 1)
                    if c >= 2:
                        pe.wait_ge(s["acc"], c - 1)
                    for i in range(CT):
                        t = CT * c + i
                        ins = pe.matmul(bank(6 + c % 2)[:, P * i:P * i + P], SWT[0:NE, P * t:P * t + P], B2S[:, :], start=True, stop=True)
                    ins.then_inc(s["b2"], 1)
                for c in range(EARLY):
                    second(c)
                for g in range(LOADS):
                    pe.wait_ge(s[f"xs{g}"], 16)
                    if g >= 2:
                        pe.wait_ge(s["xts"], g - 1)
                    for i in range(per):
                        ins = pe.transpose(bank(g % 2)[:, P * i:P * i + P], XSS[:, (per * g + i) * P:(per * g + i + 1) * P], IDF[:, :])
                    ins.then_inc(s["ts"], 1)
                pe.wait_ge(s["xts"], LOADS)
                hidden(0, 0)
                hidden(1, 1)
                with pe.Fori(0, SLOT_TILES // RING - 1) as ring:
                    for i in range(RING):
                        hidden(ring * RING + i + 2, (i + 2) % RING)
                        output(ring * RING + i, i)
                hidden(SLOT_TILES - 1, 2)
                for i in range(RING):
                    output(SLOT_TILES - RING + i, i)
                for c in range(EARLY, CHUNKS):
                    first(c)
                    if c > EARLY:
                        second(c - 1)
                second(CHUNKS - 1)

    w1_in = w1

    def linear_attention():
        s = phase_sems("linear", ("kv", "c", "take", "prod", "red", "eps", "rcp", "o"))
        N = H * E1 * DH
        QF = KT[:, :].bitcast(F32).rearrange("p (c q i d) -> p c q i d", q=2, i=CT, d=D)
        V1 = QT[:, :].bitcast(F32)[:, 0:TILES * H * E1]
        KV = [arena(1152 * i, N) for i in range(3)]
        CS = [arena(3456 + 1152 * i, N) for i in range(3)]
        PROD = arena(6912, N)
        RED = arena(8064, H * E1)
        DEN = arena(8208, H)
        RDEN = arena(8224, H)
        C = [PS[:, 2048 * i:2048 * i + N] for i in range(2)]
        parts = [(a, min(a + 512, N)) for a in range(0, N, 512)]

        def hed(a):
            return a.rearrange("p (h e d) -> p h e d", e=E1, d=DH)

        with nc.Block() as block:
            @block.gpsimd
            def _(pool):
                for t in range(TILES):
                    k = QF[:, t // CT, 1, t % CT, :].rearrange("p (h d) -> p h d", d=DH).unsqueeze(2).to_broadcast([P, H, E1, DH])
                    v = V1[:, H * E1 * t:H * E1 * (t + 1)].rearrange("p (h e) -> p h e", e=E1).unsqueeze(3).to_broadcast([P, H, E1, DH])
                    if t >= 3:
                        pool.wait_ge(s["c"], len(parts) * (t - 2))
                    pool.tensor_tensor(hed(KV[t % 3]), k, v, ALU.mult).then_inc(s["kv"], 1)

            @block.tensor
            def _(pe):
                def within(t):
                    pe.wait_ge(s["kv"], t + 1)
                    if t >= 2:
                        pe.wait_ge(s["take"], len(parts) * (t - 1))
                    for a, b in parts:
                        ins = pe.matmul(C[t % 2][:, a:b], UPTO[:, :], KV[t % 3][:, a:b], start=True, stop=t == 0)
                        if t == 0:
                            ins.then_inc(s["c"], 1)

                within(0)
                for t in range(1, TILES):
                    within(t)
                    for n, (a, b) in enumerate(parts):
                        pe.wait_ge(s["take"], len(parts) * (t - 1) + n + 1)
                        pe.matmul(C[t % 2][:, a:b], LAST[:, :], CS[(t - 1) % 3][:, a:b], start=False, stop=True).then_inc(s["c"], 1)

            @block.scalar
            def _(act):
                for t in range(TILES):
                    if t >= 3:
                        act.wait_ge(s["prod"], t - 2)
                    for n, (a, b) in enumerate(parts):
                        act.wait_ge(s["c"], len(parts) * t + n + 1)
                        act.copy(CS[t % 3][:, a:b], C[t % 2][:, a:b]).then_inc(s["take"], 1)

            @block.vector
            def _(dve):
                for t in range(TILES):
                    q = QF[:, t // CT, 0, t % CT, :].rearrange("p (h d) -> p h d", d=DH).unsqueeze(2).to_broadcast([P, H, E1, DH])
                    dve.wait_ge(s["take"], len(parts) * (t + 1))
                    dve.tensor_tensor(hed(PROD), hed(CS[t % 3]), q, ALU.mult).then_inc(s["prod"], 1)
                    dve.wait_ge(s["prod"], t + 1)
                    dve.tensor_reduce(RED, PROD.rearrange("p (n d) -> p n d", d=DH), AX.X, ALU.add).then_inc(s["red"], 1)
                    dve.wait_ge(s["red"], t + 1)
                    red = RED.rearrange("p (h e) -> p h e", e=E1)
                    dve.tensor_scalar(DEN, red[:, :, DH], 1e-6, None, ALU.add).then_inc(s["eps"], 1)
                    dve.wait_ge(s["eps"], t + 1)
                    dve.reciprocal(RDEN, DEN).then_inc(s["rcp"], 1)
                    dve.wait_ge(s["rcp"], t + 1)
                    dve.tensor_tensor(XH[:, P * t:P * t + P].rearrange("p (h d) -> p h d", d=DH), red[:, :, 0:DH],
                                      RDEN.unsqueeze(2).to_broadcast([P, H, DH]), ALU.mult).then_inc(s["o"], 1)

    def ffn(tag):
        prepare("f")
        attention(False)
        project_out(FW[:, 3 * D:4 * D], U, U)
        experts(tag)

    prepare("a")
    attention(True)
    project_out(AW[:, 3 * D:4 * D], X, X)
    ffn("first")
    prepare("l")
    linear_attention()
    project_out(LW[:, 3 * D:4 * D], X, X)
    ffn("second")

    s_out = sem("output_stored")
    with nc.Block() as block:
        @block.sync
        def _(sp):
            sp.dma_start(out.rearrange("b (t p) d -> p (b t) d", p=P), X[:, :].rearrange("p (t d) -> p t d", d=D)).then_inc(s_out, 16)
            sp.wait_ge(s_out, 16)
    top.close()


_INS = ["L0_attn_a_x", "L0_attn_a_Wq", "L0_attn_a_Wk", "L0_attn_a_Wv", "L0_attn_a_Wo", "L0_attn_b_qkv_w",
        "L0_attn_b_qkv_b", "L0_attn_b_out_w", "L0_attn_b_out_b", "L0_ffn_ln1_g", "L0_ffn_ln1_b", "L0_ffn_Wqkv",
        "L0_ffn_bqkv", "L0_ffn_Wo", "L0_ffn_bo", "L0_ffn_ln2_g", "L0_ffn_ln2_b", "L0_ffn_gate_w", "L0_ffn_W1",
        "L0_ffn_b1", "L0_ffn_W2", "L0_ffn_b2", "L0_ffn_rW1", "L0_ffn_rb1", "L0_ffn_rW2", "L0_ffn_rb2",
        "L0_ffn_coef_w", "L0_ffn_coef_b"]


def kernel(**inputs):
    import numpy as _np
    import concourse.bacc as _bacc
    from concourse import mybir as _mybir
    from concourse.bass_utils import run_bass_kernel_spmd as _run

    nc = _bacc.Bacc("TRN2", target_bir_lowering=False, num_devices=1)
    arrays, args = {}, []
    for name in _INS:
        a = _np.ascontiguousarray(inputs[name])
        arrays[f"in_{name}_dram"] = a
        args.append(nc.dram_tensor(f"in_{name}_dram", a.shape, _mybir.dt.from_np(a.dtype), kind="ExternalInput").ap())
    args.append(nc.dram_tensor("out_dram", (1, T, D), F32, kind="ExternalOutput").ap())
    slots = [nc.dram_tensor(n, (SLOT_TILES * P, D), F32).ap() for n in ("slot_in_dram", "slot_out_dram")]
    build(nc, *args, *slots)
    r = _run(nc, [arrays], core_ids=[0])
    return r.results[0]["out_dram"]
```
